# Optimizing a Trainium2 kernel written in Bass

```python
import numpy as np
import jax
import jax.numpy as jnp

def _softmax(x, axis=-1):
    return jax.nn.softmax(x, axis=axis)

def _gelu(x):
    return jax.nn.gelu(x, approximate=True)

def _silu(x):
    return jax.nn.silu(x)

def _sigmoid(x):
    return jax.nn.sigmoid(x)

def _layernorm(x, axis=-1, eps=1e-05):
    m = jnp.mean(x, axis=axis, keepdims=True)
    v = jnp.var(x, axis=axis, keepdims=True)
    return (x - m) / jnp.sqrt(v + eps)

def _scatter_add(tgt, idx, src, axis=0):
    return tgt.at[idx].add(src)

def _segment_sum(src, seg, n):
    return jax.ops.segment_sum(src, seg, n)
kernel_name = 'mk_recurrent_d1_jaxref_r4_0fa64e'

def setup_inputs(seed: int=0):
    np.random.seed(seed)
    _w = jnp.asarray

    def _L0_attn_setup():
        import jax, jax.numpy as jnp
        import numpy as np
        B, N, D, H, C = (4, 2048, 256, 16, 128)
        HD = D // H
        THRESHOLD = 0.99

        def _chunk_scan(qc, kc, vc, lf):
            mask = jnp.tril(jnp.ones((C, C), bool))

            def step(S, inputs):
                qb, kb, vb, lb = inputs
                o_inter = jnp.einsum('bhid,bhde->bhie', qb * jnp.exp(lb)[..., None], S)
                A = jnp.einsum('bhid,bhjd->bhij', qb, kb)
                diff = jnp.where(mask, lb[..., :, None] - lb[..., None, :], -jnp.inf)
                A = A * jnp.exp(diff)
                o_intra = jnp.einsum('bhij,bhjd->bhid', A, vb)
                tot = lb[..., -1]
                kd = kb * jnp.exp(tot[..., None, None] - lb[..., None])
                S_new = jnp.exp(tot)[..., None, None] * S + jnp.einsum('bhjd,bhje->bhde', kd, vb)
                return (S_new, o_inter + o_intra)
            S0 = jnp.zeros((qc.shape[1], H, HD, HD), qc.dtype)
            _, o = jax.lax.scan(step, S0, (qc, kc, vc, lf))
            return o
        key = jax.random.key(seed)
        ks = jax.random.split(key, 6)
        std = 0.02
        return {'x': jax.random.normal(ks[0], (B, N, D), jnp.float32), 'Wq': jax.random.normal(ks[1], (D, D), jnp.float32) * std, 'Wk': jax.random.normal(ks[2], (D, D), jnp.float32) * std, 'Wv': jax.random.normal(ks[3], (D, D), jnp.float32) * std, 'Wo': jax.random.normal(ks[4], (D, D), jnp.float32) * std, 'Wf': jax.random.normal(ks[5], (H, D), jnp.float32) * std, 'delta': jnp.full((H,), float(np.log(THRESHOLD / (1.0 - THRESHOLD))), jnp.float32), 'norm_weight': jnp.ones((D,), jnp.float32)}
    _L0_attn_in = _L0_attn_setup()

    def _L0_ffn_setup():
        import jax, jax.numpy as jnp
        import numpy as np
        CAPACITY = 2
        B, S, D, E, I = (4, 1024, 256, 8, 1024)
        key = jax.random.key(seed)
        k0, k1, k2, k3, k4 = jax.random.split(key, 5)
        x = jax.random.normal(k0, (B, S, D), dtype=jnp.float32)
        gate_w = jax.random.normal(k1, (E, D), dtype=jnp.float32) * 0.006
        w_gate = jax.random.normal(k2, (E, I, D), dtype=jnp.float32) * (1.0 / np.sqrt(D))
        w_up = jax.random.normal(k3, (E, I, D), dtype=jnp.float32) * (1.0 / np.sqrt(D))
        w_down = jax.random.normal(k4, (E, D, I), dtype=jnp.float32) * (1.0 / np.sqrt(I))
        return {'x': x, 'gate_w': gate_w, 'w_gate': w_gate, 'w_up': w_up, 'w_down': w_down}
    _L0_ffn_in = _L0_ffn_setup()
    _d = {'L0_attn_x': _L0_attn_in['x'], 'L0_attn_Wq': _L0_attn_in['Wq'], 'L0_attn_Wk': _L0_attn_in['Wk'], 'L0_attn_Wv': _L0_attn_in['Wv'], 'L0_attn_Wo': _L0_attn_in['Wo'], 'L0_attn_Wf': _L0_attn_in['Wf'], 'L0_attn_delta': _L0_attn_in['delta'], 'L0_attn_norm_weight': _L0_attn_in['norm_weight'], 'L0_ffn_gate_w': _L0_ffn_in['gate_w'], 'L0_ffn_w_gate': _L0_ffn_in['w_gate'], 'L0_ffn_w_up': _L0_ffn_in['w_up'], 'L0_ffn_w_down': _L0_ffn_in['w_down']}
    _x0 = _d['L0_attn_x']
    _d['L0_attn_x'] = jax.random.normal(jax.random.fold_in(jax.random.key(seed), 1), (8, 512, 256), dtype=_x0.dtype)
    del _x0
    return _d

def reference(L0_attn_x, L0_attn_Wq, L0_attn_Wk, L0_attn_Wv, L0_attn_Wo, L0_attn_Wf, L0_attn_delta, L0_attn_norm_weight, L0_ffn_gate_w, L0_ffn_w_gate, L0_ffn_w_up, L0_ffn_w_down):

    def _L0_attn_ref(x, Wq, Wk, Wv, Wo, Wf, delta, norm_weight):
        import jax, jax.numpy as jnp
        import numpy as np
        B, N, D, H, C = (4, 2048, 256, 16, 128)
        HD = D // H
        THRESHOLD = 0.99

        def _chunk_scan(qc, kc, vc, lf):
            mask = jnp.tril(jnp.ones((C, C), bool))

            def step(S, inputs):
                qb, kb, vb, lb = inputs
                o_inter = jnp.einsum('bhid,bhde->bhie', qb * jnp.exp(lb)[..., None], S)
                A = jnp.einsum('bhid,bhjd->bhij', qb, kb)
                diff = jnp.where(mask, lb[..., :, None] - lb[..., None, :], -jnp.inf)
                A = A * jnp.exp(diff)
                o_intra = jnp.einsum('bhij,bhjd->bhid', A, vb)
                tot = lb[..., -1]
                kd = kb * jnp.exp(tot[..., None, None] - lb[..., None])
                S_new = jnp.exp(tot)[..., None, None] * S + jnp.einsum('bhjd,bhje->bhde', kd, vb)
                return (S_new, o_inter + o_intra)
            S0 = jnp.zeros((qc.shape[1], H, HD, HD), qc.dtype)
            _, o = jax.lax.scan(step, S0, (qc, kc, vc, lf))
            return o
        b, n, d = x.shape
        q = jax.nn.silu(x @ Wq.T)
        k = jax.nn.silu(x @ Wk.T)
        v = x @ Wv.T
        log_f = jax.nn.log_sigmoid(x @ Wf.T + delta)
        nc = n // C

        def to_chunks(t):
            return t.reshape(b, nc, C, H, HD).transpose(1, 0, 3, 2, 4)
        qc, kc, vc = map(to_chunks, (q, k, v))
        lf = jnp.cumsum(log_f.reshape(b, nc, C, H).transpose(1, 0, 3, 2), axis=-1)
        o = _chunk_scan(qc, kc, vc, lf)
        o = o.transpose(1, 0, 3, 2, 4).reshape(b, n, d)
        o = o * jax.lax.rsqrt(jnp.mean(o * o, axis=-1, keepdims=True) + 1e-06) * norm_weight
        return o @ Wo.T

    def _L0_ffn_ref(x, gate_w, w_gate, w_up, w_down):
        import jax, jax.numpy as jnp
        import numpy as np
        CAPACITY = 2
        B, S, D = x.shape
        E = gate_w.shape[0]
        k = S // E * CAPACITY
        logits = jnp.einsum('bsd,ed->bse', x, gate_w)
        affinity = jax.nn.softmax(logits, axis=-1)
        affinity = jnp.transpose(affinity, (0, 2, 1))
        gating, idx = jax.lax.top_k(affinity, k)
        bidx = jnp.arange(B)[:, None, None]
        x_in = x[bidx, idx]
        h = jax.nn.silu(jnp.einsum('bekd,eid->beki', x_in, w_gate)) * jnp.einsum('bekd,eid->beki', x_in, w_up)
        x_e = jnp.einsum('beki,edi->bekd', h, w_down)
        out = jnp.zeros_like(x).at[bidx, idx].add(gating[..., None] * x_e)
        return out
    x = L0_attn_x
    xn = _layernorm(x, axis=-1)
    s = _L0_attn_ref(xn, L0_attn_Wq, L0_attn_Wk, L0_attn_Wv, L0_attn_Wo, L0_attn_Wf, L0_attn_delta, L0_attn_norm_weight)
    g = _silu(_L0_ffn_ref(xn, L0_ffn_gate_w, L0_ffn_w_gate, L0_ffn_w_up, L0_ffn_w_down))
    x = x + s * g
    return x

_drawn_inputs = setup_inputs


def setup_inputs(seed=0):
    import zlib

    import numpy as np

    out = dict(_drawn_inputs(seed))
    spreads = {'L0_attn_delta': (4.595119953155518, 0.6), 'L0_attn_norm_weight': (1.0, 0.6)}
    factors = {'L0_attn_Wq': 2.923,
     'L0_attn_Wk': 2.862,
     'L0_attn_Wv': 2.835,
     'L0_attn_Wo': 2.868,
     'L0_attn_Wf': 8.0,
     'L0_ffn_gate_w': 3.307,
     'L0_ffn_w_gate': 3.058,
     'L0_ffn_w_up': 2.866,
     'L0_ffn_w_down': 2.875}
    for name, (base, spread) in spreads.items():
        noise = np.random.default_rng([zlib.crc32(name.encode()), seed]).standard_normal(out[name].shape)
        drawn = base * np.exp(spread * noise) if base else spread * noise
        out[name] = jnp.asarray(drawn.astype(out[name].dtype))
    for name, factor in factors.items():
        out[name] = (out[name] * factor).astype(out[name].dtype)
    return out
```

```python
from contextlib import ExitStack

import numpy as np
import concourse.bass as bass
from concourse import mybir

ALU = mybir.AluOpType
ACT = mybir.ActivationFunctionType
AX = mybir.AxisListType
F32 = mybir.dt.float32
F32R = mybir.dt.float32r
I32 = mybir.dt.int32
U32 = mybir.dt.uint32

P = 128
B, N, D = 8, 512, 256
H, HD = 16, 16
E, I = 8, 1024
CAP = N // E * 2
TPB = N // P
NT = B * TPB
KD = D // P
NL = E + H
HH = H // KD
G4 = 4
NG = H // G4
MI = I // P
WE = 3 * I * D // P
HI, LO = 0, 1
PASSES = [(HI, HI), (HI, LO), (LO, HI)]
LN_EPS, RMS_EPS = 1e-5, 1e-6
TOPK_ROUND = 8
ROUNDS_PER_BATCH = CAP // TOPK_ROUND // B


def f32(ap):
    return ap.bitcast(F32)


def spread(ap, n):
    return ap.unsqueeze(len(ap.shape)).broadcast_to([*ap.shape, n])


def build(nc, x, w_attn, w_logit, delta, norm_w, w_experts, out):
    xn_dram = nc.dram_tensor("xn_dram", [B * N, D], F32, kind="Internal").ap()
    xt_dram = nc.dram_tensor("xt_dram", [B, P, 2 * KD * N], F32, kind="Internal").ap()
    decay_dram = nc.dram_tensor("decay_dram", [2, NT, H * P], F32, kind="Internal").ap()
    neg_decay_dram = nc.dram_tensor("neg_decay_dram", [2, NT, H * P], F32, kind="Internal").ap()
    o_dram = nc.dram_tensor("o_dram", [NT, P, D], F32, kind="Internal").ap()
    s_dram = nc.dram_tensor("s_dram", [B, P, TPB * D], F32, kind="Internal").ap()
    ffn_dram = nc.dram_tensor("ffn_dram", [B * N, D], F32, kind="Internal").ap()
    x_tiles = x.rearrange("(t p) d -> p t d", p=P)
    xn_tiles = xn_dram.rearrange("(t p) d -> p t d", p=P)
    out_tiles = out.rearrange("(t p) d -> p t d", p=P)
    ffn_tiles = ffn_dram.rearrange("(t p) d -> p t d", p=P)

    with ExitStack() as whole:
        def sb_in(stack):
            return lambda name, shape, dt=F32: stack.enter_context(nc.sbuf_tensor(name, shape, dt))

        def ps_in(stack):
            return lambda name, shape: stack.enter_context(nc.psum_tensor(name, shape, F32))

        def sems_in(stack):
            def make(*names):
                made = [stack.enter_context(nc.semaphore(n)) for n in names]
                return made if len(made) > 1 else made[0]
            return make

        def pair_in(stack):
            make = sems_in(stack)
            return lambda name: [make(f"{name}0"), make(f"{name}1")]

        makers = (sb_in, ps_in, sems_in, pair_in)
        sb = sb_in(whole)
        ident = sb("ident", [P, P])
        top_val = sb("top_val", [B * E, CAP])
        top_idx = sb("top_idx", [B * E, CAP])
        with ExitStack() as branch:
            sb = sb_in(branch)
            aff_t = sb("aff_t", [B * E, N])
            exp_lb = sb("exp_lb", [P, NT, H])
            exp_rest = sb("exp_rest", [P, NT, H])
            exp_tot = sb("exp_tot", [P, KD, NT])
            attn_w = sb("attn_w", [P, 2, 4, KD, D], F32R)
            normalise(nc, stage_of(makers), x_tiles, xn_tiles, xt_dram, decay_dram, neg_decay_dram,
                      w_attn, w_logit, delta, norm_w, ident, aff_t, exp_lb, exp_rest, exp_tot, attn_w)
            attention(nc, stage_of(makers), xt_dram, decay_dram, neg_decay_dram, o_dram, ident, aff_t,
                      top_val, top_idx, exp_lb, exp_rest, exp_tot, attn_w)
            out_proj(nc, stage_of(makers), o_dram, s_dram, ident, attn_w)
        experts(nc, stage_of(makers), xn_dram, ffn_dram, w_experts, ident, top_val, top_idx)
        combine(nc, stage_of(makers), x_tiles, s_dram, ffn_tiles, out_tiles)


def stage_of(makers):
    stack = ExitStack()
    return (stack, *(m(stack) for m in makers))


def normalise(nc, stage, x_tiles, xn_tiles, xt_dram, decay_dram, neg_decay_dram, w_attn, w_logit, delta,
              norm_w, ident, aff_t, exp_lb, exp_rest, exp_tot, attn_w):
    stack, sb, ps, sem, pair = stage
    with stack:
        x_all = sb("x_all", [P, NT, D])
        xn = [sb(f"xn{s}", [P, TPB, D]) for s in range(2)]
        xt = [sb(f"xt{s}", [P, 2, KD, N], F32R) for s in range(2)]
        w_raw = sb("w_raw", [P, 4, KD, D])
        wl_raw = sb("wl_raw", [P, KD, NL])
        wl = sb("wl", [P, 2, KD, NL], F32R)
        delta_row = sb("delta_row", [P, H])
        norm_col = sb("norm_col", [P, KD])
        tri = sb("tri", [P, P])
        ones = sb("ones", [P, P])
        head_rows = sb("head_rows", [H, KD, P])
        stats = sb("stats", [P, NT, 6])
        mv = sb("mv", [P, NT, 2])
        var = sb("var", [P, NT])
        lnv = sb("lnv", [P, NT])
        rstd0 = sb("rstd0", [P, NT])
        newton = sb("newton", [P, NT])
        rstd = sb("rstd", [P, NT])
        logits = sb("logits", [P, NT, NL])
        aff = sb("aff", [P, NT, E])
        aff_c = sb("aff_c", [P, TPB, B, E])
        peak = sb("peak", [P, NT])
        z = sb("z", [P, NT, H])
        en = sb("en", [P, NT, H])
        u = sb("u", [P, NT, H])
        lnu = sb("lnu", [P, NT, H])
        c1 = sb("c1", [P, NT, H])
        ru = sb("ru", [P, NT, H])
        lf = sb("lf", [P, NT, H])
        lb = sb("lb", [P, NT, H])
        tot_t = sb("tot_t", [H, NT])
        lbt = sb("lbt", [P, 2, TPB, P], F32R)
        nlbt = sb("nlbt", [P, 2, TPB, P], F32R)
        t_ps = [ps(f"t_ps{s}", [P, KD, N]) for s in range(2)]
        l_ps = [ps(f"l_ps{s}", [P, 512]) for s in range(2)]
        m_ps = [ps(f"m_ps{s}", [P, 512]) for s in range(2)]

        x_in = [sem(f"x_in{b}") for b in range(B)]
        w_in = sem("w_in")
        consts = sem("consts")
        w_hi, w_lo, st = sem("w_hi"), sem("w_lo"), sem("st")
        ln_act = sem("ln_act")
        xn_done, xn_stored = pair("xn_done"), pair("xn_stored")
        t_done, hi_done, lo_done = pair("t_done"), pair("hi_done"), pair("lo_done")
        xt_stored, l_done, l_read = pair("xt_stored"), pair("l_done"), pair("l_read")
        v_step, a_step, p_step, d_out = sem("v_step"), sem("a_step"), sem("p_step"), sem("d_out")

        with nc.Block() as block:
            @block.sync
            def _(sp):
                for b in range(B):
                    sp.dma_start(x_all[:, b * TPB:(b + 1) * TPB, :],
                                 x_tiles[:, b * TPB:(b + 1) * TPB, :]).then_inc(x_in[b], 16)
                with sp.Fori(0, B // 2) as i:
                    for s in range(2):
                        sp.wait_ge(xn_done[s], i + 1)
                        sp.dma_start(xn_tiles[:, bass.ds((i * 2 + s) * TPB, TPB), :],
                                     xn[s][:, :, :]).then_inc(xn_stored[s], 16)
                    for s in range(2):
                        sp.wait_ge(lo_done[s], i + 1)
                        sp.dma_start(xt_dram[bass.ds(i * 2 + s, 1), :, :].rearrange("a p n -> (a p) n"),
                                     f32(xt[s][:, :, :, :]).rearrange("p l k n -> p (l k n)"))\
                          .then_inc(xt_stored[s], 16)
                sp.wait_ge(a_step, 8)
                sp.wait_ge(v_step, 19)
                sp.dma_start(decay_dram.rearrange("l (g t) (h n) -> (t h) l g n", g=TPB, h=H),
                             f32(lbt[:, :, :, :])).then_inc(d_out, 16)
                sp.wait_ge(a_step, 10)
                sp.dma_start(neg_decay_dram.rearrange("l (g t) (h n) -> (t h) l g n", g=TPB, h=H),
                             f32(nlbt[:, :, :, :])).then_inc(d_out, 16)
                sp.wait_ge(d_out, 32)
                for s in range(2):
                    sp.wait_ge(xn_stored[s], 16 * (B // 2))
                    sp.wait_ge(xt_stored[s], 16 * (B // 2))

            @block.gpsimd
            def _(pool):
                pool.memset(ident[:, :], 0.0).then_inc(consts, 1)
                pool.memset(tri[:, :], 1.0).then_inc(consts, 1)
                pool.memset(ones[:, :], 1.0).then_inc(consts, 1)
                pool.memset(head_rows[:, :, :], 1.0).then_inc(consts, 1)
                pool.wait_ge(consts, 4)
                pool.affine_select(out=ident[:, :], in_=ident[:, :], compare_op=ALU.not_equal, fill=1.0,
                                   base=0, pattern=[[-1, P]], channel_multiplier=1).then_inc(consts, 1)
                pool.affine_select(out=tri[:, :], in_=tri[:, :], compare_op=ALU.is_ge, fill=0.0,
                                   base=0, pattern=[[1, P]], channel_multiplier=-1).then_inc(consts, 1)
                pool.affine_select(out=head_rows[:, :, :], in_=head_rows[:, :, :], compare_op=ALU.is_ge,
                                   fill=0.0, base=0, pattern=[[P, KD], [1, P]],
                                   channel_multiplier=-HD).then_inc(consts, 1)
                pool.wait_ge(consts, 7)
                pool.affine_select(out=head_rows[:, :, :], in_=head_rows[:, :, :], compare_op=ALU.is_ge,
                                   fill=0.0, base=HD - 1, pattern=[[-P, KD], [-1, P]],
                                   channel_multiplier=HD).then_inc(consts, 1)

            @block.scalar
            def _(act):
                act.dma_start(w_raw[:, :, :, :], w_attn).then_inc(w_in, 16)
                act.dma_start(wl_raw[:, :, :], w_logit).then_inc(w_in, 16)
                act.dma_start(delta_row[:, :], delta.unsqueeze(0).broadcast_to([P, H])).then_inc(w_in, 16)
                act.dma_start(norm_col[:, :], norm_w).then_inc(w_in, 16)
                act.wait_ge(st, NT + NT + 1)
                act.activation(lnv[:, :], var[:, :], ACT.Ln).then_inc(ln_act, 1)
                act.wait_ge(ln_act, 1)
                act.activation(rstd0[:, :], lnv[:, :], ACT.Exp, scale=-0.5).then_inc(ln_act, 1)
                act.wait_ge(w_in, 64)
                act.activation(wl[:, HI, :, :], wl_raw[:, :, :], ACT.Copy).then_inc(w_hi, 1)
                act.activation(attn_w[:, HI, 0:3, :, :], w_raw[:, 0:3, :, :], ACT.Copy).then_inc(w_hi, 1)
                with act.Fori(0, B // 2) as i:
                    for s in range(2):
                        act.wait_ge(t_done[s], i + 1)
                        act.wait_ge(l_done[s], i)
                        act.wait_ge(xt_stored[s], i * 16)
                        act.activation(xt[s][:, HI, :, :], t_ps[s][:, :, :], ACT.Copy)\
                           .then_inc(hi_done[s], 1)
                act.wait_ge(st, 2 * NT + 7)
                act.activation(attn_w[:, HI, 3, :, :], w_raw[:, 3, :, :], ACT.Copy).then_inc(w_hi, 1)
                act.wait_ge(v_step, 3)
                act.activation(aff[:, :, :], aff[:, :, :], ACT.Exp).then_inc(a_step, 1)
                act.wait_ge(v_step, 4)
                act.activation(en[:, :, :], en[:, :, :], ACT.Exp, scale=-1.0).then_inc(a_step, 1)
                act.wait_ge(v_step, 8)
                act.activation(lnu[:, :, :], u[:, :, :], ACT.Ln).then_inc(a_step, 1)
                act.wait_ge(p_step, 2)
                act.activation(lb[:, :, :], m_ps[1][:, :].rearrange("p (t h) -> p t h", h=H), ACT.Copy)\
                   .then_inc(a_step, 1)
                act.wait_ge(a_step, 4)
                act.activation(exp_lb[:, :, :], lb[:, :, :], ACT.Exp).then_inc(a_step, 1)
                act.wait_ge(v_step, 17)
                act.activation(exp_rest[:, :, :], exp_rest[:, :, :], ACT.Exp).then_inc(a_step, 1)
                act.wait_ge(p_step, 5)
                act.activation(exp_tot[:, :, :], m_ps[1][:, 0:KD * NT].rearrange("p (k t) -> p k t", k=KD),
                               ACT.Exp).then_inc(a_step, 1)
                act.wait_ge(p_step, 6)
                act.activation(lbt[:, HI, :, :], l_ps[0][:, :].rearrange("p (g n) -> p g n", g=TPB),
                               ACT.Copy).then_inc(a_step, 1)
                act.wait_ge(a_step, 8)
                act.activation(nlbt[:, HI, :, :], f32(lbt[:, HI, :, :]), ACT.Copy, scale=-1.0)\
                   .then_inc(a_step, 1)
                act.wait_ge(v_step, 19)
                act.activation(nlbt[:, LO, :, :], f32(lbt[:, LO, :, :]), ACT.Copy, scale=-1.0)\
                   .then_inc(a_step, 1)

            @block.vector
            def _(dve):
                for b in range(B):
                    dve.wait_ge(x_in[b], 16)
                    for t in range(b * TPB, (b + 1) * TPB):
                        dve.bn_stats(stats[:, t, :], x_all[:, t, :]).then_inc(st, 1)
                dve.wait_ge(st, NT)
                for t in range(NT):
                    dve.bn_aggr(mv[:, t, :], stats[:, t, :]).then_inc(st, 1)
                dve.wait_ge(st, 2 * NT)
                dve.tensor_scalar(var[:, :], mv[:, :, 1], LN_EPS, None, ALU.add).then_inc(st, 1)
                dve.wait_ge(ln_act, 2)
                dve.tensor_tensor(newton[:, :], rstd0[:, :], rstd0[:, :], ALU.mult).then_inc(st, 1)
                dve.wait_ge(st, 2 * NT + 2)
                dve.tensor_tensor(newton[:, :], newton[:, :], var[:, :], ALU.mult).then_inc(st, 1)
                dve.wait_ge(st, 2 * NT + 3)
                dve.tensor_scalar(newton[:, :], newton[:, :], -0.5, 1.5, ALU.mult, ALU.add).then_inc(st, 1)
                dve.wait_ge(st, 2 * NT + 4)
                dve.tensor_tensor(rstd[:, :], rstd0[:, :], newton[:, :], ALU.mult).then_inc(st, 1)
                dve.wait_ge(w_in, 64)
                for k in range(KD):
                    dve.tensor_scalar(w_raw[:, 3, k, :], w_raw[:, 3, k, :], norm_col[:, k:k + 1], None,
                                      ALU.mult).then_inc(st, 1)
                dve.wait_ge(w_hi, 2)
                dve.tensor_tensor(wl[:, LO, :, :], wl_raw[:, :, :], f32(wl[:, HI, :, :]), ALU.subtract)\
                   .then_inc(w_lo, 1)
                dve.wait_ge(st, 2 * NT + 7)
                with dve.Fori(0, B // 2) as i:
                    for s in range(2):
                        dve.wait_ge(xn_stored[s], i * 16)
                        dve.wait_ge(t_done[s], i)
                        for t in range(TPB):
                            tile = (i * 2 + s) * TPB + t
                            norm = dve.tensor_scalar(
                                xn[s][:, t, :], x_all[:, bass.ds(tile, 1), :].rearrange("p a d -> p (a d)"),
                                mv[:, bass.ds(tile, 1), 0:1].rearrange("p a d -> p (a d)"),
                                rstd[:, bass.ds(tile, 1)], ALU.subtract, ALU.mult)
                        norm.then_inc(xn_done[s], 1)
                    for s in range(2):
                        dve.wait_ge(hi_done[s], i + 1)
                        dve.tensor_tensor(xt[s][:, LO, :, :], t_ps[s][:, :, :], f32(xt[s][:, HI, :, :]),
                                          ALU.subtract).then_inc(lo_done[s], 1)
                    for s in range(2):
                        dve.wait_ge(l_done[s], i + 1)
                        dve.tensor_copy(logits[:, bass.ds((i * 2 + s) * TPB, TPB), :],
                                        l_ps[s][:, 0:TPB * NL].rearrange("p (t n) -> p t n", n=NL))\
                           .then_inc(l_read[s], 1)
                dve.wait_ge(w_hi, 3)
                dve.tensor_tensor(attn_w[:, LO, :, :, :], w_raw[:, :, :, :], f32(attn_w[:, HI, :, :, :]),
                                  ALU.subtract).then_inc(w_lo, 1)
                for s in range(2):
                    dve.wait_ge(l_read[s], B // 2)
                router, forget = logits[:, :, 0:E], logits[:, :, E:NL]
                dve.tensor_tensor(z[:, :, :], forget, delta_row[:, :].unsqueeze(1).broadcast_to([P, NT, H]),
                                  ALU.add).then_inc(v_step, 1)
                dve.tensor_reduce(peak[:, :], router, AX.X, ALU.max).then_inc(v_step, 1)
                dve.wait_ge(v_step, 2)
                dve.tensor_tensor(aff[:, :, :], router, spread(peak[:, :], E), ALU.subtract)\
                   .then_inc(v_step, 1)
                dve.scalar_tensor_tensor(out=en[:, :, :], in0=z[:, :, :], scalar=-1.0, in1=z[:, :, :],
                                         op0=ALU.mult, op1=ALU.max).then_inc(v_step, 1)
                dve.wait_ge(a_step, 1)
                dve.wait_ge(v_step, 3)
                dve.tensor_reduce(peak[:, :], aff[:, :, :], AX.X, ALU.add).then_inc(v_step, 1)
                dve.wait_ge(v_step, 5)
                dve.reciprocal(peak[:, :], peak[:, :]).then_inc(v_step, 1)
                dve.wait_ge(v_step, 6)
                dve.tensor_tensor(aff_c[:, :, :, :].rearrange("p c b e -> p b c e"),
                                  aff[:, :, :].rearrange("p (b c) e -> p b c e", c=TPB),
                                  spread(peak[:, :].rearrange("p (b c) -> p b c", c=TPB), E), ALU.mult)\
                   .then_inc(v_step, 1)
                dve.wait_ge(a_step, 2)
                dve.tensor_scalar(u[:, :, :], en[:, :, :], 1.0, None, ALU.add).then_inc(v_step, 1)
                dve.wait_ge(v_step, 8)
                dve.tensor_scalar(c1[:, :, :], u[:, :, :], -1.0, None, ALU.add).then_inc(v_step, 1)
                dve.wait_ge(v_step, 9)
                dve.tensor_tensor(c1[:, :, :], en[:, :, :], c1[:, :, :], ALU.subtract).then_inc(v_step, 1)
                dve.reciprocal(ru[:, :, :], u[:, :, :]).then_inc(v_step, 1)
                dve.wait_ge(v_step, 11)
                dve.tensor_tensor(c1[:, :, :], c1[:, :, :], ru[:, :, :], ALU.mult).then_inc(v_step, 1)
                dve.wait_ge(a_step, 3)
                dve.wait_ge(v_step, 12)
                dve.tensor_tensor(lnu[:, :, :], lnu[:, :, :], c1[:, :, :], ALU.add).then_inc(v_step, 1)
                dve.tensor_scalar(z[:, :, :], z[:, :, :], 0.0, None, ALU.min).then_inc(v_step, 1)
                dve.wait_ge(v_step, 14)
                dve.tensor_tensor(lf[:, :, :], z[:, :, :], lnu[:, :, :], ALU.subtract).then_inc(v_step, 1)
                dve.wait_ge(p_step, 1)
                dve.tensor_copy(aff_t[:, :], m_ps[0][0:B * E, :]).then_inc(v_step, 1)
                dve.wait_ge(p_step, 3)
                dve.wait_ge(a_step, 4)
                dve.tensor_tensor(exp_rest[:, :, :], t_ps[0][:, 0, :].rearrange("p (t h) -> p t h", h=H),
                                  lb[:, :, :], ALU.subtract).then_inc(v_step, 1)
                dve.wait_ge(p_step, 4)
                dve.tensor_copy(tot_t[:, :], t_ps[1][0:H, 0, 0:NT]).then_inc(v_step, 1)
                dve.wait_ge(a_step, 8)
                dve.tensor_tensor(lbt[:, LO, :, :], l_ps[0][:, :].rearrange("p (g n) -> p g n", g=TPB),
                                  f32(lbt[:, HI, :, :]), ALU.subtract).then_inc(v_step, 1)

            @block.tensor
            def _(pe):
                pe.wait_ge(consts, 8)
                pe.wait_ge(w_lo, 1)
                with pe.Fori(0, B // 2) as i:
                    for s in range(2):
                        pe.wait_ge(xn_done[s], i + 1)
                        pe.wait_ge(lo_done[s], i)
                        for k in range(KD):
                            for t in range(TPB):
                                mm = pe.transpose(t_ps[s][:, k, t * P:(t + 1) * P],
                                                  xn[s][:, t, k * P:(k + 1) * P], ident[:, :])
                        mm.then_inc(t_done[s], 1)
                    for s in range(2):
                        pe.wait_ge(lo_done[s], i + 1)
                        pe.wait_ge(l_read[s], i)
                        for t in range(TPB):
                            for n, (a, b) in enumerate(PASSES):
                                for k in range(KD):
                                    mm = pe.matmul(l_ps[s][:, t * NL:(t + 1) * NL],
                                                   xt[s][:, a, k, t * P:(t + 1) * P], wl[:, b, k, :],
                                                   start=(n == 0 and k == 0),
                                                   stop=(n == len(PASSES) - 1 and k == KD - 1))
                        mm.then_inc(l_done[s], 1)
                pe.wait_ge(v_step, 7)
                for c in range(TPB):
                    mm = pe.transpose(m_ps[0][0:B * E, c * P:(c + 1) * P],
                                      aff_c[:, c, :, :].rearrange("p b e -> p (b e)"), ident[:, :])
                mm.then_inc(p_step, 1)
                pe.wait_ge(v_step, 15)
                pe.matmul(m_ps[1][:, :], tri[:, :], lf[:, :, :].rearrange("p t h -> p (t h)"),
                          start=True, stop=True).then_inc(p_step, 1)
                pe.matmul(t_ps[0][:, 0, :], ones[:, :], lf[:, :, :].rearrange("p t h -> p (t h)"),
                          start=True, stop=True).then_inc(p_step, 1)
                for t in range(NT):
                    mm = pe.matmul(t_ps[1][0:H, 0, t:t + 1], lf[:, t, :], ones[:, 0:1],
                                   start=True, stop=True)
                mm.then_inc(p_step, 1)
                pe.wait_ge(v_step, 18)
                pe.wait_ge(a_step, 4)
                for k in range(KD):
                    mm = pe.matmul(m_ps[1][:, k * NT:(k + 1) * NT], head_rows[:, k, :], tot_t[:, :],
                                   start=True, stop=True)
                mm.then_inc(p_step, 1)
                for g in range(TPB):
                    mm = pe.transpose(l_ps[0][:, g * P:(g + 1) * P],
                                      lb[:, g * 8:(g + 1) * 8, :].rearrange("p t h -> p (t h)"),
                                      ident[:, :])
                mm.then_inc(p_step, 1)


def attention(nc, stage, xt_dram, decay_dram, neg_decay_dram, o_dram, ident, aff_t, top_val, top_idx,
              exp_lb, exp_rest, exp_tot, attn_w):
    stack, sb, ps, sem, pair = stage
    Q, K = 0, 1
    USES = [("qk", 2 * m + k) for m in range(2) for k in range(KD)] \
        + [("v", c) for c in range(TPB)] + [("kt", c) for c in range(TPB)]
    PER_BANK = len(USES) // 2
    CH = TPB // 2
    GB = NG * TPB // 2
    TOP_STEPS = 4

    with stack:
        xt = sb("xt", [P, 2, KD, N], F32R)
        qk = sb("qk", [P, 2, KD, N])
        qk_r = sb("qk_r", [P, 2, 2, KD, N], F32R)
        v = sb("v", [P, TPB, D])
        kd = sb("kd", [P, TPB, D])
        q_sep = [sb(f"q_sep{s}", [P, 2, KD, HH, P], F32R) for s in range(2)]
        pick = [sb(f"pick{s}", [P, H, P], F32R) for s in range(2)]
        lb_mov = [sb(f"lb_mov{s}", [P, P], F32R) for s in range(2)]
        pick_f = sb("pick_f", [2 * H, H, P])
        row_one = sb("row_one", [P, P])
        absd = [sb(f"absd{s}", [P, G4, P]) for s in range(2)]
        decay = [sb(f"decay{s}", [P, G4, P]) for s in range(2)]
        score = [sb(f"score{s}", [P, G4, P]) for s in range(2)]
        block_mask = sb("block_mask", [P, HH, HD])
        state = sb("state", [P, KD, P])
        upd = sb("upd", [P, KD, P])
        o_sb = [sb(f"o_sb{s}", [P, H, HD]) for s in range(2)]
        m8 = sb("m8", [B * E, ROUNDS_PER_BATCH, TOPK_ROUND])
        i8 = sb("i8", [B * E, ROUNDS_PER_BATCH, TOPK_ROUND], U32)
        p_ps = [ps(f"p_ps{s}", [P, 512]) for s in range(2)]
        d_ps = [ps(f"d_ps{s}", [P, G4, P]) for s in range(2)]
        a_ps = [ps(f"a_ps{s}", [P, G4, P]) for s in range(2)]
        o_ps = ps("o_ps", [P, 2, D])
        u_ps = ps("u_ps", [P, KD, 256])

        setup, ready = sem("setup"), sem("ready")
        turn, v_turn, sp_turn = sem("turn"), sem("v_turn"), sem("a_sp_turn")
        xt_in = sem("xt_in")
        lb_in, q_in = pair("lb_in"), pair("q_in")
        p_done, p_read, lo_done = pair("p_done"), pair("p_read"), sem("lo_done")
        d_done, d_read, e_done, e_masked = pair("d_done"), pair("d_read"), pair("e_done"), pair("e_masked")
        a_done, a_read, av_done = pair("a_done"), pair("a_read"), pair("av_done")
        o_scaled, o_read, o_stored = sem("o_scaled"), sem("o_read"), pair("o_stored")
        u_done, u_read, s_done, topk = sem("u_done"), sem("u_read"), sem("s_done"), sem("topk")

        def pass_at(kind, m):
            n = USES.index((kind, m))
            return n % 2, n // 2

        with nc.Block() as block:
            @block.sync
            def _(sp):
                sp.wait_ge(ready, 1)
                with sp.Fori(0, B) as i:
                    sp.wait_ge(p_done[1], i * PER_BANK)
                    sp.sem_inc(sp_turn, 1)
                    sp.dma_start(f32(xt[:, :, :, :]).rearrange("p l k n -> p (l k n)"),
                                 xt_dram[bass.ds(i, 1), :, :].rearrange("a p n -> (a p) n"))\
                      .then_inc(xt_in, 16)
                    for c in range(TPB):
                        s = c % 2
                        tile = i * TPB + c
                        before = 2 * (c - 1) if c >= 2 else 0
                        sp.wait_ge(d_done[1], i * GB + before)
                        sp.sem_inc(sp_turn, 1)
                        for part in range(2):
                            sp.dma_start(f32(lb_mov[s][part * H:(part + 1) * H, :]),
                                         decay_dram[part, bass.ds(tile, 1), :]
                                         .rearrange("a (h n) -> (a h) n", h=H)).then_inc(lb_in[s], 16)
                        sp.dma_start(f32(pick[s][2 * H:2 * H + 2, :, :]).rearrange("l h n -> l (h n)"),
                                     neg_decay_dram[:, bass.ds(tile, 1), :]
                                     .rearrange("l a n -> l (a n)")).then_inc(lb_in[s], 16)
                        sp.wait_ge(a_done[1], i * GB + before)
                        sp.sem_inc(sp_turn, 1)
                        sp.wait_ge(lo_done, i * 4 + 2)
                        for h in range(HH):
                            rows = slice(h * HD, (h + 1) * HD)
                            sp.dma_start(f32(q_sep[s][rows, :, :, h, :]),
                                         f32(qk_r[rows, Q, :, :, c * P:(c + 1) * P])).then_inc(q_in[s], 16)

            @block.gpsimd
            def _(pool):
                pool.memset(pick_f[:, :, :], 0.0).then_inc(setup, 1)
                pool.memset(row_one[:, :], 1.0).then_inc(setup, 1)
                pool.memset(block_mask[:, :, :], 1.0).then_inc(setup, 1)
                pool.wait_ge(setup, 3)
                pool.affine_select(out=pick_f[:, :, :], in_=pick_f[:, :, :], compare_op=ALU.not_equal,
                                   fill=1.0, base=0, pattern=[[-1, H], [0, P]], channel_multiplier=1)\
                    .then_inc(setup, 1)
                pool.affine_select(out=block_mask[:, :, :], in_=block_mask[:, :, :], compare_op=ALU.is_ge,
                                   fill=0.0, base=0, pattern=[[-HD, HH], [0, HD]], channel_multiplier=1)\
                    .then_inc(setup, 1)
                pool.wait_ge(setup, 5)
                pool.affine_select(out=pick_f[:, :, :], in_=pick_f[:, :, :], compare_op=ALU.not_equal,
                                   fill=1.0, base=-H, pattern=[[-1, H], [0, P]], channel_multiplier=1)\
                    .then_inc(setup, 1)
                pool.affine_select(out=block_mask[:, :, :], in_=block_mask[:, :, :], compare_op=ALU.is_ge,
                                   fill=0.0, base=HD - 1, pattern=[[HD, HH], [0, HD]],
                                   channel_multiplier=-1).then_inc(setup, 1)
                for s in range(2):
                    pool.memset(f32(q_sep[s][:, :, :, :, :]), 0.0).then_inc(setup, 1)
                    pool.memset(f32(pick[s][:, :, :]), 0.0).then_inc(setup, 1)
                    pool.memset(f32(lb_mov[s][:, :]), 0.0).then_inc(setup, 1)
                with pool.Fori(0, B) as i:
                    def store(c):
                        pool.wait_ge(o_read, i * TPB + c + 1)
                        pool.sem_inc(turn, 1)
                        pool.dma_start(o_dram[bass.ds(i * TPB + c, 1), :, :].rearrange("a p d -> (a p) d"),
                                       o_sb[c % 2][:, :, :].rearrange("p h d -> p (h d)"))\
                            .then_inc(o_stored[c % 2], 16)

                    for c in range(TPB):
                        for g in range(NG):
                            p, n = g % 2, 2 * c + g // 2
                            pool.wait_ge(e_done[p], i * GB + n + 1)
                            pool.sem_inc(turn, 1)
                            pool.affine_select(out=decay[p][:, :, :], in_=decay[p][:, :, :],
                                               compare_op=ALU.is_ge, fill=0.0, base=0,
                                               pattern=[[0, G4], [1, P]], channel_multiplier=-1)\
                                .then_inc(e_masked[p], 1)
                        if c >= 1:
                            store(c - 1)
                    store(TPB - 1)
                for s in range(2):
                    pool.wait_ge(o_stored[s], 16 * B * CH)

            @block.scalar
            def _(act):
                with act.Fori(0, B) as i:
                    act.wait_ge(lo_done, i * 4)
                    act.wait_ge(q_in[0], i * CH * HH * 16)
                    act.wait_ge(q_in[1], i * CH * HH * 16)
                    for n, (what, m) in enumerate(USES[:4 + TPB]):
                        b, k = n % 2, n // 2
                        act.wait_ge(p_done[b], i * PER_BANK + k + 1)
                        if what == "qk":
                            act.activation(qk[:, m // 2, m % 2, :], p_ps[b][:, :], ACT.Silu)
                            act.activation(qk_r[:, m // 2, HI, m % 2, :], p_ps[b][:, :], ACT.Silu)\
                               .then_inc(p_read[b], 1)
                        else:
                            act.activation(v[:, m, :], p_ps[b][:, 0:D], ACT.Copy).then_inc(p_read[b], 1)
                    for c in range(TPB):
                        for g in range(NG):
                            p, n = g % 2, 2 * c + g // 2
                            act.wait_ge(d_done[p], i * GB + n + 1)
                            act.activation(absd[p][:, :, :], d_ps[p][:, :, :], ACT.Abs)\
                               .then_inc(d_read[p], 1)
                            act.wait_ge(d_read[p], i * GB + n + 1)
                            act.wait_ge(a_read[p], i * GB + n)
                            act.activation(decay[p][:, :, :], absd[p][:, :, :], ACT.Exp, scale=-1.0)\
                               .then_inc(e_done[p], 1)

            @block.vector
            def _(dve):
                dve.wait_ge(setup, 13)
                for s in range(2):
                    dve.tensor_copy(pick[s][0:2 * H, :, :], pick_f[:, :, :]).then_inc(setup, 1)
                    dve.tensor_copy(lb_mov[s][2 * H:2 * H + 2, :], row_one[2 * H:2 * H + 2, :])\
                       .then_inc(setup, 1)
                dve.wait_ge(setup, 17)
                dve.sem_inc(ready, 1)
                with dve.Fori(0, B) as i:
                    for r in range(ROUNDS_PER_BATCH):
                        at = (i * ROUNDS_PER_BATCH + r) * TOPK_ROUND
                        before = (i * ROUNDS_PER_BATCH + r) * TOP_STEPS
                        dve.wait_ge(topk, before)
                        dve.sem_inc(v_turn, 1)
                        dve.max(m8[:, r, :], aff_t[:, :]).then_inc(topk, 1)
                        dve.wait_ge(topk, before + 1)
                        dve.sem_inc(v_turn, 1)
                        dve.max_index(i8[:, r, :], m8[:, r, :], aff_t[:, :]).then_inc(topk, 1)
                        dve.wait_ge(topk, before + 2)
                        dve.sem_inc(v_turn, 1)
                        dve.match_replace(aff_t[:, :], m8[:, r, :], aff_t[:, :], -1.0).then_inc(topk, 1)
                        dve.tensor_copy(top_val[:, bass.ds(at, TOPK_ROUND)], m8[:, r, :])
                        dve.tensor_copy(top_idx[:, bass.ds(at, TOPK_ROUND)], i8[:, r, :]).then_inc(topk, 1)
                    dve.memset(state[:, :, :], 0.0).then_inc(s_done, 1)
                    for m in range(4):
                        b, k = pass_at("qk", m)
                        dve.wait_ge(p_read[b], i * PER_BANK + k + 1)
                        dve.tensor_tensor(qk_r[:, m // 2, LO, m % 2, :], qk[:, m // 2, m % 2, :],
                                          f32(qk_r[:, m // 2, HI, m % 2, :]), ALU.subtract)\
                           .then_inc(lo_done, 1)
                    for c in range(TPB):
                        b, k = pass_at("kt", c)
                        dve.wait_ge(p_done[b], i * PER_BANK + k + 1)
                        dve.tensor_tensor(kd[:, c, :].rearrange("p (h d) -> p h d", h=H),
                                          p_ps[b][:, 0:D].rearrange("p (h d) -> p h d", h=H),
                                          spread(exp_rest[:, bass.ds(i * TPB + c, 1), :]
                                                 .rearrange("p a h -> p (a h)"), HD),
                                          ALU.mult).then_inc(p_read[b], 1)
                    for c in range(TPB):
                        s = c % 2
                        tile = i * TPB + c
                        for g in range(NG):
                            p, n = g % 2, 2 * c + g // 2
                            dve.wait_ge(a_done[p], i * GB + n + 1)
                            dve.wait_ge(e_masked[p], i * GB + n + 1)
                            dve.wait_ge(av_done[p], i * GB + n)
                            dve.tensor_tensor(score[p][:, :, :], a_ps[p][:, :, :], decay[p][:, :, :],
                                              ALU.mult).then_inc(a_read[p], 1)
                        dve.wait_ge(av_done[1], i * GB + 2 * c + 2)
                        dve.wait_ge(o_stored[s], (i * CH + c // 2) * 16)
                        dve.tensor_tensor(o_sb[s][:, :, :],
                                          o_ps[:, 1, :].rearrange("p (h d) -> p h d", h=H),
                                          spread(exp_lb[:, bass.ds(tile, 1), :]
                                                 .rearrange("p a h -> p (a h)"), HD),
                                          ALU.mult).then_inc(o_scaled, 1)
                        dve.wait_ge(o_scaled, i * TPB + c + 1)
                        dve.tensor_tensor(o_sb[s][:, :, :], o_sb[s][:, :, :],
                                          o_ps[:, 0, :].rearrange("p (h d) -> p h d", h=H), ALU.add)\
                           .then_inc(o_read, 1)
                        if c == TPB - 1:
                            continue
                        n = i * (TPB - 1) + c
                        dve.wait_ge(u_done, n + 1)
                        dve.wait_ge(s_done, i * TPB + c + 1)
                        dve.tensor_tensor(upd[:, :, :], u_ps[:, :, 0:P],
                                          block_mask[:, :, :].rearrange("p h d -> p (h d)").unsqueeze(1)
                                          .broadcast_to([P, KD, P]), ALU.mult).then_inc(u_read, 1)
                        dve.wait_ge(u_read, n + 1)
                        for k in range(KD):
                            ins = dve.scalar_tensor_tensor(
                                out=state[:, k, :], in0=state[:, k, :],
                                scalar=exp_tot[:, k, bass.ds(tile, 1)], in1=upd[:, k, :],
                                op0=ALU.mult, op1=ALU.add)
                        ins.then_inc(s_done, 1)

            @block.tensor
            def _(pe):
                pe.wait_ge(ready, 1)
                with pe.Fori(0, B) as i:
                    pe.wait_ge(xt_in, i * 16 + 16)
                    for n, (what, m) in enumerate(USES):
                        b, k = n % 2, n // 2
                        pe.wait_ge(p_read[b], i * PER_BANK + k)
                        if what == "qk":
                            for j, (wp, xp) in enumerate(PASSES):
                                for kk in range(KD):
                                    mm = pe.matmul(p_ps[b][:, :],
                                                   attn_w[:, wp, m // 2, kk, (m % 2) * P:(m % 2 + 1) * P],
                                                   xt[:, xp, kk, :], start=(j == 0 and kk == 0),
                                                   stop=(j == len(PASSES) - 1 and kk == KD - 1))
                        elif what == "v":
                            for j, (xp, wp) in enumerate(PASSES):
                                for kk in range(KD):
                                    mm = pe.matmul(p_ps[b][:, 0:D], xt[:, xp, kk, m * P:(m + 1) * P],
                                                   attn_w[:, wp, 2, kk, :], start=(j == 0 and kk == 0),
                                                   stop=(j == len(PASSES) - 1 and kk == KD - 1))
                        else:
                            for kk in range(KD):
                                mm = pe.transpose(p_ps[b][:, kk * P:(kk + 1) * P],
                                                  qk[:, K, kk, m * P:(m + 1) * P], ident[:, :])
                        mm.then_inc(p_done[b], 1)

                    def decays(c, g):
                        s, p, n = c % 2, g % 2, 2 * c + g // 2
                        if g == 0:
                            pe.wait_ge(lb_in[s], (i * CH + c // 2 + 1) * 48)
                        pe.wait_ge(d_read[p], i * GB + n)
                        for j in range(G4):
                            mm = pe.matmul(d_ps[p][:, j, :], pick[s][:, g * G4 + j, :], lb_mov[s][:, :],
                                           start=True, stop=True)
                        mm.then_inc(d_done[p], 1)

                    def scores(c, g):
                        s, p, n = c % 2, g % 2, 2 * c + g // 2
                        kk, first = g * G4 // HH, g * G4 % HH
                        if g == 0:
                            pe.wait_ge(q_in[s], (i * CH + c // 2 + 1) * HH * 16)
                            pe.wait_ge(lo_done, i * 4 + 4)
                        pe.wait_ge(a_read[p], i * GB + n)
                        for j, (kp, qp) in enumerate(PASSES):
                            mm = pe.matmul(a_ps[p][:, :, :].rearrange("p h n -> p (h n)"),
                                           qk_r[:, K, kp, kk, c * P:(c + 1) * P],
                                           q_sep[s][:, qp, kk, first:first + G4, :]
                                           .rearrange("p h n -> p (h n)"),
                                           start=(j == 0), stop=(j == len(PASSES) - 1))
                        mm.then_inc(a_done[p], 1)

                    def values(c, g):
                        p, n = g % 2, 2 * c + g // 2
                        if g == 0:
                            b, k = pass_at("v", c)
                            pe.wait_ge(o_read, i * TPB + c)
                            pe.wait_ge(p_read[b], i * PER_BANK + k + 1)
                        pe.wait_ge(a_read[p], i * GB + n + 1)
                        for j in range(G4):
                            h = g * G4 + j
                            mm = pe.matmul(o_ps[:, 0, h * HD:(h + 1) * HD], score[p][:, j, :],
                                           v[:, c, h * HD:(h + 1) * HD], start=True, stop=True)
                        mm.then_inc(av_done[p], 1)

                    for c in range(TPB):
                        decays(c, 0)
                        scores(c, 0)
                        for g in range(1, NG):
                            decays(c, g)
                            scores(c, g)
                            values(c, g - 1)
                        if c < TPB - 1:
                            b, k = pass_at("kt", c)
                            pe.wait_ge(u_read, i * (TPB - 1) + c)
                            pe.wait_ge(p_read[b], i * PER_BANK + k + 1)
                            for kk in range(KD):
                                mm = pe.matmul(u_ps[:, kk, 0:P], kd[:, c, kk * P:(kk + 1) * P],
                                               v[:, c, kk * P:(kk + 1) * P], start=True, stop=True)
                            mm.then_inc(u_done, 1)
                        pe.wait_ge(s_done, i * TPB + c + 1)
                        for kk in range(KD):
                            pe.matmul(o_ps[:, 1, kk * P:(kk + 1) * P], qk[:, Q, kk, c * P:(c + 1) * P],
                                      state[:, kk, :], start=True, stop=True)
                        values(c, NG - 1)


def out_proj(nc, stage, o_dram, s_dram, ident, attn_w):
    stack, sb, ps, sem, pair = stage
    with stack:
        o_in_sb = [sb(f"o_in_sb{s}", [P, TPB, D]) for s in range(2)]
        square = [sb(f"square{s}", [P, TPB, D]) for s in range(2)]
        sumsq = [sb(f"sumsq{s}", [P, TPB]) for s in range(2)]
        ms = [sb(f"ms{s}", [P, TPB]) for s in range(2)]
        ln_ms = [sb(f"ln_ms{s}", [P, TPB]) for s in range(2)]
        r0 = [sb(f"r0{s}", [P, TPB]) for s in range(2)]
        r1 = [sb(f"r1{s}", [P, TPB]) for s in range(2)]
        ot = [sb(f"ot{s}", [P, 2, KD, N], F32R) for s in range(2)]
        s_sb = [sb(f"s_sb{s}", [P, TPB, D]) for s in range(2)]
        t_ps = [ps(f"ot_ps{s}", [P, KD, N]) for s in range(2)]
        y_ps = [ps(f"s_ps{s}", [P, TPB, D]) for s in range(2)]
        o_in, sq_done, s_stored = pair("po_in"), pair("sq_done"), pair("s_stored")
        t_done, hi_done, lo_done, y_done, y_read = (pair("ot_done"), pair("ohi_done"), pair("olo_done"),
                                                    pair("s_made"), pair("s_read"))
        ms_step, r_step = pair("ms_step"), pair("r_step")

        with nc.Block() as block:
            @block.sync
            def _(sp):
                with sp.Fori(0, B // 2) as i:
                    for s in range(2):
                        sp.wait_ge(t_done[s], i)
                        sp.wait_ge(sq_done[s], i)
                        sp.dma_start(o_in_sb[s][:, :, :],
                                     o_dram[bass.ds((i * 2 + s) * TPB, TPB), :, :]
                                     .rearrange("t p d -> p t d")).then_inc(o_in[s], 16)
                    for s in range(2):
                        sp.wait_ge(y_read[s], i + 1)
                        sp.dma_start(s_dram[bass.ds(i * 2 + s, 1), :, :].rearrange("a p n -> (a p) n"),
                                     s_sb[s][:, :, :].rearrange("p t d -> p (t d)")).then_inc(s_stored[s], 16)
                for s in range(2):
                    sp.wait_ge(s_stored[s], 16 * (B // 2))

            @block.scalar
            def _(act):
                with act.Fori(0, B // 2) as i:
                    for s in range(2):
                        act.wait_ge(t_done[s], i + 1)
                        act.wait_ge(y_done[s], i)
                        act.activation(ot[s][:, HI, :, :], t_ps[s][:, :, :], ACT.Copy)\
                           .then_inc(hi_done[s], 1)
                        act.wait_ge(ms_step[s], i)
                        for t in range(TPB):
                            ins = act.activation(square[s][:, t, :], o_in_sb[s][:, t, :], ACT.Square,
                                                 accum_out=sumsq[s][:, t:t + 1])
                        ins.then_inc(sq_done[s], 1)
                    for s in range(2):
                        act.wait_ge(ms_step[s], i + 1)
                        act.activation(ln_ms[s][:, :], ms[s][:, :], ACT.Ln).then_inc(r_step[s], 1)
                        act.wait_ge(r_step[s], i * 5 + 1)
                        act.activation(r0[s][:, :], ln_ms[s][:, :], ACT.Exp, scale=-0.5)\
                           .then_inc(r_step[s], 1)

            @block.vector
            def _(dve):
                with dve.Fori(0, B // 2) as i:
                    for s in range(2):
                        dve.wait_ge(hi_done[s], i + 1)
                        dve.tensor_tensor(ot[s][:, LO, :, :], t_ps[s][:, :, :], f32(ot[s][:, HI, :, :]),
                                          ALU.subtract).then_inc(lo_done[s], 1)
                        dve.wait_ge(sq_done[s], i + 1)
                        dve.wait_ge(y_read[s], i)
                        dve.tensor_scalar(ms[s][:, :], sumsq[s][:, :], 1.0 / D, RMS_EPS, ALU.mult, ALU.add)\
                           .then_inc(ms_step[s], 1)
                    for s in range(2):
                        dve.wait_ge(r_step[s], i * 5 + 2)
                        dve.tensor_tensor(r1[s][:, :], r0[s][:, :], r0[s][:, :], ALU.mult)\
                           .then_inc(r_step[s], 1)
                        dve.wait_ge(r_step[s], i * 5 + 3)
                        dve.tensor_tensor(r1[s][:, :], r1[s][:, :], ms[s][:, :], ALU.mult)\
                           .then_inc(r_step[s], 1)
                        dve.wait_ge(r_step[s], i * 5 + 4)
                        dve.tensor_scalar(r1[s][:, :], r1[s][:, :], -0.5, 1.5, ALU.mult, ALU.add)\
                           .then_inc(r_step[s], 1)
                        dve.wait_ge(r_step[s], i * 5 + 5)
                        dve.wait_ge(y_done[s], i + 1)
                        dve.wait_ge(s_stored[s], i * 16)
                        for t in range(TPB):
                            ins = dve.tensor_scalar(s_sb[s][:, t, :], y_ps[s][:, t, :], r0[s][:, t:t + 1],
                                                    r1[s][:, t:t + 1], ALU.mult, ALU.mult)
                        ins.then_inc(y_read[s], 1)

            @block.tensor
            def _(pe):
                with pe.Fori(0, B // 2) as i:
                    for s in range(2):
                        pe.wait_ge(o_in[s], i * 16 + 16)
                        pe.wait_ge(lo_done[s], i)
                        for k in range(KD):
                            for t in range(TPB):
                                mm = pe.transpose(t_ps[s][:, k, t * P:(t + 1) * P],
                                                  o_in_sb[s][:, t, k * P:(k + 1) * P], ident[:, :])
                        mm.then_inc(t_done[s], 1)
                    for s in range(2):
                        pe.wait_ge(lo_done[s], i + 1)
                        pe.wait_ge(y_read[s], i)
                        for t in range(TPB):
                            for j, (a, b) in enumerate(PASSES):
                                for k in range(KD):
                                    mm = pe.matmul(y_ps[s][:, t, :], ot[s][:, a, k, t * P:(t + 1) * P],
                                                   attn_w[:, b, 3, k, :], start=(j == 0 and k == 0),
                                                   stop=(j == len(PASSES) - 1 and k == KD - 1))
                        mm.then_inc(y_done[s], 1)


def experts(nc, stage, xn_dram, ffn_dram, w_experts, ident, top_val, top_idx):
    stack, sb, ps, sem, pair = stage
    SEC = WE // 3
    GATE, UP, DOWN = range(3)
    PIECES = 12
    PW = WE // PIECES
    HALVES = B // TPB
    STEPS = HALVES * MI
    SB2 = STEPS // 2
    FILLS = HALVES * KD
    with stack:
        w_raw = sb("we_raw", [P, WE])
        w_r = [sb(f"we_r{s}", [P, 2, WE], F32R) for s in range(2)]
        xg = sb("xg", [P, B, D])
        xgt = [sb(f"xgt{s}", [P, 2, KD, B * CAP], F32R) for s in range(2)]
        sg = [sb(f"sg{s}", [P, 512]) for s in range(2)]
        hid = [sb(f"hid{s}", [P, 512]) for s in range(2)]
        hid_r = [sb(f"hid_r{s}", [P, 2, 512], F32R) for s in range(2)]
        y_sb = [sb(f"y_sb{s}", [P, TPB, D]) for s in range(HALVES)]
        gate_all = sb("gate_all", [P, E, B])
        idx_all = sb("idx_all", [P, E, B], I32)
        batch_base = sb("batch_base", [P, B, E])
        gate_e = [sb(f"gate_e{s}", [P, B]) for s in range(2)]
        idx_e = [sb(f"idx_e{s}", [P, B], I32) for s in range(2)]
        zeros = sb("zeros", [P, 2 * D])
        g_ps = [ps(f"g_ps{s}", [P, 512]) for s in range(2)]
        up_ps = [ps(f"up_ps{s}", [P, 512]) for s in range(2)]
        y_ps = ps("ye_ps", [P, TPB, D])
        x_ps = [ps(f"x_ps{s}", [P, 512]) for s in range(2)]

        zero_set, zeroed, base_set = sem("zero_set"), sem("zeroed"), sem("base_set")
        top_t, top_read = sem("top_t"), sem("top_read")
        w_in, w_hi, w_lo = sem("we_in"), sem("we_hi"), sem("we_lo")
        staged, gathered, x_read = sem("staged"), sem("gathered"), pair("x_read")
        x_done, x_hi = pair("x_done"), pair("x_hi")
        gu_done, sg_done, h_done = pair("gu_done"), pair("sg_done"), pair("h_done")
        hh_done, hl_done, dn_done = pair("hh_done"), pair("hl_done"), pair("dn_done")
        y_read, scattered = sem("ye_read"), pair("scattered")
        turn, sp_turn = sem("e_turn"), sem("sp_turn")

        def each_expert(eng, unit):
            with eng.Fori(0, E // 2 - 1) as i:
                for s in range(2):
                    unit(i * 2 + s, i, s, True)
            unit(E - 2, E // 2 - 1, 0, True)
            unit(E - 1, E // 2 - 1, 1, False)

        with nc.Block() as block:
            @block.sync
            def _(sp):
                def load(e):
                    sp.wait_ge(w_lo, e * PIECES)
                    sp.sem_inc(sp_turn, 1)
                    sp.dma_start(w_raw[:, :], w_experts[e, :, :] if isinstance(e, int) else
                                 w_experts[bass.ds(e, 1), :, :].rearrange("a p n -> (a p) n"))\
                      .then_inc(w_in, 16)

                load(0)
                sp.wait_ge(zero_set, 1)
                rows = ffn_dram.rearrange("(p n) d -> p (n d)", p=P)
                for n in range(B * N * D // P // (2 * D)):
                    sp.dma_start(rows[:, n * 2 * D:(n + 1) * 2 * D], zeros[:, :]).then_inc(zeroed, 16)

                def unit(e, i, s, more):
                    if more:
                        load(e + 1)
                each_expert(sp, unit)

            @block.gpsimd
            def _(pool):
                pool.memset(zeros[:, :], 0.0).then_inc(zero_set, 1)
                pool.iota(batch_base[:, :, :], pattern=[[N, B], [0, E]], base=0, channel_multiplier=0,
                          allow_small_or_imprecise_dtypes=True).then_inc(base_set, 1)

                def low(e, s, n):
                    at = slice(n * PW, (n + 1) * PW)
                    pool.wait_ge(w_hi, e * PIECES + n + 1)
                    pool.tensor_tensor(w_r[s][:, LO, at], w_raw[:, at], f32(w_r[s][:, HI, at]),
                                       ALU.subtract).then_inc(w_lo, 1)

                def gather(e, i, s):
                    pool.wait_ge(scattered[s], i * 128)
                    pool.sem_inc(turn, 1)
                    pool.tensor_copy(idx_e[s][:, :], pick_expert(idx_all, e)).then_inc(staged, 1)
                    pool.tensor_copy(gate_e[s][:, :], pick_expert(gate_all, e)).then_inc(staged, 1)
                    pool.wait_ge(staged, e * 2 + 2)
                    pool.sem_inc(turn, 1)
                    for b in range(2):
                        pool.wait_ge(x_read[b], e * (FILLS // 2))
                        pool.sem_inc(turn, 1)
                    for b in range(B):
                        pool.indirect_dma_start(
                            out=xg[:, b, :], out_offset=None, in_=xn_dram[:, :],
                            in_offset=bass.IndirectOffsetOnAxis(ap=idx_e[s][:, b:b + 1], axis=0))\
                            .then_inc(gathered, 16)

                def scatter(e, i, s, half):
                    pool.wait_ge(y_read, e * HALVES + half + 1)
                    pool.sem_inc(turn, 1)
                    if half == 0:
                        pool.wait_ge(scattered[1 - s], (i + s) * 128)
                        pool.sem_inc(turn, 1)
                    for t in range(TPB):
                        b = half * TPB + t
                        pool.indirect_dma_start(
                            out=ffn_dram[:, :],
                            out_offset=bass.IndirectOffsetOnAxis(ap=idx_e[s][:, b:b + 1], axis=0),
                            in_=y_sb[half][:, t, :], in_offset=None, compute_op=ALU.add)\
                            .then_inc(scattered[s], 16)

                pool.wait_ge(top_read, 2)
                gather(0, 0, 0)
                for n in range(PIECES):
                    low(0, 0, n)
                pool.wait_ge(zeroed, 16 * (B * N * D // P // (2 * D)))

                def unit(e, i, s, more):
                    if more:
                        gather(e + 1, i + s, 1 - s)
                        for n in range(PIECES // 2):
                            low(e + 1, 1 - s, n)
                    scatter(e, i, s, 0)
                    if more:
                        for n in range(PIECES // 2, PIECES):
                            low(e + 1, 1 - s, n)
                    scatter(e, i, s, 1)
                each_expert(pool, unit)
                for s in range(2):
                    pool.wait_ge(scattered[s], E // 2 * 128)

            @block.scalar
            def _(act):
                def high(e, i, s, n):
                    at = slice(n * PW, (n + 1) * PW)
                    if n == 0:
                        act.wait_ge(w_in, e * 16 + 16)
                        act.wait_ge(dn_done[1], (e - 1) * SB2 if not isinstance(e, int) or e > 0 else 0)
                    act.activation(w_r[s][:, HI, at], w_raw[:, at], ACT.Copy).then_inc(w_hi, 1)

                def x_high(e, s, f):
                    b = f % 2
                    act.wait_ge(x_done[b], e * (FILLS // 2) + f // 2 + 1)
                    act.activation(xgt[s][:, HI, f % KD, (f // KD) * 512:(f // KD + 1) * 512], x_ps[b][:, :],
                                   ACT.Copy).then_inc(x_hi[b], 1)

                for n in range(PIECES):
                    high(0, 0, 0, n)
                for f in range(FILLS):
                    x_high(0, 0, f)

                def unit(e, i, s, more):
                    for t in range(STEPS):
                        p, n = t % 2, t // 2
                        act.wait_ge(gu_done[p], e * SB2 + n + 1)
                        act.activation(sg[p][:, :], g_ps[p][:, :], ACT.Silu).then_inc(sg_done[p], 1)
                        if more and t < PIECES:
                            high(e + 1, i + s, 1 - s, t)
                        if more and t >= STEPS - FILLS:
                            x_high(e + 1, 1 - s, t - (STEPS - FILLS))
                        act.wait_ge(h_done[p], e * SB2 + n + 1)
                        act.wait_ge(dn_done[p], e * SB2 + n)
                        act.activation(hid_r[p][:, HI, :], hid[p][:, :], ACT.Copy).then_inc(hh_done[p], 1)
                each_expert(act, unit)

            @block.vector
            def _(dve):
                dve.wait_ge(top_t, 1)
                dve.wait_ge(base_set, 1)
                dve.tensor_copy(gate_all[:, :, :].rearrange("p e b -> p b e"),
                                x_ps[0][:, 0:B * E].rearrange("p (b e) -> p b e", b=B)).then_inc(top_read, 1)
                dve.tensor_tensor(idx_all[:, :, :].rearrange("p e b -> p b e"),
                                  x_ps[0][:, B * E:2 * B * E].rearrange("p (b e) -> p b e", b=B),
                                  batch_base[:, :, :], ALU.add).then_inc(top_read, 1)

                def x_low(e, s, f):
                    b = f % 2
                    dst = slice((f // KD) * 512, (f // KD + 1) * 512)
                    dve.wait_ge(x_hi[b], e * (FILLS // 2) + f // 2 + 1)
                    dve.tensor_tensor(xgt[s][:, LO, f % KD, dst], x_ps[b][:, :],
                                      f32(xgt[s][:, HI, f % KD, dst]), ALU.subtract).then_inc(x_read[b], 1)

                for f in range(FILLS):
                    x_low(0, 0, f)

                def gated(e, i, s, half):
                    dve.wait_ge(dn_done[1], e * SB2 + (half + 1) * MI // 2)
                    dve.wait_ge(scattered[1 - s], (i + s) * 128)
                    dve.wait_ge(staged, e * 2 + 2)
                    for t in range(TPB):
                        b = half * TPB + t
                        ins = dve.tensor_scalar(y_sb[half][:, t, :], y_ps[:, t, :], gate_e[s][:, b:b + 1],
                                                None, ALU.mult)
                    ins.then_inc(y_read, 1)

                def unit(e, i, s, more):
                    for t in range(STEPS):
                        p, n = t % 2, t // 2
                        dve.wait_ge(sg_done[p], e * SB2 + n + 1)
                        dve.tensor_tensor(hid[p][:, :], sg[p][:, :], up_ps[p][:, :], ALU.mult)\
                           .then_inc(h_done[p], 1)
                        if more and t >= STEPS - FILLS:
                            x_low(e + 1, 1 - s, t - (STEPS - FILLS))
                        dve.wait_ge(hh_done[p], e * SB2 + n + 1)
                        dve.tensor_tensor(hid_r[p][:, LO, :], hid[p][:, :], f32(hid_r[p][:, HI, :]),
                                          ALU.subtract).then_inc(hl_done[p], 1)
                        if t == MI:
                            gated(e, i, s, 0)
                    gated(e, i, s, 1)
                each_expert(dve, unit)

            @block.tensor
            def _(pe):
                pe.transpose(x_ps[0][:, 0:B * E], top_val[:, :], ident[0:B * E, 0:B * E])
                pe.transpose(x_ps[0][:, B * E:2 * B * E], top_idx[:, :], ident[0:B * E, 0:B * E])\
                  .then_inc(top_t, 1)
                pe.wait_ge(top_read, 2)

                def turn_tokens(e, f):
                    b = f % 2
                    if f == 0:
                        pe.wait_ge(gathered, e * 128 + 128)
                    pe.wait_ge(x_read[b], e * (FILLS // 2) + f // 2)
                    for t in range(TPB):
                        mm = pe.transpose(x_ps[b][:, t * P:(t + 1) * P],
                                          xg[:, (f // KD) * TPB + t, (f % KD) * P:(f % KD + 1) * P],
                                          ident[:, :])
                    mm.then_inc(x_done[b], 1)

                for f in range(FILLS):
                    turn_tokens(0, f)

                def gate_up(e, s, t):
                    p, n, half, m = t % 2, t // 2, t // MI, t % MI
                    pe.wait_ge(h_done[p], e * SB2 + n)
                    for sec, bank in ((GATE, g_ps[p]), (UP, up_ps[p])):
                        for j, (a, b) in enumerate(PASSES):
                            for k in range(KD):
                                at = sec * SEC + k * I + m * P
                                mm = pe.matmul(bank[:, :], w_r[s][:, a, at:at + P],
                                               xgt[s][:, b, k, half * 512:(half + 1) * 512],
                                               start=(j == 0 and k == 0),
                                               stop=(j == len(PASSES) - 1 and k == KD - 1))
                    mm.then_inc(gu_done[p], 1)

                def down(e, s, t):
                    p, n, half, m = t % 2, t // 2, t // MI, t % MI
                    pe.wait_ge(hl_done[p], e * SB2 + n + 1)
                    if m == 0:
                        pe.wait_ge(y_read, e * HALVES + half)
                    at = DOWN * SEC + m * D
                    for j in range(TPB):
                        for q, (a, b) in enumerate(PASSES):
                            mm = pe.matmul(y_ps[:, j, :], hid_r[p][:, a, j * P:(j + 1) * P],
                                           w_r[s][:, b, at:at + D],
                                           start=(m == 0 and q == 0 and j % 2 == 0),
                                           stop=(m == MI - 1 and q == len(PASSES) - 1),
                                           skip_group_check=True)
                    mm.then_inc(dn_done[p], 1)

                def unit(e, i, s, more):
                    pe.wait_ge(w_lo, (e + 1) * PIECES)
                    for b in range(2):
                        pe.wait_ge(x_read[b], (e + 1) * (FILLS // 2))
                    for t in range(STEPS):
                        gate_up(e, s, t)
                        if t >= 1:
                            down(e, s, t - 1)
                        if more and t >= STEPS - FILLS:
                            turn_tokens(e + 1, t - (STEPS - FILLS))
                    down(e, s, STEPS - 1)
                each_expert(pe, unit)


def pick_expert(table, e):
    if isinstance(e, int):
        return table[:, e, :]
    return table[:, bass.ds(e, 1), :].rearrange("p a b -> p (a b)")


def combine(nc, stage, x_tiles, s_dram, ffn_tiles, out_tiles):
    stack, sb, ps, sem, pair = stage
    with stack:
        xb = [sb(f"xb{s}", [P, TPB, D]) for s in range(2)]
        sbuf = [sb(f"sbuf{s}", [P, TPB, D]) for s in range(2)]
        fb = [sb(f"fb{s}", [P, TPB, D]) for s in range(2)]
        ob = [sb(f"ob{s}", [P, TPB, D]) for s in range(2)]
        x_in, s_in, f_in = pair("cx_in"), pair("cs_in"), pair("cf_in")
        g_done, m_done, o_done, o_out = pair("cg_done"), pair("cm_done"), pair("co_done"), pair("co_out")

        with nc.Block() as block:
            @block.sync
            def _(sp):
                with sp.Fori(0, B // 2) as i:
                    for s in range(2):
                        tiles = bass.ds((i * 2 + s) * TPB, TPB)
                        sp.wait_ge(o_done[s], i)
                        sp.dma_start(fb[s][:, :, :], ffn_tiles[:, tiles, :]).then_inc(f_in[s], 16)
                        sp.dma_start(sbuf[s][:, :, :].rearrange("p t d -> p (t d)"),
                                     s_dram[bass.ds(i * 2 + s, 1), :, :].rearrange("a p n -> (a p) n"))\
                          .then_inc(s_in[s], 16)
                        sp.dma_start(xb[s][:, :, :], x_tiles[:, tiles, :]).then_inc(x_in[s], 16)

            @block.scalar
            def _(act):
                with act.Fori(0, B // 2) as i:
                    for s in range(2):
                        act.wait_ge(f_in[s], i * 16 + 16)
                        act.activation(fb[s][:, :, :], fb[s][:, :, :], ACT.Silu).then_inc(g_done[s], 1)
                    for s in range(2):
                        act.wait_ge(o_done[s], i + 1)
                        act.dma_start(out_tiles[:, bass.ds((i * 2 + s) * TPB, TPB), :],
                                      ob[s][:, :, :]).then_inc(o_out[s], 16)
                for s in range(2):
                    act.wait_ge(o_out[s], 16 * (B // 2))

            @block.vector
            def _(dve):
                with dve.Fori(0, B // 2) as i:
                    for s in range(2):
                        dve.wait_ge(s_in[s], i * 16 + 16)
                        dve.wait_ge(g_done[s], i + 1)
                        dve.tensor_tensor(fb[s][:, :, :], fb[s][:, :, :], sbuf[s][:, :, :], ALU.mult)\
                           .then_inc(m_done[s], 1)
                        dve.wait_ge(m_done[s], i + 1)
                        dve.wait_ge(x_in[s], i * 16 + 16)
                        dve.wait_ge(o_out[s], i * 16)
                        dve.tensor_tensor(ob[s][:, :, :], fb[s][:, :, :], xb[s][:, :, :], ALU.add)\
                           .then_inc(o_done[s], 1)


def kernel(L0_attn_x, L0_attn_Wq, L0_attn_Wk, L0_attn_Wv, L0_attn_Wo, L0_attn_Wf, L0_attn_delta,
           L0_attn_norm_weight, L0_ffn_gate_w, L0_ffn_w_gate, L0_ffn_w_up, L0_ffn_w_down):
    import concourse.bacc as bacc
    from concourse.bass_utils import run_bass_kernel_spmd

    def rows_in_halves(w):
        w = np.asarray(w).T
        return w.reshape(-1, P, w.shape[1]).transpose(1, 0, 2)

    w_attn = np.stack([rows_in_halves(w) for w in (L0_attn_Wq, L0_attn_Wk, L0_attn_Wv, L0_attn_Wo)], 1)
    w_logit = rows_in_halves(np.concatenate([np.asarray(L0_ffn_gate_w), np.asarray(L0_attn_Wf)], 0))
    w_experts = np.stack([
        np.concatenate([rows_in_halves(w[e]).reshape(P, -1)
                        for w in (L0_ffn_w_gate, L0_ffn_w_up, L0_ffn_w_down)], 1) for e in range(E)], 0)
    arrays = {
        "x": np.asarray(L0_attn_x).reshape(B * N, D),
        "w_attn": w_attn,
        "w_logit": w_logit,
        "delta": np.asarray(L0_attn_delta),
        "norm_w": np.asarray(L0_attn_norm_weight).reshape(KD, P).T,
        "w_experts": w_experts,
    }
    arrays = {n: np.ascontiguousarray(a) for n, a in arrays.items()}
    nc = bacc.Bacc("TRN2", target_bir_lowering=False, num_devices=1)
    aps = {n: nc.dram_tensor(n, a.shape, mybir.dt.from_np(a.dtype), kind="ExternalInput").ap()
           for n, a in arrays.items()}
    out = nc.dram_tensor("out", (B * N, D), F32, kind="ExternalOutput").ap()
    build(nc, out=out, **aps)
    result = run_bass_kernel_spmd(nc, [arrays], core_ids=[0])
    return result.results[0]["out"].reshape(B, N, D)
```

```python
from contextlib import ExitStack

import numpy as np
import concourse.bass as bass
from concourse import mybir

ALU = mybir.AluOpType
ACT = mybir.ActivationFunctionType
AX = mybir.AxisListType
F32 = mybir.dt.float32
F32R = mybir.dt.float32r
I32 = mybir.dt.int32
U32 = mybir.dt.uint32

P = 128
B, N, D = 8, 512, 256
H, HD = 16, 16
E, I = 8, 1024
CAP = N // E * 2
TPB = N // P
NT = B * TPB
KD = D // P
NL = E + H
HH = H // KD
G4 = 4
NG = H // G4
MI = I // P
WE = 3 * I * D // P
HI, LO = 0, 1
PASSES = [(HI, HI), (HI, LO), (LO, HI)]
LN_EPS, RMS_EPS = 1e-5, 1e-6
TOPK_ROUND = 8
ROUNDS_PER_BATCH = CAP // TOPK_ROUND // B


def f32(ap):
    return ap.bitcast(F32)


def spread(ap, n):
    return ap.unsqueeze(len(ap.shape)).broadcast_to([*ap.shape, n])


def build(nc, x, w_attn, w_logit, delta, norm_w, w_experts, out):
    xn_dram = nc.dram_tensor("xn_dram", [B * N, D], F32, kind="Internal").ap()
    xt_dram = nc.dram_tensor("xt_dram", [B, P, 2 * KD * N], F32, kind="Internal").ap()
    decay_dram = nc.dram_tensor("decay_dram", [2, NT, H * P], F32, kind="Internal").ap()
    neg_decay_dram = nc.dram_tensor("neg_decay_dram", [2, NT, H * P], F32, kind="Internal").ap()
    o_dram = nc.dram_tensor("o_dram", [NT, P, D], F32, kind="Internal").ap()
    s_dram = nc.dram_tensor("s_dram", [B, P, TPB * D], F32, kind="Internal").ap()
    ffn_dram = nc.dram_tensor("ffn_dram", [B * N, D], F32, kind="Internal").ap()
    x_tiles = x.rearrange("(t p) d -> p t d", p=P)
    xn_tiles = xn_dram.rearrange("(t p) d -> p t d", p=P)
    out_tiles = out.rearrange("(t p) d -> p t d", p=P)
    ffn_tiles = ffn_dram.rearrange("(t p) d -> p t d", p=P)

    with ExitStack() as whole:
        def sb_in(stack):
            return lambda name, shape, dt=F32: stack.enter_context(nc.sbuf_tensor(name, shape, dt))

        def ps_in(stack):
            return lambda name, shape: stack.enter_context(nc.psum_tensor(name, shape, F32))

        def sems_in(stack):
            def make(*names):
                made = [stack.enter_context(nc.semaphore(n)) for n in names]
                return made if len(made) > 1 else made[0]
            return make

        def pair_in(stack):
            make = sems_in(stack)
            return lambda name: [make(f"{name}0"), make(f"{name}1")]

        makers = (sb_in, ps_in, sems_in, pair_in)
        sb = sb_in(whole)
        ident = sb("ident", [P, P])
        top_val = sb("top_val", [B * E, CAP])
        top_idx = sb("top_idx", [B * E, CAP])
        wo_r = sb("wo_r", [P, 2, KD, D], F32R)
        o_stats = sb("o_stats", [P, NT, 6])
        with ExitStack() as branch:
            sb = sb_in(branch)
            aff_t = sb("aff_t", [B * E, N])
            exp_lb = sb("exp_lb", [P, NT, H])
            exp_rest = sb("exp_rest", [P, NT, H])
            exp_tot = sb("exp_tot", [P, KD, NT])
            attn_w = sb("attn_w", [P, 2, 3, KD, D], F32R)
            normalise(nc, stage_of(makers), x_tiles, xn_tiles, xt_dram, decay_dram, neg_decay_dram,
                      w_attn, w_logit, delta, norm_w, ident, aff_t, exp_lb, exp_rest, exp_tot, attn_w,
                      wo_r)
            attention(nc, stage_of(makers), xt_dram, decay_dram, neg_decay_dram, o_dram, ident, aff_t,
                      top_val, top_idx, exp_lb, exp_rest, exp_tot, attn_w, o_stats)
        experts(nc, stage_of(makers), makers, x_tiles, xn_dram, o_dram, s_dram, ffn_dram, ffn_tiles,
                out_tiles, w_experts, ident, top_val, top_idx, wo_r, o_stats)


def stage_of(makers):
    stack = ExitStack()
    return (stack, *(m(stack) for m in makers))


def normalise(nc, stage, x_tiles, xn_tiles, xt_dram, decay_dram, neg_decay_dram, w_attn, w_logit, delta,
              norm_w, ident, aff_t, exp_lb, exp_rest, exp_tot, attn_w, wo_r):
    stack, sb, ps, sem, pair = stage
    with stack:
        x_all = sb("x_all", [P, NT, D])
        xn = [sb(f"xn{s}", [P, TPB, D]) for s in range(2)]
        xt = [sb(f"xt{s}", [P, 2, KD, N], F32R) for s in range(2)]
        w_raw = sb("w_raw", [P, 4, KD, D])
        wl_raw = sb("wl_raw", [P, KD, NL])
        wl = sb("wl", [P, 2, KD, NL], F32R)
        delta_row = sb("delta_row", [P, H])
        norm_col = sb("norm_col", [P, KD])
        tri = sb("tri", [P, P])
        ones = sb("ones", [P, P])
        head_rows = sb("head_rows", [H, KD, P])
        stats = sb("stats", [P, NT, 6])
        mv = sb("mv", [P, NT, 2])
        var = sb("var", [P, NT])
        lnv = sb("lnv", [P, NT])
        rstd0 = sb("rstd0", [P, NT])
        newton = sb("newton", [P, NT])
        rstd = sb("rstd", [P, NT])
        logits = sb("logits", [P, NT, NL])
        aff = sb("aff", [P, NT, E])
        aff_c = sb("aff_c", [P, TPB, B, E])
        peak = sb("peak", [P, NT])
        z = sb("z", [P, NT, H])
        en = sb("en", [P, NT, H])
        u = sb("u", [P, NT, H])
        lnu = sb("lnu", [P, NT, H])
        c1 = sb("c1", [P, NT, H])
        ru = sb("ru", [P, NT, H])
        lf = sb("lf", [P, NT, H])
        lb = sb("lb", [P, NT, H])
        tot_t = sb("tot_t", [H, NT])
        lbt = sb("lbt", [P, 2, TPB, P], F32R)
        nlbt = sb("nlbt", [P, 2, TPB, P], F32R)
        t_ps = [ps(f"t_ps{s}", [P, KD, N]) for s in range(2)]
        l_ps = [ps(f"l_ps{s}", [P, 512]) for s in range(2)]
        m_ps = [ps(f"m_ps{s}", [P, 512]) for s in range(2)]

        x_in = [sem(f"x_in{b}") for b in range(B)]
        w_in = sem("w_in")
        consts = sem("consts")
        w_hi, w_lo, st = sem("w_hi"), sem("w_lo"), sem("st")
        ln_act = sem("ln_act")
        xn_done, xn_stored = pair("xn_done"), pair("xn_stored")
        t_done, hi_done, lo_done = pair("t_done"), pair("hi_done"), pair("lo_done")
        xt_stored, l_done, l_read = pair("xt_stored"), pair("l_done"), pair("l_read")
        v_step, a_step, p_step, d_out = sem("v_step"), sem("a_step"), sem("p_step"), sem("d_out")

        with nc.Block() as block:
            @block.sync
            def _(sp):
                for b in range(B):
                    sp.dma_start(x_all[:, b * TPB:(b + 1) * TPB, :],
                                 x_tiles[:, b * TPB:(b + 1) * TPB, :]).then_inc(x_in[b], 16)
                with sp.Fori(0, B // 2) as i:
                    for s in range(2):
                        sp.wait_ge(xn_done[s], i + 1)
                        sp.dma_start(xn_tiles[:, bass.ds((i * 2 + s) * TPB, TPB), :],
                                     xn[s][:, :, :]).then_inc(xn_stored[s], 16)
                    for s in range(2):
                        sp.wait_ge(lo_done[s], i + 1)
                        sp.dma_start(xt_dram[bass.ds(i * 2 + s, 1), :, :].rearrange("a p n -> (a p) n"),
                                     f32(xt[s][:, :, :, :]).rearrange("p l k n -> p (l k n)"))\
                          .then_inc(xt_stored[s], 16)
                sp.wait_ge(a_step, 8)
                sp.wait_ge(v_step, 19)
                sp.dma_start(decay_dram.rearrange("l (g t) (h n) -> (t h) l g n", g=TPB, h=H),
                             f32(lbt[:, :, :, :])).then_inc(d_out, 16)
                sp.wait_ge(a_step, 10)
                sp.dma_start(neg_decay_dram.rearrange("l (g t) (h n) -> (t h) l g n", g=TPB, h=H),
                             f32(nlbt[:, :, :, :])).then_inc(d_out, 16)
                sp.wait_ge(d_out, 32)
                for s in range(2):
                    sp.wait_ge(xn_stored[s], 16 * (B // 2))
                    sp.wait_ge(xt_stored[s], 16 * (B // 2))

            @block.gpsimd
            def _(pool):
                pool.memset(ident[:, :], 0.0).then_inc(consts, 1)
                pool.memset(tri[:, :], 1.0).then_inc(consts, 1)
                pool.memset(ones[:, :], 1.0).then_inc(consts, 1)
                pool.memset(head_rows[:, :, :], 1.0).then_inc(consts, 1)
                pool.wait_ge(consts, 4)
                pool.affine_select(out=ident[:, :], in_=ident[:, :], compare_op=ALU.not_equal, fill=1.0,
                                   base=0, pattern=[[-1, P]], channel_multiplier=1).then_inc(consts, 1)
                pool.affine_select(out=tri[:, :], in_=tri[:, :], compare_op=ALU.is_ge, fill=0.0,
                                   base=0, pattern=[[1, P]], channel_multiplier=-1).then_inc(consts, 1)
                pool.affine_select(out=head_rows[:, :, :], in_=head_rows[:, :, :], compare_op=ALU.is_ge,
                                   fill=0.0, base=0, pattern=[[P, KD], [1, P]],
                                   channel_multiplier=-HD).then_inc(consts, 1)
                pool.wait_ge(consts, 7)
                pool.affine_select(out=head_rows[:, :, :], in_=head_rows[:, :, :], compare_op=ALU.is_ge,
                                   fill=0.0, base=HD - 1, pattern=[[-P, KD], [-1, P]],
                                   channel_multiplier=HD).then_inc(consts, 1)

            @block.scalar
            def _(act):
                act.dma_start(w_raw[:, :, :, :], w_attn).then_inc(w_in, 16)
                act.dma_start(wl_raw[:, :, :], w_logit).then_inc(w_in, 16)
                act.dma_start(delta_row[:, :], delta.unsqueeze(0).broadcast_to([P, H])).then_inc(w_in, 16)
                act.dma_start(norm_col[:, :], norm_w).then_inc(w_in, 16)
                act.wait_ge(st, NT + NT + 1)
                act.activation(lnv[:, :], var[:, :], ACT.Ln).then_inc(ln_act, 1)
                act.wait_ge(ln_act, 1)
                act.activation(rstd0[:, :], lnv[:, :], ACT.Exp, scale=-0.5).then_inc(ln_act, 1)
                act.wait_ge(w_in, 64)
                act.activation(wl[:, HI, :, :], wl_raw[:, :, :], ACT.Copy).then_inc(w_hi, 1)
                act.activation(attn_w[:, HI, :, :, :], w_raw[:, 0:3, :, :], ACT.Copy).then_inc(w_hi, 1)
                with act.Fori(0, B // 2) as i:
                    for s in range(2):
                        act.wait_ge(t_done[s], i + 1)
                        act.wait_ge(l_done[s], i)
                        act.wait_ge(xt_stored[s], i * 16)
                        act.activation(xt[s][:, HI, :, :], t_ps[s][:, :, :], ACT.Copy)\
                           .then_inc(hi_done[s], 1)
                act.wait_ge(st, 2 * NT + 7)
                act.activation(wo_r[:, HI, :, :], w_raw[:, 3, :, :], ACT.Copy).then_inc(w_hi, 1)
                act.wait_ge(v_step, 3)
                act.activation(aff[:, :, :], aff[:, :, :], ACT.Exp).then_inc(a_step, 1)
                act.wait_ge(v_step, 4)
                act.activation(en[:, :, :], en[:, :, :], ACT.Exp, scale=-1.0).then_inc(a_step, 1)
                act.wait_ge(v_step, 8)
                act.activation(lnu[:, :, :], u[:, :, :], ACT.Ln).then_inc(a_step, 1)
                act.wait_ge(p_step, 2)
                act.activation(lb[:, :, :], m_ps[1][:, :].rearrange("p (t h) -> p t h", h=H), ACT.Copy)\
                   .then_inc(a_step, 1)
                act.wait_ge(a_step, 4)
                act.activation(exp_lb[:, :, :], lb[:, :, :], ACT.Exp).then_inc(a_step, 1)
                act.wait_ge(v_step, 17)
                act.activation(exp_rest[:, :, :], exp_rest[:, :, :], ACT.Exp).then_inc(a_step, 1)
                act.wait_ge(p_step, 5)
                act.activation(exp_tot[:, :, :], m_ps[1][:, 0:KD * NT].rearrange("p (k t) -> p k t", k=KD),
                               ACT.Exp).then_inc(a_step, 1)
                act.wait_ge(p_step, 6)
                act.activation(lbt[:, HI, :, :], l_ps[0][:, :].rearrange("p (g n) -> p g n", g=TPB),
                               ACT.Copy).then_inc(a_step, 1)
                act.wait_ge(a_step, 8)
                act.activation(nlbt[:, HI, :, :], f32(lbt[:, HI, :, :]), ACT.Copy, scale=-1.0)\
                   .then_inc(a_step, 1)
                act.wait_ge(v_step, 19)
                act.activation(nlbt[:, LO, :, :], f32(lbt[:, LO, :, :]), ACT.Copy, scale=-1.0)\
                   .then_inc(a_step, 1)

            @block.vector
            def _(dve):
                for b in range(B):
                    dve.wait_ge(x_in[b], 16)
                    for t in range(b * TPB, (b + 1) * TPB):
                        dve.bn_stats(stats[:, t, :], x_all[:, t, :]).then_inc(st, 1)
                dve.wait_ge(st, NT)
                for t in range(NT):
                    dve.bn_aggr(mv[:, t, :], stats[:, t, :]).then_inc(st, 1)
                dve.wait_ge(st, 2 * NT)
                dve.tensor_scalar(var[:, :], mv[:, :, 1], LN_EPS, None, ALU.add).then_inc(st, 1)
                dve.wait_ge(ln_act, 2)
                dve.tensor_tensor(newton[:, :], rstd0[:, :], rstd0[:, :], ALU.mult).then_inc(st, 1)
                dve.wait_ge(st, 2 * NT + 2)
                dve.tensor_tensor(newton[:, :], newton[:, :], var[:, :], ALU.mult).then_inc(st, 1)
                dve.wait_ge(st, 2 * NT + 3)
                dve.tensor_scalar(newton[:, :], newton[:, :], -0.5, 1.5, ALU.mult, ALU.add).then_inc(st, 1)
                dve.wait_ge(st, 2 * NT + 4)
                dve.tensor_tensor(rstd[:, :], rstd0[:, :], newton[:, :], ALU.mult).then_inc(st, 1)
                dve.wait_ge(w_in, 64)
                for k in range(KD):
                    dve.tensor_scalar(w_raw[:, 3, k, :], w_raw[:, 3, k, :], norm_col[:, k:k + 1], None,
                                      ALU.mult).then_inc(st, 1)
                dve.wait_ge(w_hi, 2)
                dve.tensor_tensor(wl[:, LO, :, :], wl_raw[:, :, :], f32(wl[:, HI, :, :]), ALU.subtract)\
                   .then_inc(w_lo, 1)
                dve.wait_ge(st, 2 * NT + 7)
                with dve.Fori(0, B // 2) as i:
                    for s in range(2):
                        dve.wait_ge(xn_stored[s], i * 16)
                        dve.wait_ge(t_done[s], i)
                        for t in range(TPB):
                            tile = (i * 2 + s) * TPB + t
                            norm = dve.tensor_scalar(
                                xn[s][:, t, :], x_all[:, bass.ds(tile, 1), :].rearrange("p a d -> p (a d)"),
                                mv[:, bass.ds(tile, 1), 0:1].rearrange("p a d -> p (a d)"),
                                rstd[:, bass.ds(tile, 1)], ALU.subtract, ALU.mult)
                        norm.then_inc(xn_done[s], 1)
                    for s in range(2):
                        dve.wait_ge(hi_done[s], i + 1)
                        dve.tensor_tensor(xt[s][:, LO, :, :], t_ps[s][:, :, :], f32(xt[s][:, HI, :, :]),
                                          ALU.subtract).then_inc(lo_done[s], 1)
                    for s in range(2):
                        dve.wait_ge(l_done[s], i + 1)
                        dve.tensor_copy(logits[:, bass.ds((i * 2 + s) * TPB, TPB), :],
                                        l_ps[s][:, 0:TPB * NL].rearrange("p (t n) -> p t n", n=NL))\
                           .then_inc(l_read[s], 1)
                dve.wait_ge(w_hi, 3)
                dve.tensor_tensor(attn_w[:, LO, :, :, :], w_raw[:, 0:3, :, :], f32(attn_w[:, HI, :, :, :]),
                                  ALU.subtract).then_inc(w_lo, 1)
                dve.tensor_tensor(wo_r[:, LO, :, :], w_raw[:, 3, :, :], f32(wo_r[:, HI, :, :]),
                                  ALU.subtract).then_inc(w_lo, 1)
                for s in range(2):
                    dve.wait_ge(l_read[s], B // 2)
                router, forget = logits[:, :, 0:E], logits[:, :, E:NL]
                dve.tensor_tensor(z[:, :, :], forget, delta_row[:, :].unsqueeze(1).broadcast_to([P, NT, H]),
                                  ALU.add).then_inc(v_step, 1)
                dve.tensor_reduce(peak[:, :], router, AX.X, ALU.max).then_inc(v_step, 1)
                dve.wait_ge(v_step, 2)
                dve.tensor_tensor(aff[:, :, :], router, spread(peak[:, :], E), ALU.subtract)\
                   .then_inc(v_step, 1)
                dve.scalar_tensor_tensor(out=en[:, :, :], in0=z[:, :, :], scalar=-1.0, in1=z[:, :, :],
                                         op0=ALU.mult, op1=ALU.max).then_inc(v_step, 1)
                dve.wait_ge(a_step, 1)
                dve.wait_ge(v_step, 3)
                dve.tensor_reduce(peak[:, :], aff[:, :, :], AX.X, ALU.add).then_inc(v_step, 1)
                dve.wait_ge(v_step, 5)
                dve.reciprocal(peak[:, :], peak[:, :]).then_inc(v_step, 1)
                dve.wait_ge(v_step, 6)
                dve.tensor_tensor(aff_c[:, :, :, :].rearrange("p c b e -> p b c e"),
                                  aff[:, :, :].rearrange("p (b c) e -> p b c e", c=TPB),
                                  spread(peak[:, :].rearrange("p (b c) -> p b c", c=TPB), E), ALU.mult)\
                   .then_inc(v_step, 1)
                dve.wait_ge(a_step, 2)
                dve.tensor_scalar(u[:, :, :], en[:, :, :], 1.0, None, ALU.add).then_inc(v_step, 1)
                dve.wait_ge(v_step, 8)
                dve.tensor_scalar(c1[:, :, :], u[:, :, :], -1.0, None, ALU.add).then_inc(v_step, 1)
                dve.wait_ge(v_step, 9)
                dve.tensor_tensor(c1[:, :, :], en[:, :, :], c1[:, :, :], ALU.subtract).then_inc(v_step, 1)
                dve.reciprocal(ru[:, :, :], u[:, :, :]).then_inc(v_step, 1)
                dve.wait_ge(v_step, 11)
                dve.tensor_tensor(c1[:, :, :], c1[:, :, :], ru[:, :, :], ALU.mult).then_inc(v_step, 1)
                dve.wait_ge(a_step, 3)
                dve.wait_ge(v_step, 12)
                dve.tensor_tensor(lnu[:, :, :], lnu[:, :, :], c1[:, :, :], ALU.add).then_inc(v_step, 1)
                dve.tensor_scalar(z[:, :, :], z[:, :, :], 0.0, None, ALU.min).then_inc(v_step, 1)
                dve.wait_ge(v_step, 14)
                dve.tensor_tensor(lf[:, :, :], z[:, :, :], lnu[:, :, :], ALU.subtract).then_inc(v_step, 1)
                dve.wait_ge(p_step, 1)
                dve.tensor_copy(aff_t[:, :], m_ps[0][0:B * E, :]).then_inc(v_step, 1)
                dve.wait_ge(p_step, 3)
                dve.wait_ge(a_step, 4)
                dve.tensor_tensor(exp_rest[:, :, :], t_ps[0][:, 0, :].rearrange("p (t h) -> p t h", h=H),
                                  lb[:, :, :], ALU.subtract).then_inc(v_step, 1)
                dve.wait_ge(p_step, 4)
                dve.tensor_copy(tot_t[:, :], t_ps[1][0:H, 0, 0:NT]).then_inc(v_step, 1)
                dve.wait_ge(a_step, 8)
                dve.tensor_tensor(lbt[:, LO, :, :], l_ps[0][:, :].rearrange("p (g n) -> p g n", g=TPB),
                                  f32(lbt[:, HI, :, :]), ALU.subtract).then_inc(v_step, 1)

            @block.tensor
            def _(pe):
                pe.wait_ge(consts, 8)
                pe.wait_ge(w_lo, 1)
                with pe.Fori(0, B // 2) as i:
                    for s in range(2):
                        pe.wait_ge(xn_done[s], i + 1)
                        pe.wait_ge(lo_done[s], i)
                        for k in range(KD):
                            for t in range(TPB):
                                mm = pe.transpose(t_ps[s][:, k, t * P:(t + 1) * P],
                                                  xn[s][:, t, k * P:(k + 1) * P], ident[:, :])
                        mm.then_inc(t_done[s], 1)
                    for s in range(2):
                        pe.wait_ge(lo_done[s], i + 1)
                        pe.wait_ge(l_read[s], i)
                        for t in range(TPB):
                            for n, (a, b) in enumerate(PASSES):
                                for k in range(KD):
                                    mm = pe.matmul(l_ps[s][:, t * NL:(t + 1) * NL],
                                                   xt[s][:, a, k, t * P:(t + 1) * P], wl[:, b, k, :],
                                                   start=(n == 0 and k == 0),
                                                   stop=(n == len(PASSES) - 1 and k == KD - 1))
                        mm.then_inc(l_done[s], 1)
                pe.wait_ge(v_step, 7)
                for c in range(TPB):
                    mm = pe.transpose(m_ps[0][0:B * E, c * P:(c + 1) * P],
                                      aff_c[:, c, :, :].rearrange("p b e -> p (b e)"), ident[:, :])
                mm.then_inc(p_step, 1)
                pe.wait_ge(v_step, 15)
                pe.matmul(m_ps[1][:, :], tri[:, :], lf[:, :, :].rearrange("p t h -> p (t h)"),
                          start=True, stop=True).then_inc(p_step, 1)
                pe.matmul(t_ps[0][:, 0, :], ones[:, :], lf[:, :, :].rearrange("p t h -> p (t h)"),
                          start=True, stop=True).then_inc(p_step, 1)
                for t in range(NT):
                    mm = pe.matmul(t_ps[1][0:H, 0, t:t + 1], lf[:, t, :], ones[:, 0:1],
                                   start=True, stop=True)
                mm.then_inc(p_step, 1)
                pe.wait_ge(v_step, 18)
                pe.wait_ge(a_step, 4)
                for k in range(KD):
                    mm = pe.matmul(m_ps[1][:, k * NT:(k + 1) * NT], head_rows[:, k, :], tot_t[:, :],
                                   start=True, stop=True)
                mm.then_inc(p_step, 1)
                for g in range(TPB):
                    mm = pe.transpose(l_ps[0][:, g * P:(g + 1) * P],
                                      lb[:, g * 8:(g + 1) * 8, :].rearrange("p t h -> p (t h)"),
                                      ident[:, :])
                mm.then_inc(p_step, 1)


def attention(nc, stage, xt_dram, decay_dram, neg_decay_dram, o_dram, ident, aff_t, top_val, top_idx,
              exp_lb, exp_rest, exp_tot, attn_w, o_stats):
    stack, sb, ps, sem, pair = stage
    Q, K = 0, 1
    USES = [("qk", 2 * m + k) for m in range(2) for k in range(KD)] \
        + [("v", c) for c in range(TPB)] + [("kt", c) for c in range(TPB)]
    PER_BANK = len(USES) // 2
    CH = TPB // 2
    GB = NG * TPB // 2
    TOP_STEPS = 4

    with stack:
        xt = sb("xt", [P, 2, KD, N], F32R)
        qk = sb("qk", [P, 2, KD, N])
        qk_r = sb("qk_r", [P, 2, 2, KD, N], F32R)
        v = sb("v", [P, TPB, D])
        kd = sb("kd", [P, TPB, D])
        q_sep = sb("q_sep", [P, HH, 2, KD, N], F32R)
        pick = [sb(f"pick{s}", [P, H, P], F32R) for s in range(2)]
        lb_cols = [sb(f"lb_cols{s}", [P, P], F32R) for s in range(2)]
        pick_f = sb("pick_f", [2 * H, H, P])
        row_one = sb("row_one", [P, P])
        absd = [sb(f"absd{s}", [P, G4, P]) for s in range(2)]
        decay = [sb(f"decay{s}", [P, G4, P]) for s in range(2)]
        score = [sb(f"score{s}", [P, G4, P]) for s in range(2)]
        block_mask = sb("block_mask", [P, HH, HD])
        state = sb("state", [P, KD, P])
        upd = sb("upd", [P, KD, P])
        o_sb = [sb(f"o_sb{s}", [P, H, HD]) for s in range(2)]
        m8 = sb("m8", [B * E, ROUNDS_PER_BATCH, TOPK_ROUND])
        i8 = sb("i8", [B * E, ROUNDS_PER_BATCH, TOPK_ROUND], U32)
        p_ps = [ps(f"p_ps{s}", [P, 512]) for s in range(2)]
        d_ps = [ps(f"d_ps{s}", [P, G4, P]) for s in range(2)]
        a_ps = [ps(f"a_ps{s}", [P, G4, P]) for s in range(2)]
        o_ps = ps("o_ps", [P, 2, D])
        u_ps = ps("u_ps", [P, KD, 256])

        setup, ready = sem("setup"), sem("ready")
        turn, v_turn, sp_turn = sem("turn"), sem("v_turn"), sem("a_sp_turn")
        xt_in = sem("xt_in")
        lb_in, q_in = pair("lb_in"), sem("q_in")
        p_done, p_read, lo_done = pair("p_done"), pair("p_read"), sem("lo_done")
        d_done, d_read, e_done, e_masked = pair("d_done"), pair("d_read"), pair("e_done"), pair("e_masked")
        a_done, a_read, av_done = pair("a_done"), pair("a_read"), pair("av_done")
        o_scaled, o_read, o_stored = sem("o_scaled"), sem("o_read"), pair("o_stored")
        u_done, u_read, s_done, topk = sem("u_done"), sem("u_read"), sem("s_done"), sem("topk")
        inter_done, stats_done = sem("inter_done"), sem("stats_done")

        def pass_at(kind, m):
            n = USES.index((kind, m))
            return n % 2, n // 2

        with nc.Block() as block:
            @block.sync
            def _(sp):
                sp.wait_ge(ready, 1)
                with sp.Fori(0, B) as i:
                    sp.wait_ge(p_done[1], i * PER_BANK)
                    sp.sem_inc(sp_turn, 1)
                    sp.dma_start(f32(xt[:, :, :, :]).rearrange("p l k n -> p (l k n)"),
                                 xt_dram[bass.ds(i, 1), :, :].rearrange("a p n -> (a p) n"))\
                      .then_inc(xt_in, 16)
                    for c in range(TPB):
                        if c == 2:
                            sp.wait_ge(a_done[1], i * GB)
                            sp.sem_inc(sp_turn, 1)
                            sp.wait_ge(lo_done, i * 4 + 2)
                            for h in range(HH):
                                rows = slice(h * HD, (h + 1) * HD)
                                sp.dma_start(f32(q_sep[rows, h, :, :, :]), f32(qk_r[rows, Q, :, :, :]))\
                                  .then_inc(q_in, 16)
                        s = c % 2
                        tile = i * TPB + c
                        before = 2 * (c - 1) if c >= 2 else 0
                        sp.wait_ge(d_done[1], i * GB + before)
                        sp.sem_inc(sp_turn, 1)
                        for part in range(2):
                            sp.dma_start(f32(lb_cols[s][part * H:(part + 1) * H, :]),
                                         neg_decay_dram[part, bass.ds(tile, 1), :]
                                         .rearrange("a (h n) -> (a h) n", h=H)).then_inc(lb_in[s], 16)
                        sp.dma_start(f32(pick[s][2 * H:2 * H + 2, :, :]).rearrange("l h n -> l (h n)"),
                                     decay_dram[:, bass.ds(tile, 1), :]
                                     .rearrange("l a n -> l (a n)")).then_inc(lb_in[s], 16)

            @block.gpsimd
            def _(pool):
                pool.memset(pick_f[:, :, :], 0.0).then_inc(setup, 1)
                pool.memset(row_one[:, :], 1.0).then_inc(setup, 1)
                pool.memset(block_mask[:, :, :], 1.0).then_inc(setup, 1)
                pool.wait_ge(setup, 3)
                pool.affine_select(out=pick_f[:, :, :], in_=pick_f[:, :, :], compare_op=ALU.not_equal,
                                   fill=1.0, base=0, pattern=[[-1, H], [0, P]], channel_multiplier=1)\
                    .then_inc(setup, 1)
                pool.affine_select(out=block_mask[:, :, :], in_=block_mask[:, :, :], compare_op=ALU.is_ge,
                                   fill=0.0, base=0, pattern=[[-HD, HH], [0, HD]], channel_multiplier=1)\
                    .then_inc(setup, 1)
                pool.wait_ge(setup, 5)
                pool.affine_select(out=pick_f[:, :, :], in_=pick_f[:, :, :], compare_op=ALU.not_equal,
                                   fill=1.0, base=-H, pattern=[[-1, H], [0, P]], channel_multiplier=1)\
                    .then_inc(setup, 1)
                pool.affine_select(out=block_mask[:, :, :], in_=block_mask[:, :, :], compare_op=ALU.is_ge,
                                   fill=0.0, base=HD - 1, pattern=[[HD, HH], [0, HD]],
                                   channel_multiplier=-1).then_inc(setup, 1)
                pool.memset(f32(q_sep[:, :, :, :, :]), 0.0).then_inc(setup, 1)
                for s in range(2):
                    pool.memset(f32(pick[s][:, :, :]), 0.0).then_inc(setup, 1)
                    pool.memset(f32(lb_cols[s][:, :]), 0.0).then_inc(setup, 1)
                with pool.Fori(0, B) as i:
                    def store(c):
                        pool.wait_ge(o_read, i * TPB + c + 1)
                        pool.sem_inc(turn, 1)
                        pool.dma_start(o_dram[bass.ds(i * TPB + c, 1), :, :].rearrange("a p d -> (a p) d"),
                                       o_sb[c % 2][:, :, :].rearrange("p h d -> p (h d)"))\
                            .then_inc(o_stored[c % 2], 16)

                    for c in range(TPB):
                        for g in range(NG):
                            p, n = g % 2, 2 * c + g // 2
                            pool.wait_ge(e_done[p], i * GB + n + 1)
                            pool.sem_inc(turn, 1)
                            pool.affine_select(out=decay[p][:, :, :], in_=decay[p][:, :, :],
                                               compare_op=ALU.is_ge, fill=0.0, base=0,
                                               pattern=[[0, G4], [1, P]], channel_multiplier=-1)\
                                .then_inc(e_masked[p], 1)
                        if c >= 1:
                            store(c - 1)
                    store(TPB - 1)
                for s in range(2):
                    pool.wait_ge(o_stored[s], 16 * B * CH)

            @block.scalar
            def _(act):
                with act.Fori(0, B) as i:
                    act.wait_ge(lo_done, i * 4)
                    act.wait_ge(q_in, i * HH * 16)
                    for n, (what, m) in enumerate(USES[:4 + TPB]):
                        b, k = n % 2, n // 2
                        act.wait_ge(p_done[b], i * PER_BANK + k + 1)
                        if what == "qk":
                            act.activation(qk[:, m // 2, m % 2, :], p_ps[b][:, :], ACT.Silu)
                            act.activation(qk_r[:, m // 2, HI, m % 2, :], p_ps[b][:, :], ACT.Silu)\
                               .then_inc(p_read[b], 1)
                        else:
                            act.activation(v[:, m, :], p_ps[b][:, 0:D], ACT.Copy).then_inc(p_read[b], 1)
                    for c in range(TPB):
                        for g in range(NG):
                            p, n = g % 2, 2 * c + g // 2
                            act.wait_ge(d_done[p], i * GB + n + 1)
                            act.activation(absd[p][:, :, :], d_ps[p][:, :, :], ACT.Abs)\
                               .then_inc(d_read[p], 1)
                            act.wait_ge(d_read[p], i * GB + n + 1)
                            act.wait_ge(a_read[p], i * GB + n)
                            act.activation(decay[p][:, :, :], absd[p][:, :, :], ACT.Exp, scale=-1.0)\
                               .then_inc(e_done[p], 1)

            @block.vector
            def _(dve):
                dve.wait_ge(setup, 12)
                for s in range(2):
                    dve.tensor_copy(pick[s][0:2 * H, :, :], pick_f[:, :, :]).then_inc(setup, 1)
                    dve.tensor_copy(lb_cols[s][2 * H:2 * H + 2, :], row_one[2 * H:2 * H + 2, :])\
                       .then_inc(setup, 1)
                dve.wait_ge(setup, 16)
                dve.sem_inc(ready, 1)
                with dve.Fori(0, B) as i:
                    def top_step(r, step):
                        at = (i * ROUNDS_PER_BATCH + r) * TOPK_ROUND
                        dve.wait_ge(topk, (i * ROUNDS_PER_BATCH + r) * TOP_STEPS + step)
                        dve.sem_inc(v_turn, 1)
                        if step == 0:
                            dve.max(m8[:, r, :], aff_t[:, :]).then_inc(topk, 1)
                        elif step == 1:
                            dve.max_index(i8[:, r, :], m8[:, r, :], aff_t[:, :]).then_inc(topk, 1)
                        else:
                            dve.match_replace(aff_t[:, :], m8[:, r, :], aff_t[:, :], -1.0).then_inc(topk, 1)
                            dve.tensor_copy(top_val[:, bass.ds(at, TOPK_ROUND)], m8[:, r, :])
                            dve.tensor_copy(top_idx[:, bass.ds(at, TOPK_ROUND)], i8[:, r, :])\
                               .then_inc(topk, 1)

                    dve.memset(state[:, :, :], 0.0).then_inc(s_done, 1)
                    for m in range(4):
                        b, k = pass_at("qk", m)
                        dve.wait_ge(p_read[b], i * PER_BANK + k + 1)
                        dve.tensor_tensor(qk_r[:, m // 2, LO, m % 2, :], qk[:, m // 2, m % 2, :],
                                          f32(qk_r[:, m // 2, HI, m % 2, :]), ALU.subtract)\
                           .then_inc(lo_done, 1)
                    for c in range(TPB):
                        b, k = pass_at("kt", c)
                        dve.wait_ge(p_done[b], i * PER_BANK + k + 1)
                        dve.tensor_tensor(kd[:, c, :].rearrange("p (h d) -> p h d", h=H),
                                          p_ps[b][:, 0:D].rearrange("p (h d) -> p h d", h=H),
                                          spread(exp_rest[:, bass.ds(i * TPB + c, 1), :]
                                                 .rearrange("p a h -> p (a h)"), HD),
                                          ALU.mult).then_inc(p_read[b], 1)

                    def output(c):
                        s = c % 2
                        dve.wait_ge(av_done[1], i * GB + 2 * c + 2)
                        dve.wait_ge(o_stored[s], (i * CH + c // 2) * 16)
                        dve.wait_ge(stats_done, i * TPB + c)
                        dve.tensor_tensor(o_sb[s][:, :, :],
                                          o_ps[:, 1, :].rearrange("p (h d) -> p h d", h=H),
                                          spread(exp_lb[:, bass.ds(i * TPB + c, 1), :]
                                                 .rearrange("p a h -> p (a h)"), HD),
                                          ALU.mult).then_inc(o_scaled, 1)
                        dve.wait_ge(o_scaled, i * TPB + c + 1)
                        dve.tensor_tensor(o_sb[s][:, :, :], o_sb[s][:, :, :],
                                          o_ps[:, 0, :].rearrange("p (h d) -> p h d", h=H), ALU.add)\
                           .then_inc(o_read, 1)
                        dve.wait_ge(o_read, i * TPB + c + 1)
                        dve.bn_stats(o_stats[:, bass.ds(i * TPB + c, 1), :].rearrange("p a n -> p (a n)"),
                                     o_sb[s][:, :, :].rearrange("p h d -> p (h d)")).then_inc(stats_done, 1)

                    def advance(c):
                        n = i * (TPB - 1) + c
                        dve.wait_ge(u_done, n + 1)
                        dve.tensor_tensor(upd[:, :, :], u_ps[:, :, 0:P],
                                          block_mask[:, :, :].rearrange("p h d -> p (h d)").unsqueeze(1)
                                          .broadcast_to([P, KD, P]), ALU.mult).then_inc(u_read, 1)
                        dve.wait_ge(u_read, n + 1)
                        dve.wait_ge(s_done, i * TPB + c + 1)
                        dve.wait_ge(inter_done, i * TPB + c + 1)
                        for k in range(KD):
                            ins = dve.scalar_tensor_tensor(
                                out=state[:, k, :], in0=state[:, k, :],
                                scalar=exp_tot[:, k, bass.ds(i * TPB + c, 1)], in1=upd[:, k, :],
                                op0=ALU.mult, op1=ALU.add)
                        ins.then_inc(s_done, 1)

                    for t in range(TPB * NG):
                        c, g, p, n = t // NG, t % NG, t % 2, t // 2
                        dve.wait_ge(a_done[p], i * GB + n + 1)
                        dve.wait_ge(e_masked[p], i * GB + n + 1)
                        dve.wait_ge(av_done[p], i * GB + n)
                        dve.tensor_tensor(score[p][:, :, :], a_ps[p][:, :, :], decay[p][:, :, :],
                                          ALU.mult).then_inc(a_read[p], 1)
                        if g == 0 and c >= 1:
                            output(c - 1)
                        elif g == 2 and c < TPB - 1:
                            advance(c)
                        elif p == 1 and n < 3 * ROUNDS_PER_BATCH:
                            top_step(n // 3, n % 3)
                    output(TPB - 1)

            @block.tensor
            def _(pe):
                pe.wait_ge(ready, 1)

                def project(i, n):
                    what, m = USES[n]
                    b, k = n % 2, n // 2
                    if n == 0:
                        pe.wait_ge(xt_in, i * 16 + 16)
                    pe.wait_ge(p_read[b], i * PER_BANK + k)
                    if what == "qk":
                        for j, (wp, xp) in enumerate(PASSES):
                            for kk in range(KD):
                                mm = pe.matmul(p_ps[b][:, :],
                                               attn_w[:, wp, m // 2, kk, (m % 2) * P:(m % 2 + 1) * P],
                                               xt[:, xp, kk, :], start=(j == 0 and kk == 0),
                                               stop=(j == len(PASSES) - 1 and kk == KD - 1))
                    elif what == "v":
                        for j, (xp, wp) in enumerate(PASSES):
                            for kk in range(KD):
                                mm = pe.matmul(p_ps[b][:, 0:D], xt[:, xp, kk, m * P:(m + 1) * P],
                                               attn_w[:, wp, 2, kk, :], start=(j == 0 and kk == 0),
                                               stop=(j == len(PASSES) - 1 and kk == KD - 1))
                    else:
                        for kk in range(KD):
                            mm = pe.transpose(p_ps[b][:, kk * P:(kk + 1) * P],
                                              qk[:, K, kk, m * P:(m + 1) * P], ident[:, :])
                    mm.then_inc(p_done[b], 1)

                def decays(i, t):
                    c, g, p, n = t // NG, t % NG, t % 2, t // 2
                    s = c % 2
                    if g == 0:
                        pe.wait_ge(lb_in[s], (i * CH + c // 2 + 1) * 48)
                    pe.wait_ge(d_read[p], i * GB + n)
                    pe.matmul(d_ps[p][:, :, :], lb_cols[s][:, :], pick[s][:, g * G4:(g + 1) * G4, :],
                              start=True, stop=True).then_inc(d_done[p], 1)

                def scores(i, t):
                    c, g, p, n = t // NG, t % NG, t % 2, t // 2
                    kk, first = g * G4 // HH, g * G4 % HH
                    if t == 0:
                        pe.wait_ge(q_in, (i + 1) * HH * 16)
                        pe.wait_ge(lo_done, i * 4 + 4)
                    pe.wait_ge(a_read[p], i * GB + n)
                    for j, (kp, qp) in enumerate(PASSES):
                        mm = pe.matmul(a_ps[p][:, :, :], qk_r[:, K, kp, kk, c * P:(c + 1) * P],
                                       q_sep[:, first:first + G4, qp, kk, c * P:(c + 1) * P],
                                       start=(j == 0), stop=(j == len(PASSES) - 1))
                    mm.then_inc(a_done[p], 1)

                def values(i, t):
                    c, g, p, n = t // NG, t % NG, t % 2, t // 2
                    pe.wait_ge(a_read[p], i * GB + n + 1)
                    for j in range(G4):
                        h = g * G4 + j
                        mm = pe.matmul(o_ps[:, 0, h * HD:(h + 1) * HD], score[p][:, j, :],
                                       v[:, c, h * HD:(h + 1) * HD], start=True, stop=True)
                    mm.then_inc(av_done[p], 1)

                def from_state(i, c):
                    pe.wait_ge(s_done, i * TPB + c + 1)
                    pe.wait_ge(o_read, i * TPB + c)
                    for kk in range(KD):
                        mm = pe.matmul(o_ps[:, 1, kk * P:(kk + 1) * P], qk[:, Q, kk, c * P:(c + 1) * P],
                                       state[:, kk, :], start=True, stop=True)
                    mm.then_inc(inter_done, 1)
                    if c == TPB - 1:
                        return
                    pe.wait_ge(u_read, i * (TPB - 1) + c)
                    for kk in range(KD):
                        mm = pe.matmul(u_ps[:, kk, 0:P], kd[:, c, kk * P:(kk + 1) * P],
                                       v[:, c, kk * P:(kk + 1) * P], start=True, stop=True)
                    mm.then_inc(u_done, 1)

                def groups(i):
                    for n in range(2):
                        b, k = pass_at("kt", TPB - 2 + n)
                        pe.wait_ge(p_read[b], i * PER_BANK + k + 1)
                    for t in range(TPB * NG):
                        if t + 1 < TPB * NG:
                            decays(i, t + 1)
                        scores(i, t)
                        if t % NG == 1:
                            from_state(i, t // NG)
                        if t >= 1:
                            values(i, t - 1)

                for n in range(len(USES)):
                    project(0, n)
                decays(0, 0)
                with pe.Fori(0, B - 1) as i:
                    groups(i)
                    project(i + 1, 0)
                    values(i, TPB * NG - 1)
                    for n in range(1, len(USES)):
                        project(i + 1, n)
                    decays(i + 1, 0)
                groups(B - 1)
                values(B - 1, TPB * NG - 1)


def out_proj(nc, stage, o_dram, s_dram, ident, wo_r, o_stats, beside):
    stack, sb, ps, sem, pair = stage
    PER = beside["pieces"] // (B // 2 - 1)
    with stack:
        o_in_sb = [sb(f"o_in_sb{s}", [P, TPB, D]) for s in range(2)]
        s_sb = sb("s_sb", [P, NT, D])
        mv = sb("o_mv", [P, NT, 2])
        ms = sb("ms", [P, NT])
        ln_ms = sb("ln_ms", [P, NT])
        r0 = sb("r0", [P, NT])
        r1 = sb("r1", [P, NT])
        ot = [sb(f"ot{s}", [P, 2, KD, N], F32R) for s in range(2)]
        t_ps = [ps(f"ot_ps{s}", [P, KD, N]) for s in range(2)]
        y_ps = ps("s_ps", [P, TPB, D])
        o_in, r_step = pair("po_in"), sem("r_step")
        t_done, hi_done, lo_done = pair("ot_done"), pair("ohi_done"), pair("olo_done")
        y_done, y_read, s_stored = pair("s_made"), sem("s_read"), sem("s_stored")

        def each_batch(eng, unit):
            with eng.Fori(0, B // 2 - 1) as i:
                for s in range(2):
                    unit(i * 2 + s, i, s, True)
            for s in range(2):
                unit(B - 2 + s, B // 2 - 1, s, False)

        with nc.Block() as block:
            @block.sync
            def _(sp):
                def load_batches(i):
                    for s in range(2):
                        sp.wait_ge(t_done[s], i)
                        sp.dma_start(o_in_sb[s][:, :, :], o_dram[bass.ds((i * 2 + s) * TPB, TPB), :, :]
                                     .rearrange("t p d -> p t d")).then_inc(o_in[s], 16)

                for i in range(2):
                    load_batches(i)
                beside["load"](sp)
                with sp.Fori(2, B // 2) as i:
                    load_batches(i)
                beside["sp"](sp)

            @block.gpsimd
            def _(pool):
                beside["pool"](pool)

            @block.scalar
            def _(act):
                act.wait_ge(r_step, NT + 3)
                act.activation(ln_ms[:, :], ms[:, :], ACT.Ln).then_inc(r_step, 1)
                act.wait_ge(r_step, NT + 4)
                act.activation(r0[:, :], ln_ms[:, :], ACT.Exp, scale=-0.5).then_inc(r_step, 1)

                def turned(i, s):
                    act.wait_ge(t_done[s], i + 1)
                    act.wait_ge(y_done[s], i)
                    act.activation(ot[s][:, HI, :, :], t_ps[s][:, :, :], ACT.Copy)\
                       .then_inc(hi_done[s], 1)

                for s in range(2):
                    turned(0, s)

                def store(b):
                    act.wait_ge(y_read, (b + 2) * 2)
                    act.dma_start(s_dram[bass.ds(b, 1), :, :].rearrange("a p n -> (a p) n"),
                                  s_sb[:, bass.ds(b * TPB, TPB), :].rearrange("p t d -> p (t d)"))\
                       .then_inc(s_stored, 16)

                with act.Fori(1, B // 2) as i:
                    for s in range(2):
                        turned(i, s)
                        store(i * 2 + s - 2)
                        for n in range(PER // 2):
                            beside["piece"](act, (i - 1) * PER + s * (PER // 2) + n)
                beside["act_end"](act)
                for b in range(B - 2, B):
                    store(b)
                act.wait_ge(s_stored, 16 * B)

            @block.vector
            def _(dve):
                beside["dve_start"](dve)
                for t in range(NT):
                    dve.bn_aggr(mv[:, t, :], o_stats[:, t, :]).then_inc(r_step, 1)
                dve.wait_ge(r_step, NT)
                dve.tensor_tensor(ms[:, :], mv[:, :, 0], mv[:, :, 0], ALU.mult).then_inc(r_step, 1)
                dve.wait_ge(r_step, NT + 1)
                dve.tensor_tensor(ms[:, :], ms[:, :], mv[:, :, 1], ALU.add).then_inc(r_step, 1)
                dve.wait_ge(r_step, NT + 2)
                dve.tensor_scalar(ms[:, :], ms[:, :], RMS_EPS, None, ALU.add).then_inc(r_step, 1)
                dve.wait_ge(r_step, NT + 5)
                dve.tensor_tensor(r1[:, :], r0[:, :], r0[:, :], ALU.mult).then_inc(r_step, 1)
                dve.wait_ge(r_step, NT + 6)
                dve.tensor_tensor(r1[:, :], r1[:, :], ms[:, :], ALU.mult).then_inc(r_step, 1)
                dve.wait_ge(r_step, NT + 7)
                dve.tensor_scalar(r1[:, :], r1[:, :], -0.5, 1.5, ALU.mult, ALU.add).then_inc(r_step, 1)
                dve.wait_ge(r_step, NT + 8)
                dve.tensor_tensor(r1[:, :], r1[:, :], r0[:, :], ALU.mult).then_inc(r_step, 1)
                dve.wait_ge(r_step, NT + 9)

                def low(i, s):
                    dve.wait_ge(hi_done[s], i + 1)
                    dve.tensor_tensor(ot[s][:, LO, :, :], t_ps[s][:, :, :], f32(ot[s][:, HI, :, :]),
                                      ALU.subtract).then_inc(lo_done[s], 1)

                def unit(b, i, s, more):
                    if more or s == 0:
                        low(i + s, 1 - s)
                    dve.wait_ge(y_done[s], i + 1)
                    for t in range(TPB):
                        ins = dve.tensor_scalar(
                            s_sb[:, bass.ds(b * TPB + t, 1), :].rearrange("p a d -> p (a d)"), y_ps[:, t, :],
                            r1[:, bass.ds(b * TPB + t, 1)], None, ALU.mult)
                        if t % 2 == 1:
                            ins.then_inc(y_read, 1)
                dve.sem_inc(y_read, 2)
                low(0, 0)
                each_batch(dve, unit)
                beside["dve"](dve)

            @block.tensor
            def _(pe):
                beside["pe_start"](pe)

                def turn(i, s):
                    pe.wait_ge(o_in[s], i * 16 + 16)
                    pe.wait_ge(lo_done[s], i)
                    for k in range(KD):
                        for t in range(TPB):
                            mm = pe.transpose(t_ps[s][:, k, t * P:(t + 1) * P],
                                              o_in_sb[s][:, t, k * P:(k + 1) * P], ident[:, :])
                    mm.then_inc(t_done[s], 1)

                def unit(b, i, s, more):
                    pe.wait_ge(lo_done[s], i + 1)
                    for t in range(TPB):
                        if t % 2 == 0:
                            pe.wait_ge(y_read, b * 2 + t // 2 + 1)
                        for j, (wp, xp) in enumerate(PASSES):
                            for k in range(KD):
                                mm = pe.matmul(y_ps[:, t, :], ot[s][:, wp, k, t * P:(t + 1) * P],
                                               wo_r[:, xp, k, :], start=(j == 0 and k == 0),
                                               stop=(j == len(PASSES) - 1 and k == KD - 1))
                    mm.then_inc(y_done[s], 1)
                    if more:
                        turn(i + 1, s)

                for s in range(2):
                    turn(0, s)
                each_batch(pe, unit)
                beside["pe"](pe)


def experts(nc, stage, makers, x_tiles, xn_dram, o_dram, s_dram, ffn_dram, ffn_tiles, out_tiles,
            w_experts, ident, top_val, top_idx, wo_r, o_stats):
    stack, sb, ps, sem, pair = stage
    SEC = WE // 3
    GATE, UP, DOWN = range(3)
    PIECES = 12
    PW = WE // PIECES
    HALVES = B // TPB
    STEPS = HALVES * MI
    SB2 = STEPS // 2
    FILLS = HALVES * KD
    with stack:
        w_raw = sb("we_raw", [P, WE])
        w_r = [sb("we_r0", [P, 2, WE], F32R)]
        xg = sb("xg", [P, B, D])
        xgt = [sb("xgt0", [P, 2, KD, B * CAP], F32R)]
        gate_all = sb("gate_all", [P, E, B])
        idx_all = sb("idx_all", [P, E, B], I32)
        batch_base = sb("batch_base", [P, B, E])
        gate_e = [sb(f"gate_e{s}", [P, B]) for s in range(2)]
        idx_e = [sb(f"idx_e{s}", [P, B], I32) for s in range(2)]
        zeros = sb("zeros", [P, 2 * D])
        x_ps = [ps(f"x_ps{s}", [P, 512]) for s in range(2)]

        zero_set, zeroed, base_set = sem("zero_set"), sem("zeroed"), sem("base_set")
        top_t, top_read = sem("top_t"), sem("top_read")
        w_in, w_hi, w_lo = sem("we_in"), sem("we_hi"), sem("we_lo")
        staged, gathered, x_read = sem("staged"), sem("gathered"), pair("x_read")
        x_done, x_hi = pair("x_done"), pair("x_hi")
        gu_done, sg_done, h_done = pair("gu_done"), pair("sg_done"), pair("h_done")
        hh_done, hl_done, dn_done = pair("hh_done"), pair("hl_done"), pair("dn_done")
        y_read, scattered = sem("ye_read"), pair("scattered")
        turn, sp_turn = sem("e_turn"), sem("sp_turn")

        def each_expert(eng, unit):
            with eng.Fori(0, E // 2 - 1) as i:
                for s in range(2):
                    unit(i * 2 + s, i, s, True)
            unit(E - 2, E // 2 - 1, 0, True)
            unit(E - 1, E // 2 - 1, 1, False)

        ZEROED = 16 * (B * N * D // P // (2 * D))

        def load(sp, e):
            sp.wait_ge(w_lo, e * PIECES)
            sp.sem_inc(sp_turn, 1)
            sp.dma_start(w_raw[:, :], w_experts[e, :, :] if isinstance(e, int) else
                         w_experts[bass.ds(e, 1), :, :].rearrange("a p n -> (a p) n")).then_inc(w_in, 16)

        def low(pool, e, s, n):
            at = slice(n * PW, (n + 1) * PW)
            pool.wait_ge(w_hi, e * PIECES + n + 1)
            pool.tensor_tensor(w_r[s][:, LO, at], w_raw[:, at], f32(w_r[s][:, HI, at]),
                               ALU.subtract).then_inc(w_lo, 1)

        def gather(pool, e, i, s):
            pool.wait_ge(scattered[s], i * 128)
            pool.sem_inc(turn, 1)
            pool.tensor_copy(idx_e[s][:, :], pick_expert(idx_all, e)).then_inc(staged, 1)
            pool.tensor_copy(gate_e[s][:, :], pick_expert(gate_all, e)).then_inc(staged, 1)
            pool.wait_ge(staged, e * 2 + 2)
            pool.sem_inc(turn, 1)
            for b in range(2):
                pool.wait_ge(x_read[b], e * (FILLS // 2))
                pool.sem_inc(turn, 1)
            for b in range(B):
                pool.indirect_dma_start(
                    out=xg[:, b, :], out_offset=None, in_=xn_dram[:, :],
                    in_offset=bass.IndirectOffsetOnAxis(ap=idx_e[s][:, b:b + 1], axis=0))\
                    .then_inc(gathered, 16)

        def high(act, e, s, n):
            at = slice(n * PW, (n + 1) * PW) if isinstance(n, int) else bass.ds(n * PW, PW)
            if isinstance(n, int) and n == 0:
                act.wait_ge(w_in, e * 16 + 16)
                act.wait_ge(dn_done[1], (e - 1) * SB2)
            act.activation(w_r[s][:, HI, at], w_raw[:, at], ACT.Copy).then_inc(w_hi, 1)

        def x_high(act, e, s, f):
            b = f % 2
            act.wait_ge(x_done[b], e * (FILLS // 2) + f // 2 + 1)
            act.activation(xgt[s][:, HI, f % KD, (f // KD) * 512:(f // KD + 1) * 512], x_ps[b][:, :],
                           ACT.Copy).then_inc(x_hi[b], 1)

        def x_low(dve, e, s, f):
            b = f % 2
            dst = slice((f // KD) * 512, (f // KD + 1) * 512)
            dve.wait_ge(x_hi[b], e * (FILLS // 2) + f // 2 + 1)
            dve.tensor_tensor(xgt[s][:, LO, f % KD, dst], x_ps[b][:, :],
                              f32(xgt[s][:, HI, f % KD, dst]), ALU.subtract).then_inc(x_read[b], 1)

        def turn_tokens(pe, e, f):
            b = f % 2
            if f == 0:
                pe.wait_ge(gathered, e * 128 + 128)
            pe.wait_ge(x_read[b], e * (FILLS // 2) + f // 2)
            for t in range(TPB):
                mm = pe.transpose(x_ps[b][:, t * P:(t + 1) * P],
                                  xg[:, (f // KD) * TPB + t, (f % KD) * P:(f % KD + 1) * P],
                                  ident[:, :])
            mm.then_inc(x_done[b], 1)

        def first_sp(sp):
            sp.wait_ge(zero_set, 1)
            rows = ffn_dram.rearrange("(p n) d -> p (n d)", p=P)
            for n in range(B * N * D // P // (2 * D)):
                sp.dma_start(rows[:, n * 2 * D:(n + 1) * 2 * D], zeros[:, :]).then_inc(zeroed, 16)

        def first_pool(pool):
            pool.memset(zeros[:, :], 0.0).then_inc(zero_set, 1)
            pool.iota(batch_base[:, :, :], pattern=[[N, B], [0, E]], base=0, channel_multiplier=0,
                      allow_small_or_imprecise_dtypes=True).then_inc(base_set, 1)
            pool.wait_ge(top_read, 2)
            gather(pool, 0, 0, 0)
            for n in range(PIECES):
                low(pool, 0, 0, n)

        def first_piece(act, n):
            act.wait_ge(w_in, 16)
            high(act, 0, 0, n)

        def first_act_end(act):
            for f in range(FILLS):
                x_high(act, 0, 0, f)

        def first_dve_start(dve):
            dve.wait_ge(top_t, 1)
            dve.wait_ge(base_set, 1)
            dve.tensor_copy(gate_all[:, :, :].rearrange("p e b -> p b e"),
                            x_ps[0][:, 0:B * E].rearrange("p (b e) -> p b e", b=B)).then_inc(top_read, 1)
            dve.tensor_tensor(idx_all[:, :, :].rearrange("p e b -> p b e"),
                              x_ps[0][:, B * E:2 * B * E].rearrange("p (b e) -> p b e", b=B),
                              batch_base[:, :, :], ALU.add).then_inc(top_read, 1)

        def first_dve(dve):
            dve.sem_inc(y_read, 2)
            for f in range(FILLS):
                x_low(dve, 0, 0, f)

        def first_pe_start(pe):
            pe.transpose(x_ps[0][:, 0:B * E], top_val[:, :], ident[0:B * E, 0:B * E])
            pe.transpose(x_ps[0][:, B * E:2 * B * E], top_idx[:, :], ident[0:B * E, 0:B * E])\
              .then_inc(top_t, 1)

        def first_pe(pe):
            pe.wait_ge(top_read, 2)
            for f in range(FILLS):
                turn_tokens(pe, 0, f)

        out_proj(nc, stage_of(makers), o_dram, s_dram, ident, wo_r, o_stats,
                 dict(load=lambda sp: load(sp, 0), sp=first_sp, pool=first_pool, pieces=PIECES,
                      piece=first_piece, act_end=first_act_end, dve_start=first_dve_start, dve=first_dve, pe_start=first_pe_start, pe=first_pe))

        w_r.append(sb("we_r1", [P, 2, WE], F32R))
        xgt.append(sb("xgt1", [P, 2, KD, B * CAP], F32R))
        sg = [sb(f"sg{s}", [P, 512]) for s in range(2)]
        hid = [sb(f"hid{s}", [P, 512]) for s in range(2)]
        hid_r = [sb(f"hid_r{s}", [P, 2, 512], F32R) for s in range(2)]
        y_sb = [sb(f"y_sb{s}", [P, TPB, D]) for s in range(HALVES)]
        g_ps = [ps(f"g_ps{s}", [P, 512]) for s in range(2)]
        up_ps = [ps(f"up_ps{s}", [P, 512]) for s in range(2)]
        y_ps = ps("ye_ps", [P, TPB, D])
        TD = TPB * D
        last_w = [f32(w_r[s][:, :, :]).rearrange("p l n -> p (l n)") for s in range(2)]
        s_at = [last_w[0][:, b * TD:(b + 1) * TD] for b in range(B)]
        f_at = [last_w[1][:, b * TD:(b + 1) * TD] for b in range(B)]
        xg_flat = xg[:, :, :].rearrange("p b d -> p (b d)")
        x_at = [w_raw[:, b * TD:(b + 1) * TD] for b in range(WE // TD)] \
            + [xg_flat[:, b * TD:(b + 1) * TD] for b in range(B - WE // TD)]
        o_at = [y_sb[h][:, :, :].rearrange("p t d -> p (t d)") for h in range(HALVES)] \
            + [sb(f"o_at{s}", [P, TD])[:, :] for s in range(2)]
        x_in, s_in = sem("cx_in"), sem("cs_in")

        with nc.Block() as block:
            @block.sync
            def _(sp):
                def unit(e, i, s, more):
                    if more:
                        load(sp, e + 1)
                each_expert(sp, unit)
                sp.wait_ge(dn_done[1], (E - 1) * SB2)
                for b in range(B):
                    sp.dma_start(s_at[b], s_dram[b, :, :]).then_inc(s_in, 16)
                sp.wait_ge(w_lo, E * PIECES)
                for b in range(2):
                    sp.wait_ge(x_done[b], E * (FILLS // 2))
                for b in range(B):
                    sp.dma_start(x_at[b].rearrange("p (t d) -> p t d", t=TPB),
                                 x_tiles[:, b * TPB:(b + 1) * TPB, :]).then_inc(x_in, 16)

            @block.gpsimd
            def _(pool):
                pool.wait_ge(zeroed, ZEROED)

                def scatter(e, i, s, half):
                    pool.wait_ge(y_read, (e * HALVES + half + 2) * 2)
                    pool.sem_inc(turn, 1)
                    if half == 0:
                        pool.wait_ge(scattered[1 - s], (i + s) * 128)
                        pool.sem_inc(turn, 1)
                    for t in range(TPB):
                        b = half * TPB + t
                        pool.indirect_dma_start(
                            out=ffn_dram[:, :],
                            out_offset=bass.IndirectOffsetOnAxis(ap=idx_e[s][:, b:b + 1], axis=0),
                            in_=y_sb[half][:, t, :], in_offset=None, compute_op=ALU.add)\
                            .then_inc(scattered[s], 16)

                def unit(e, i, s, more):
                    if more:
                        gather(pool, e + 1, i + s, 1 - s)
                        for n in range(PIECES // 2):
                            low(pool, e + 1, 1 - s, n)
                    scatter(e, i, s, 0)
                    if more:
                        for n in range(PIECES // 2, PIECES):
                            low(pool, e + 1, 1 - s, n)
                    scatter(e, i, s, 1)
                each_expert(pool, unit)
                for s in range(2):
                    pool.wait_ge(scattered[s], E // 2 * 128)

            @block.scalar
            def _(act):
                def unit(e, i, s, more):
                    for t in range(STEPS):
                        p, n = t % 2, t // 2
                        act.wait_ge(gu_done[p], e * SB2 + n + 1)
                        act.activation(sg[p][:, :], g_ps[p][:, :], ACT.Silu).then_inc(sg_done[p], 1)
                        if more and t < PIECES:
                            high(act, e + 1, 1 - s, t)
                        if more and t >= STEPS - FILLS:
                            x_high(act, e + 1, 1 - s, t - (STEPS - FILLS))
                        act.wait_ge(h_done[p], e * SB2 + n + 1)
                        act.wait_ge(dn_done[p], e * SB2 + n)
                        act.activation(hid_r[p][:, HI, :], hid[p][:, :], ACT.Copy).then_inc(hh_done[p], 1)
                each_expert(act, unit)

            @block.vector
            def _(dve):
                def gated(e, i, s, half):
                    dve.wait_ge(dn_done[1], e * SB2 + (half + 1) * MI // 2)
                    dve.wait_ge(scattered[1 - s], (i + s) * 128)
                    dve.wait_ge(staged, e * 2 + 2)
                    for t in range(TPB):
                        b = half * TPB + t
                        ins = dve.tensor_scalar(y_sb[half][:, t, :], y_ps[:, t, :], gate_e[s][:, b:b + 1],
                                                None, ALU.mult)
                        if t % 2 == 1:
                            ins.then_inc(y_read, 1)

                def unit(e, i, s, more):
                    for t in range(STEPS):
                        p, n = t % 2, t // 2
                        dve.wait_ge(sg_done[p], e * SB2 + n + 1)
                        dve.tensor_tensor(hid[p][:, :], sg[p][:, :], up_ps[p][:, :], ALU.mult)\
                           .then_inc(h_done[p], 1)
                        if more and t >= STEPS - FILLS:
                            x_low(dve, e + 1, 1 - s, t - (STEPS - FILLS))
                        dve.wait_ge(hh_done[p], e * SB2 + n + 1)
                        dve.tensor_tensor(hid_r[p][:, LO, :], hid[p][:, :], f32(hid_r[p][:, HI, :]),
                                          ALU.subtract).then_inc(hl_done[p], 1)
                        if t == MI:
                            gated(e, i, s, 0)
                    gated(e, i, s, 1)
                each_expert(dve, unit)

            @block.tensor
            def _(pe):
                def gate_up(e, s, t):
                    p, n, half, m = t % 2, t // 2, t // MI, t % MI
                    pe.wait_ge(h_done[p], e * SB2 + n)
                    for sec, bank in ((GATE, g_ps[p]), (UP, up_ps[p])):
                        for j, (a, b) in enumerate(PASSES):
                            for k in range(KD):
                                at = sec * SEC + k * I + m * P
                                mm = pe.matmul(bank[:, :], w_r[s][:, a, at:at + P],
                                               xgt[s][:, b, k, half * 512:(half + 1) * 512],
                                               start=(j == 0 and k == 0),
                                               stop=(j == len(PASSES) - 1 and k == KD - 1))
                    mm.then_inc(gu_done[p], 1)

                def down(e, s, t):
                    p, n, half, m = t % 2, t // 2, t // MI, t % MI
                    pe.wait_ge(hl_done[p], e * SB2 + n + 1)
                    at = DOWN * SEC + m * D
                    for j in range(TPB):
                        if m == 0 and j % 2 == 0:
                            pe.wait_ge(y_read, (e * HALVES + half) * 2 + j // 2 + 1)
                        for q, (a, b) in enumerate(PASSES):
                            mm = pe.matmul(y_ps[:, j, :], hid_r[p][:, a, j * P:(j + 1) * P],
                                           w_r[s][:, b, at:at + D],
                                           start=(m == 0 and q == 0 and j % 2 == 0),
                                           stop=(m == MI - 1 and q == len(PASSES) - 1),
                                           skip_group_check=True)
                    mm.then_inc(dn_done[p], 1)

                def start(e, s):
                    pe.wait_ge(w_lo, (e + 1) * PIECES)
                    for b in range(2):
                        pe.wait_ge(x_read[b], (e + 1) * (FILLS // 2))
                    gate_up(e, s, 0)

                def unit(e, i, s, more):
                    for t in range(1, STEPS):
                        gate_up(e, s, t)
                        down(e, s, t - 1)
                        if more and t >= STEPS - FILLS:
                            turn_tokens(pe, e + 1, t - (STEPS - FILLS))
                    if more:
                        start(e + 1, 1 - s)
                    down(e, s, STEPS - 1)

                start(0, 0)
                each_expert(pe, unit)

        combine(nc, stage_of(makers), f_at, o_at, x_at, s_at, x_in, s_in, ffn_tiles, out_tiles)


def pick_expert(table, e):
    if isinstance(e, int):
        return table[:, e, :]
    return table[:, bass.ds(e, 1), :].rearrange("p a b -> p (a b)")


def combine(nc, stage, fb, ob, x_at, s_at, x_in, s_in, ffn_tiles, out_tiles):
    stack, sb, ps, sem, pair = stage
    with stack:
        f_in = [sem(f"cf_in{b}") for b in range(B)]
        g_done, m_done, o_done = sem("cg_done"), sem("cm_done"), sem("co_done")
        o_out = [sem(f"co_out{b}") for b in range(B)]

        def tiles(dram, b):
            return dram[:, b * TPB:(b + 1) * TPB, :]

        with nc.Block() as block:
            @block.sync
            def _(sp):
                for b in range(B):
                    sp.dma_start(fb[b].rearrange("p (t d) -> p t d", t=TPB), tiles(ffn_tiles, b))\
                      .then_inc(f_in[b], 16)
                for b in range(B):
                    sp.wait_ge(o_done, b + 1)
                    sp.dma_start(tiles(out_tiles, b), ob[b % 4].rearrange("p (t d) -> p t d", t=TPB))\
                      .then_inc(o_out[b], 16)
                for b in range(B):
                    sp.wait_ge(o_out[b], 16)

            @block.scalar
            def _(act):
                for b in range(B):
                    act.wait_ge(f_in[b], 16)
                    if b >= 4:
                        act.wait_ge(o_out[b - 4], 16)
                    act.activation(ob[b % 4], fb[b], ACT.Silu).then_inc(g_done, 1)

            @block.vector
            def _(dve):
                dve.wait_ge(s_in, 16 * B)
                dve.wait_ge(x_in, 16 * B)
                for b in range(B):
                    dve.wait_ge(g_done, b + 1)
                    dve.tensor_tensor(ob[b % 4], ob[b % 4], s_at[b], ALU.mult).then_inc(m_done, 1)
                    dve.wait_ge(m_done, b + 1)
                    dve.tensor_tensor(ob[b % 4], ob[b % 4], x_at[b], ALU.add).then_inc(o_done, 1)


def kernel(L0_attn_x, L0_attn_Wq, L0_attn_Wk, L0_attn_Wv, L0_attn_Wo, L0_attn_Wf, L0_attn_delta,
           L0_attn_norm_weight, L0_ffn_gate_w, L0_ffn_w_gate, L0_ffn_w_up, L0_ffn_w_down):
    import concourse.bacc as bacc
    from concourse.bass_utils import run_bass_kernel_spmd

    def rows_in_halves(w):
        w = np.asarray(w).T
        return w.reshape(-1, P, w.shape[1]).transpose(1, 0, 2)

    w_attn = np.stack([rows_in_halves(w) for w in (L0_attn_Wq, L0_attn_Wk, L0_attn_Wv, L0_attn_Wo)], 1)
    w_logit = rows_in_halves(np.concatenate([np.asarray(L0_ffn_gate_w), np.asarray(L0_attn_Wf)], 0))
    w_experts = np.stack([
        np.concatenate([rows_in_halves(w[e]).reshape(P, -1)
                        for w in (L0_ffn_w_gate, L0_ffn_w_up, L0_ffn_w_down)], 1) for e in range(E)], 0)
    arrays = {
        "x": np.asarray(L0_attn_x).reshape(B * N, D),
        "w_attn": w_attn,
        "w_logit": w_logit,
        "delta": np.asarray(L0_attn_delta),
        "norm_w": np.asarray(L0_attn_norm_weight).reshape(KD, P).T,
        "w_experts": w_experts,
    }
    arrays = {n: np.ascontiguousarray(a) for n, a in arrays.items()}
    nc = bacc.Bacc("TRN2", target_bir_lowering=False, num_devices=1)
    aps = {n: nc.dram_tensor(n, a.shape, mybir.dt.from_np(a.dtype), kind="ExternalInput").ap()
           for n, a in arrays.items()}
    out = nc.dram_tensor("out", (B * N, D), F32, kind="ExternalOutput").ap()
    build(nc, out=out, **aps)
    result = run_bass_kernel_spmd(nc, [arrays], core_ids=[0])
    return result.results[0]["out"].reshape(B, N, D)
```

```python
from contextlib import ExitStack

import numpy as np
import concourse.bass as bass
from concourse import mybir

ALU = mybir.AluOpType
ACT = mybir.ActivationFunctionType
AX = mybir.AxisListType
F32 = mybir.dt.float32
F32R = mybir.dt.float32r
I32 = mybir.dt.int32
U32 = mybir.dt.uint32

P = 128
B, N, D = 8, 512, 256
H, HD = 16, 16
E, I = 8, 1024
CAP = N // E * 2
TPB = N // P
NT = B * TPB
KD = D // P
NL = E + H
HH = H // KD
G4 = 4
NG = H // G4
MI = I // P
WE = 3 * I * D // P
HI, LO = 0, 1
PASSES = [(HI, HI), (HI, LO), (LO, HI)]
LN_EPS, RMS_EPS = 1e-5, 1e-6
TOPK_ROUND = 8
ROUNDS_PER_BATCH = CAP // TOPK_ROUND // B


def f32(ap):
    return ap.bitcast(F32)


def spread(ap, n):
    return ap.unsqueeze(len(ap.shape)).broadcast_to([*ap.shape, n])


def each_batch(eng, unit):
    with eng.Fori(0, B // 2 - 1) as i:
        for s in range(2):
            unit(i * 2 + s, i, s, True)
    for s in range(2):
        unit(B - 2 + s, B // 2 - 1, s, False)


def build(nc, x, w_attn, w_logit, delta, norm_w, w_experts, out):
    xn_dram = nc.dram_tensor("xn_dram", [B * N, D], F32, kind="Internal").ap()
    xt_dram = nc.dram_tensor("xt_dram", [B, P, 2 * KD * N], F32, kind="Internal").ap()
    decay_dram = nc.dram_tensor("decay_dram", [2, NT, H * P], F32, kind="Internal").ap()
    neg_decay_dram = nc.dram_tensor("neg_decay_dram", [2, NT, H * P], F32, kind="Internal").ap()
    o_dram = nc.dram_tensor("o_dram", [NT, P, D], F32, kind="Internal").ap()
    s_dram = nc.dram_tensor("s_dram", [B, P, TPB * D], F32, kind="Internal").ap()
    ffn_dram = nc.dram_tensor("ffn_dram", [B * N, D], F32, kind="Internal").ap()
    x_tiles = x.rearrange("(t p) d -> p t d", p=P)
    xn_tiles = xn_dram.rearrange("(t p) d -> p t d", p=P)
    out_tiles = out.rearrange("(t p) d -> p t d", p=P)
    ffn_tiles = ffn_dram.rearrange("(t p) d -> p t d", p=P)

    with ExitStack() as whole:
        def sb_in(stack):
            return lambda name, shape, dt=F32: stack.enter_context(nc.sbuf_tensor(name, shape, dt))

        def ps_in(stack):
            return lambda name, shape: stack.enter_context(nc.psum_tensor(name, shape, F32))

        def sems_in(stack):
            def make(*names):
                made = [stack.enter_context(nc.semaphore(n)) for n in names]
                return made if len(made) > 1 else made[0]
            return make

        def pair_in(stack):
            make = sems_in(stack)
            return lambda name: [make(f"{name}0"), make(f"{name}1")]

        makers = (sb_in, ps_in, sems_in, pair_in)
        sb = sb_in(whole)
        d_out = sems_in(whole)("d_out")
        ident = sb("ident", [P, P])
        top_val = sb("top_val", [B * E, CAP])
        top_idx = sb("top_idx", [B * E, CAP])
        wo_r = sb("wo_r", [P, 2, KD, D], F32R)
        o_stats = sb("o_stats", [P, NT, 6])
        with ExitStack() as branch:
            sb = sb_in(branch)
            aff_t = sb("aff_t", [B * E, N])
            exp_lb = sb("exp_lb", [P, NT, H])
            exp_rest = sb("exp_rest", [P, NT, H])
            exp_tot = sb("exp_tot", [P, KD, NT])
            attn_w = sb("attn_w", [P, 2, 3, KD, D], F32R)
            q_sep = sb("q_sep", [P, HH, 2, KD, N], F32R)
            pick = [sb(f"pick{s}", [P, H, P], F32R) for s in range(2)]
            lb_cols = [sb(f"lb_cols{s}", [P, P], F32R) for s in range(2)]
            block_mask = sb("block_mask", [P, HH, HD])
            fixed = (q_sep, pick, lb_cols, block_mask)
            normalise(nc, stage_of(makers), x_tiles, xn_tiles, xt_dram, decay_dram, neg_decay_dram, d_out,
                      w_attn, w_logit, delta, norm_w, ident, aff_t, exp_lb, exp_rest, exp_tot, attn_w,
                      wo_r, fixed)
            attention(nc, stage_of(makers), xt_dram, decay_dram, neg_decay_dram, d_out, o_dram, ident, aff_t,
                      top_val, top_idx, exp_lb, exp_rest, exp_tot, attn_w, o_stats, fixed)
        experts(nc, stage_of(makers), makers, x_tiles, xn_dram, o_dram, s_dram, ffn_dram, ffn_tiles,
                out_tiles, w_experts, ident, top_val, top_idx, wo_r, o_stats)


def stage_of(makers):
    stack = ExitStack()
    return (stack, *(m(stack) for m in makers))


def normalise(nc, stage, x_tiles, xn_tiles, xt_dram, decay_dram, neg_decay_dram, d_out, w_attn, w_logit, delta,
              norm_w, ident, aff_t, exp_lb, exp_rest, exp_tot, attn_w, wo_r, fixed):
    stack, sb, ps, sem, pair = stage
    GROUPS = (range(2), range(2, B))
    with stack:
        x_all = sb("x_all", [P, NT, D])
        xn = [sb(f"xn{s}", [P, TPB, D]) for s in range(2)]
        xt = [sb(f"xt{s}", [P, 2, KD, N], F32R) for s in range(2)]
        w_raw = sb("w_raw", [P, 4, KD, D])
        wl_raw = sb("wl_raw", [P, KD, NL])
        wl = sb("wl", [P, 2, KD, NL], F32R)
        delta_row = sb("delta_row", [P, H])
        norm_col = sb("norm_col", [P, KD])
        tri = sb("tri", [P, P])
        ones = sb("ones", [P, P])
        head_rows = sb("head_rows", [H, KD, P])
        stats = sb("stats", [P, NT, 6])
        mv = sb("mv", [P, NT, 2])
        var = sb("var", [P, NT])
        lnv = sb("lnv", [P, NT])
        rstd0 = sb("rstd0", [P, NT])
        newton = sb("newton", [P, NT])
        rstd = sb("rstd", [P, NT])
        lt = [sb(f"lt{s}", [NL, N]) for s in range(2)]
        logits = sb("logits", [P, NT, NL])
        aff = sb("aff", [P, NT, E])
        aff_c = sb("aff_c", [P, TPB, B, E])
        peak = sb("peak", [P, NT])
        work = sb("work", [P, 6, NT, H])
        z, en, u, lnu, c1, ru = (work[:, n, :, :] for n in range(6))
        pick_f = work[0:2 * H, 0:4, :, :].rearrange("p a t h -> p (a t h)").rearrange("p (h n) -> p h n", h=H)
        row_one = sb("row_one", [P, P])
        q_sep, pick, lb_cols, block_mask = fixed
        setup = sem("setup")
        lf = c1
        lb = sb("lb", [P, NT, H])
        tot_t = sb("tot_t", [H, NT])
        lbt = sb("lbt", [P, 2, TPB, P], F32R)
        nlbt = sb("nlbt", [P, 2, TPB, P], F32R)
        t_ps = [ps(f"t_ps{s}", [P, KD, N]) for s in range(2)]
        l_ps = [ps(f"l_ps{s}", [P, 512]) for s in range(2)]
        m_ps = [ps(f"m_ps{s}", [P, 512]) for s in range(2)]

        x_in = [sem(f"x_in{b}") for b in range(B)]
        w_in = sem("w_in")
        consts = sem("consts")
        w_hi, w_lo, st = sem("w_hi"), sem("w_lo"), sem("st")
        ln_act, aggr, var_done, nw, wo_scaled = sem("ln_act", "aggr", "var_done", "nw", "wo_scaled")
        xn_done, xn_stored = pair("xn_done"), pair("xn_stored")
        t_done, hi_done, lo_done = pair("t_done"), pair("hi_done"), pair("lo_done")
        xt_stored, l_done, l_read = pair("xt_stored"), pair("l_done"), pair("l_read")
        lt_done, lt_turned, ru_done = pair("lt_done"), pair("lt_turned"), sem("ru_done")
        pe_turn = sem("pe_turn")
        v_step, a_step, p_step = sem("v_step"), sem("a_step"), sem("p_step")

        with nc.Block() as block:
            @block.sync
            def _(sp):
                for b in range(B):
                    sp.dma_start(x_all[:, b * TPB:(b + 1) * TPB, :],
                                 x_tiles[:, b * TPB:(b + 1) * TPB, :]).then_inc(x_in[b], 16)

                def store_xn(b, i, s):
                    sp.wait_ge(xn_done[s], i + 1)
                    sp.dma_start(xn_tiles[:, bass.ds(b * TPB, TPB), :], xn[s][:, :, :])\
                      .then_inc(xn_stored[s], 16)

                def unit(b, i, s, more):
                    if more:
                        store_xn(b + 2, i + 1, s)
                    sp.wait_ge(lo_done[s], i + 1)
                    sp.dma_start(xt_dram[bass.ds(b, 1), :, :].rearrange("a p n -> (a p) n"),
                                 f32(xt[s][:, :, :, :]).rearrange("p l k n -> p (l k n)"))\
                      .then_inc(xt_stored[s], 16)

                for s in range(2):
                    store_xn(s, 0, s)
                each_batch(sp, unit)
                sp.wait_ge(a_step, 8)
                sp.wait_ge(v_step, 18)
                sp.dma_start(decay_dram.rearrange("l (g t) (h n) -> (t h) l g n", g=TPB, h=H),
                             f32(lbt[:, :, :, :])).then_inc(d_out, 16)
                sp.wait_ge(a_step, 10)
                sp.dma_start(neg_decay_dram.rearrange("l (g t) (h n) -> (t h) l g n", g=TPB, h=H),
                             f32(nlbt[:, :, :, :])).then_inc(d_out, 16)
                for s in range(2):
                    sp.wait_ge(xn_stored[s], 16 * (B // 2))
                    sp.wait_ge(xt_stored[s], 16 * (B // 2))

            @block.gpsimd
            def _(pool):
                pool.memset(ident[:, :], 0.0).then_inc(consts, 1)
                pool.memset(tri[:, :], 1.0).then_inc(consts, 1)
                pool.memset(ones[:, :], 1.0).then_inc(consts, 1)
                pool.memset(head_rows[:, :, :], 1.0).then_inc(consts, 1)
                pool.wait_ge(consts, 4)
                pool.affine_select(out=ident[:, :], in_=ident[:, :], compare_op=ALU.not_equal, fill=1.0,
                                   base=0, pattern=[[-1, P]], channel_multiplier=1).then_inc(consts, 1)
                pool.affine_select(out=tri[:, :], in_=tri[:, :], compare_op=ALU.is_ge, fill=0.0,
                                   base=0, pattern=[[1, P]], channel_multiplier=-1).then_inc(consts, 1)
                pool.affine_select(out=head_rows[:, :, :], in_=head_rows[:, :, :], compare_op=ALU.is_ge,
                                   fill=0.0, base=0, pattern=[[P, KD], [1, P]],
                                   channel_multiplier=-HD).then_inc(consts, 1)
                pool.wait_ge(consts, 7)
                pool.affine_select(out=head_rows[:, :, :], in_=head_rows[:, :, :], compare_op=ALU.is_ge,
                                   fill=0.0, base=HD - 1, pattern=[[-P, KD], [-1, P]],
                                   channel_multiplier=HD).then_inc(consts, 1)
                pool.memset(pick_f[:, :, :], 0.0).then_inc(setup, 1)
                pool.memset(row_one[:, :], 1.0).then_inc(setup, 1)
                pool.memset(block_mask[:, :, :], 1.0).then_inc(setup, 1)
                pool.wait_ge(setup, 3)
                pool.affine_select(out=pick_f[:, :, :], in_=pick_f[:, :, :], compare_op=ALU.not_equal,
                                   fill=1.0, base=0, pattern=[[-1, H], [0, P]], channel_multiplier=1)\
                    .then_inc(setup, 1)
                pool.affine_select(out=block_mask[:, :, :], in_=block_mask[:, :, :], compare_op=ALU.is_ge,
                                   fill=0.0, base=0, pattern=[[-HD, HH], [0, HD]], channel_multiplier=1)\
                    .then_inc(setup, 1)
                pool.wait_ge(setup, 5)
                pool.affine_select(out=pick_f[:, :, :], in_=pick_f[:, :, :], compare_op=ALU.not_equal,
                                   fill=1.0, base=-H, pattern=[[-1, H], [0, P]], channel_multiplier=1)\
                    .then_inc(setup, 1)
                pool.affine_select(out=block_mask[:, :, :], in_=block_mask[:, :, :], compare_op=ALU.is_ge,
                                   fill=0.0, base=HD - 1, pattern=[[HD, HH], [0, HD]],
                                   channel_multiplier=-1).then_inc(setup, 1)
                pool.memset(f32(q_sep[:, :, :, :, :]), 0.0).then_inc(setup, 1)
                for s in range(2):
                    pool.memset(f32(pick[s][:, :, :]), 0.0).then_inc(setup, 1)
                    pool.memset(f32(lb_cols[s][:, :]), 0.0).then_inc(setup, 1)

            @block.scalar
            def _(act):
                act.dma_start(w_raw[:, :, :, :], w_attn).then_inc(w_in, 16)
                act.dma_start(wl_raw[:, :, :], w_logit).then_inc(w_in, 16)
                act.dma_start(delta_row[:, :], delta.unsqueeze(0).broadcast_to([P, H])).then_inc(w_in, 16)
                act.dma_start(norm_col[:, :], norm_w).then_inc(w_in, 16)

                def roots(g):
                    r = slice(GROUPS[g][0] * TPB, (GROUPS[g][-1] + 1) * TPB)
                    act.wait_ge(var_done, g + 1)
                    act.activation(lnv[:, r], var[:, r], ACT.Ln).then_inc(ln_act, 1)
                    act.wait_ge(ln_act, 2 * g + 1)
                    act.activation(rstd0[:, r], lnv[:, r], ACT.Exp, scale=-0.5).then_inc(ln_act, 1)

                roots(0)
                act.wait_ge(w_in, 64)
                act.activation(wl[:, HI, :, :], wl_raw[:, :, :], ACT.Copy).then_inc(w_hi, 1)

                def high(i, s):
                    act.wait_ge(t_done[s], i + 1)
                    act.wait_ge(l_done[s], i)
                    act.wait_ge(xt_stored[s], i * 16)
                    act.activation(xt[s][:, HI, :, :], t_ps[s][:, :, :], ACT.Copy).then_inc(hi_done[s], 1)

                def unit(b, i, s, more):
                    act.wait_ge(l_done[s], i + 1)
                    act.wait_ge(lt_turned[s], i)
                    act.activation(lt[s][:, :], l_ps[s][0:NL, :], ACT.Copy).then_inc(lt_done[s], 1)
                    if more:
                        high(i + 1, s)

                for s in range(2):
                    high(0, s)
                roots(1)
                each_batch(act, unit)
                act.wait_ge(wo_scaled, KD)
                act.activation(attn_w[:, HI, :, :, :], w_raw[:, 0:3, :, :], ACT.Copy).then_inc(w_hi, 1)
                act.activation(wo_r[:, HI, :, :], w_raw[:, 3, :, :], ACT.Copy).then_inc(w_hi, 1)
                act.wait_ge(v_step, 2)
                act.activation(en[:, :, :], en[:, :, :], ACT.Exp, scale=-1.0).then_inc(a_step, 1)
                act.wait_ge(v_step, 4)
                act.activation(aff[:, :, :], aff[:, :, :], ACT.Exp).then_inc(a_step, 1)
                act.wait_ge(v_step, 5)
                act.activation(lnu[:, :, :], u[:, :, :], ACT.Ln).then_inc(a_step, 1)
                act.wait_ge(a_step, 3)
                act.activation(ru[:, :, :], lnu[:, :, :], ACT.Exp, scale=-1.0).then_inc(ru_done, 1)
                act.wait_ge(p_step, 2)
                act.activation(lb[:, :, :], m_ps[1][:, :].rearrange("p (t h) -> p t h", h=H), ACT.Copy)\
                   .then_inc(a_step, 1)
                act.wait_ge(a_step, 4)
                act.activation(exp_lb[:, :, :], lb[:, :, :], ACT.Exp).then_inc(a_step, 1)
                act.wait_ge(v_step, 16)
                act.activation(exp_rest[:, :, :], exp_rest[:, :, :], ACT.Exp).then_inc(a_step, 1)
                act.wait_ge(p_step, 5)
                act.activation(exp_tot[:, :, :], m_ps[1][:, 0:KD * NT].rearrange("p (k t) -> p k t", k=KD),
                               ACT.Exp).then_inc(a_step, 1)
                act.wait_ge(p_step, 6)
                act.activation(lbt[:, HI, :, :], l_ps[0][:, :].rearrange("p (g n) -> p g n", g=TPB),
                               ACT.Copy).then_inc(a_step, 1)
                act.wait_ge(a_step, 8)
                act.activation(nlbt[:, HI, :, :], f32(lbt[:, HI, :, :]), ACT.Copy, scale=-1.0)\
                   .then_inc(a_step, 1)
                act.wait_ge(v_step, 18)
                act.activation(nlbt[:, LO, :, :], f32(lbt[:, LO, :, :]), ACT.Copy, scale=-1.0)\
                   .then_inc(a_step, 1)

            @block.vector
            def _(dve):
                def measure(batches):
                    for b in batches:
                        dve.wait_ge(x_in[b], 16)
                        for t in range(b * TPB, (b + 1) * TPB):
                            dve.bn_stats(stats[:, t, :], x_all[:, t, :]).then_inc(st, 1)

                def variances(g):
                    first, last = GROUPS[g][0] * TPB, (GROUPS[g][-1] + 1) * TPB
                    dve.wait_ge(st, last)
                    for t in range(first, last):
                        dve.bn_aggr(mv[:, t, :], stats[:, t, :]).then_inc(aggr, 1)
                    dve.wait_ge(aggr, last)
                    dve.tensor_scalar(var[:, first:last], mv[:, first:last, 1], LN_EPS, None, ALU.add)\
                       .then_inc(var_done, 1)

                def rstds(g):
                    r = slice(GROUPS[g][0] * TPB, (GROUPS[g][-1] + 1) * TPB)
                    dve.wait_ge(ln_act, 2 * g + 2)
                    dve.tensor_tensor(newton[:, r], rstd0[:, r], rstd0[:, r], ALU.mult).then_inc(nw, 1)
                    dve.wait_ge(nw, 4 * g + 1)
                    dve.tensor_tensor(newton[:, r], newton[:, r], var[:, r], ALU.mult).then_inc(nw, 1)
                    dve.wait_ge(nw, 4 * g + 2)
                    dve.tensor_scalar(newton[:, r], newton[:, r], -0.5, 1.5, ALU.mult, ALU.add)\
                       .then_inc(nw, 1)
                    dve.wait_ge(nw, 4 * g + 3)
                    dve.tensor_tensor(rstd[:, r], rstd0[:, r], newton[:, r], ALU.mult).then_inc(nw, 1)
                    dve.wait_ge(nw, 4 * g + 4)

                def norm(b, i, s):
                    dve.wait_ge(xn_stored[s], i * 16)
                    dve.wait_ge(t_done[s], i)
                    for t in range(TPB):
                        tile = b * TPB + t
                        ins = dve.tensor_scalar(
                            xn[s][:, t, :], x_all[:, bass.ds(tile, 1), :].rearrange("p a d -> p (a d)"),
                            mv[:, bass.ds(tile, 1), 0:1].rearrange("p a d -> p (a d)"),
                            rstd[:, bass.ds(tile, 1)], ALU.subtract, ALU.mult)
                    ins.then_inc(xn_done[s], 1)

                def low(i, s):
                    dve.wait_ge(hi_done[s], i + 1)
                    dve.tensor_tensor(xt[s][:, LO, :, :], t_ps[s][:, :, :], f32(xt[s][:, HI, :, :]),
                                      ALU.subtract).then_inc(lo_done[s], 1)

                def set_fixed():
                    dve.wait_ge(setup, 12)
                    for s in range(2):
                        dve.tensor_copy(pick[s][0:2 * H, :, :], pick_f[:, :, :]).then_inc(setup, 1)
                        dve.tensor_copy(lb_cols[s][2 * H:2 * H + 2, :], row_one[2 * H:2 * H + 2, :])\
                           .then_inc(setup, 1)

                def unit(b, i, s, more):
                    if more:
                        norm(b + 2, i + 1, s)
                    if more or s == 0:
                        low(i + s, 1 - s)
                    if not more and s == 1:
                        set_fixed()
                    dve.wait_ge(lt_turned[s], i + 1)
                    dve.tensor_copy(logits[:, bass.ds(b * TPB, TPB), :],
                                    m_ps[s][:, 0:TPB * NL].rearrange("p (t n) -> p t n", n=NL))\
                       .then_inc(l_read[s], 1)

                measure(range(2))
                variances(0)
                measure(range(2, 4))
                rstds(0)
                for s in range(2):
                    norm(s, 0, s)
                measure(range(4, B))
                variances(1)
                dve.wait_ge(w_in, 64)
                for k in range(KD):
                    dve.tensor_scalar(w_raw[:, 3, k, :], w_raw[:, 3, k, :], norm_col[:, k:k + 1], None,
                                      ALU.mult).then_inc(wo_scaled, 1)
                dve.wait_ge(w_hi, 1)
                dve.tensor_tensor(wl[:, LO, :, :], wl_raw[:, :, :], f32(wl[:, HI, :, :]), ALU.subtract)\
                   .then_inc(w_lo, 1)
                low(0, 0)
                rstds(1)
                each_batch(dve, unit)
                for s in range(2):
                    dve.wait_ge(l_read[s], B // 2)
                dve.wait_ge(setup, 16)
                router, forget = logits[:, :, 0:E], logits[:, :, E:NL]
                dve.tensor_tensor(z[:, :, :], forget, delta_row[:, :].unsqueeze(1).broadcast_to([P, NT, H]),
                                  ALU.add).then_inc(v_step, 1)
                dve.wait_ge(v_step, 1)
                dve.scalar_tensor_tensor(out=en[:, :, :], in0=z[:, :, :], scalar=-1.0, in1=z[:, :, :],
                                         op0=ALU.mult, op1=ALU.max).then_inc(v_step, 1)
                dve.tensor_reduce(peak[:, :], router, AX.X, ALU.max).then_inc(v_step, 1)
                dve.wait_ge(v_step, 3)
                dve.tensor_tensor(aff[:, :, :], router, spread(peak[:, :], E), ALU.subtract)\
                   .then_inc(v_step, 1)
                dve.wait_ge(a_step, 1)
                dve.tensor_scalar(u[:, :, :], en[:, :, :], 1.0, None, ALU.add).then_inc(v_step, 1)
                dve.wait_ge(v_step, 5)
                dve.tensor_scalar(c1[:, :, :], u[:, :, :], -1.0, None, ALU.add).then_inc(v_step, 1)
                dve.wait_ge(v_step, 6)
                dve.tensor_tensor(c1[:, :, :], en[:, :, :], c1[:, :, :], ALU.subtract).then_inc(v_step, 1)
                dve.wait_ge(a_step, 2)
                dve.wait_ge(v_step, 4)
                dve.tensor_reduce(peak[:, :], aff[:, :, :], AX.X, ALU.add).then_inc(v_step, 1)
                dve.wait_ge(v_step, 8)
                dve.reciprocal(peak[:, :], peak[:, :]).then_inc(v_step, 1)
                dve.wait_ge(v_step, 9)
                dve.tensor_tensor(aff_c[:, :, :, :].rearrange("p c b e -> p b c e"),
                                  aff[:, :, :].rearrange("p (b c) e -> p b c e", c=TPB),
                                  spread(peak[:, :].rearrange("p (b c) -> p b c", c=TPB), E), ALU.mult)\
                   .then_inc(v_step, 1)
                dve.wait_ge(w_hi, 3)
                dve.tensor_tensor(attn_w[:, LO, :, :, :], w_raw[:, 0:3, :, :], f32(attn_w[:, HI, :, :, :]),
                                  ALU.subtract).then_inc(w_lo, 1)
                dve.tensor_tensor(wo_r[:, LO, :, :], w_raw[:, 3, :, :], f32(wo_r[:, HI, :, :]),
                                  ALU.subtract).then_inc(w_lo, 1)
                dve.wait_ge(ru_done, 1)
                dve.tensor_tensor(c1[:, :, :], c1[:, :, :], ru[:, :, :], ALU.mult).then_inc(v_step, 1)
                dve.wait_ge(a_step, 3)
                dve.wait_ge(v_step, 11)
                dve.tensor_tensor(lnu[:, :, :], lnu[:, :, :], c1[:, :, :], ALU.add).then_inc(v_step, 1)
                dve.tensor_scalar(z[:, :, :], z[:, :, :], 0.0, None, ALU.min).then_inc(v_step, 1)
                dve.wait_ge(v_step, 13)
                dve.tensor_tensor(lf[:, :, :], z[:, :, :], lnu[:, :, :], ALU.subtract).then_inc(v_step, 1)
                dve.wait_ge(p_step, 1)
                dve.tensor_copy(aff_t[:, :], m_ps[0][0:B * E, :]).then_inc(v_step, 1)
                dve.wait_ge(p_step, 3)
                dve.wait_ge(a_step, 4)
                dve.tensor_tensor(exp_rest[:, :, :], t_ps[0][:, 0, :].rearrange("p (t h) -> p t h", h=H),
                                  lb[:, :, :], ALU.subtract).then_inc(v_step, 1)
                dve.wait_ge(p_step, 4)
                dve.tensor_copy(tot_t[:, :], t_ps[1][0:H, 0, 0:NT]).then_inc(v_step, 1)
                dve.wait_ge(a_step, 8)
                dve.tensor_tensor(lbt[:, LO, :, :], l_ps[0][:, :].rearrange("p (g n) -> p g n", g=TPB),
                                  f32(lbt[:, HI, :, :]), ALU.subtract).then_inc(v_step, 1)

            @block.tensor
            def _(pe):
                pe.wait_ge(consts, 8)

                def turn(i, s):
                    pe.wait_ge(xn_done[s], i + 1)
                    pe.wait_ge(lo_done[s], i)
                    for k in range(KD):
                        for t in range(TPB):
                            mm = pe.transpose(t_ps[s][:, k, t * P:(t + 1) * P],
                                              xn[s][:, t, k * P:(k + 1) * P], ident[:, :])
                    mm.then_inc(t_done[s], 1)

                def unit(b, i, s, more):
                    pe.wait_ge(lo_done[s], i + 1)
                    pe.wait_ge(lt_done[s], i)
                    for n, (xp, wp) in enumerate(PASSES):
                        for k in range(KD):
                            mm = pe.matmul(l_ps[s][0:NL, :], wl[:, wp, k, :], xt[s][:, xp, k, :],
                                           start=(n == 0 and k == 0),
                                           stop=(n == len(PASSES) - 1 and k == KD - 1))
                    mm.then_inc(l_done[s], 1)
                    if more:
                        turn(i + 1, s)
                    pe.wait_ge(lt_done[s], i + 1)
                    pe.wait_ge(l_read[s], i)
                    pe.sem_inc(pe_turn, 1)
                    for t in range(TPB):
                        mm = pe.transpose(m_ps[s][:, t * NL:(t + 1) * NL], lt[s][:, t * P:(t + 1) * P],
                                          ident[0:NL, 0:NL])
                    mm.then_inc(lt_turned[s], 1)

                for s in range(2):
                    turn(0, s)
                pe.wait_ge(w_lo, 1)
                each_batch(pe, unit)
                pe.wait_ge(v_step, 10)
                for c in range(TPB):
                    mm = pe.transpose(m_ps[0][0:B * E, c * P:(c + 1) * P],
                                      aff_c[:, c, :, :].rearrange("p b e -> p (b e)"), ident[:, :])
                mm.then_inc(p_step, 1)
                pe.wait_ge(v_step, 14)
                pe.matmul(m_ps[1][:, :], tri[:, :], lf[:, :, :].rearrange("p t h -> p (t h)"),
                          start=True, stop=True).then_inc(p_step, 1)
                pe.matmul(t_ps[0][:, 0, :], ones[:, :], lf[:, :, :].rearrange("p t h -> p (t h)"),
                          start=True, stop=True).then_inc(p_step, 1)
                for t in range(NT):
                    mm = pe.matmul(t_ps[1][0:H, 0, t:t + 1], lf[:, t, :], ones[:, 0:1],
                                   start=True, stop=True)
                mm.then_inc(p_step, 1)
                pe.wait_ge(v_step, 17)
                pe.wait_ge(a_step, 4)
                for k in range(KD):
                    mm = pe.matmul(m_ps[1][:, k * NT:(k + 1) * NT], head_rows[:, k, :], tot_t[:, :],
                                   start=True, stop=True)
                mm.then_inc(p_step, 1)
                for g in range(TPB):
                    mm = pe.transpose(l_ps[0][:, g * P:(g + 1) * P],
                                      lb[:, g * 8:(g + 1) * 8, :].rearrange("p t h -> p (t h)"),
                                      ident[:, :])
                mm.then_inc(p_step, 1)


def attention(nc, stage, xt_dram, decay_dram, neg_decay_dram, d_out, o_dram, ident, aff_t, top_val, top_idx,
              exp_lb, exp_rest, exp_tot, attn_w, o_stats, fixed):
    stack, sb, ps, sem, pair = stage
    q_sep, pick, lb_cols, block_mask = fixed
    Q, K = 0, 1
    USES = [("qk", 0), ("qk", 1), ("qk", 2), ("v", 0), ("qk", 3), ("v", 1), ("v", 2), ("v", 3)] \
        + [("kt", c) for c in range(TPB)]
    PER_BANK = len(USES) // 2
    CH = TPB // 2
    GB = NG * TPB // 2
    AHEAD = 2
    TOP_STEPS = 4

    with stack:
        xt = sb("xt", [P, 2, KD, N], F32R)
        qk = sb("qk", [P, 2, KD, N])
        qk_r = sb("qk_r", [P, 2, 2, KD, N], F32R)
        v = sb("v", [P, TPB, D])
        kd = sb("kd", [P, TPB, D])
        absd = [sb(f"absd{s}", [P, G4, P]) for s in range(2)]
        decay = [sb(f"decay{s}", [P, G4, P]) for s in range(2)]
        score = [sb(f"score{s}", [P, G4, P]) for s in range(2)]
        state = sb("state", [P, KD, P])
        upd = sb("upd", [P, KD, P])
        o_sb = [sb(f"o_sb{s}", [P, H, HD]) for s in range(2)]
        m8 = sb("m8", [B * E, ROUNDS_PER_BATCH, TOPK_ROUND])
        i8 = sb("i8", [B * E, ROUNDS_PER_BATCH, TOPK_ROUND], U32)
        p_ps = [ps(f"p_ps{s}", [P, 512]) for s in range(2)]
        d_ps = [ps(f"d_ps{s}", [P, G4, P]) for s in range(2)]
        a_ps = [ps(f"a_ps{s}", [P, G4, P]) for s in range(2)]
        o_ps = [ps(f"o_ps{s}", [P, 2, D]) for s in range(2)]
        u_ps = p_ps[0][:, 0:D].rearrange("p (k n) -> p k n", k=KD)

        turn, v_turn, sp_turn = sem("turn"), sem("v_turn"), sem("a_sp_turn")
        xt_in = sem("xt_in")
        lb_in, q_in = pair("lb_in"), sem("q_in")
        p_done, p_read, lo_done = pair("p_done"), pair("p_read"), sem("lo_done")
        d_done, d_read, e_done, e_masked = pair("d_done"), pair("d_read"), pair("e_done"), pair("e_masked")
        a_done, a_read, av_done = pair("a_done"), pair("a_read"), pair("av_done")
        o_scaled, o_read, o_stored = sem("o_scaled"), sem("o_read"), pair("o_stored")
        u_done, u_read, s_done, topk = sem("u_done"), sem("u_read"), sem("s_done"), sem("topk")
        k_hi = sem("k_hi")
        inter_done, stats_done = sem("inter_done"), sem("stats_done")

        def pass_at(kind, m):
            n = USES.index((kind, m))
            return n % 2, n // 2

        with nc.Block() as block:
            @block.sync
            def _(sp):
                with sp.Fori(0, B) as i:
                    sp.wait_ge(p_done[1], i * PER_BANK)
                    sp.sem_inc(sp_turn, 1)
                    sp.dma_start(f32(xt[:, :, :, :]).rearrange("p l k n -> p (l k n)"),
                                 xt_dram[bass.ds(i, 1), :, :].rearrange("a p n -> (a p) n"))\
                      .then_inc(xt_in, 16)
                    sp.wait_ge(d_out, 32)
                    for c in range(TPB):
                        if c == 2:
                            sp.wait_ge(a_done[1], i * GB)
                            sp.sem_inc(sp_turn, 1)
                            sp.wait_ge(lo_done, i * 4 + 2)
                            for h in range(HH):
                                rows = slice(h * HD, (h + 1) * HD)
                                sp.dma_start(f32(q_sep[rows, h, :, :, :]), f32(qk_r[rows, Q, :, :, :]))\
                                  .then_inc(q_in, 16)
                        s = c % 2
                        tile = i * TPB + c
                        before = 2 * (c - 1) if c >= 2 else 0
                        sp.wait_ge(d_done[1], i * GB + before)
                        sp.sem_inc(sp_turn, 1)
                        for part in range(2):
                            sp.dma_start(f32(lb_cols[s][part * H:(part + 1) * H, :]),
                                         neg_decay_dram[part, bass.ds(tile, 1), :]
                                         .rearrange("a (h n) -> (a h) n", h=H)).then_inc(lb_in[s], 16)
                        sp.dma_start(f32(pick[s][2 * H:2 * H + 2, :, :]).rearrange("l h n -> l (h n)"),
                                     decay_dram[:, bass.ds(tile, 1), :]
                                     .rearrange("l a n -> l (a n)")).then_inc(lb_in[s], 16)

            @block.gpsimd
            def _(pool):
                with pool.Fori(0, B) as i:
                    def store(c):
                        pool.wait_ge(o_read, i * TPB + c + 1)
                        pool.sem_inc(turn, 1)
                        pool.dma_start(o_dram[bass.ds(i * TPB + c, 1), :, :].rearrange("a p d -> (a p) d"),
                                       o_sb[c % 2][:, :, :].rearrange("p h d -> p (h d)"))\
                            .then_inc(o_stored[c % 2], 16)

                    for c in range(TPB):
                        for g in range(NG):
                            p, n = g % 2, 2 * c + g // 2
                            pool.wait_ge(e_done[p], i * GB + n + 1)
                            pool.sem_inc(turn, 1)
                            pool.affine_select(out=decay[p][:, :, :], in_=decay[p][:, :, :],
                                               compare_op=ALU.is_ge, fill=0.0, base=0,
                                               pattern=[[0, G4], [1, P]], channel_multiplier=-1)\
                                .then_inc(e_masked[p], 1)
                        if c >= 1:
                            store(c - 1)
                    store(TPB - 1)
                for s in range(2):
                    pool.wait_ge(o_stored[s], 16 * B * CH)

            @block.scalar
            def _(act):
                with act.Fori(0, B) as i:
                    act.wait_ge(lo_done, i * 4)
                    act.wait_ge(q_in, i * HH * 16)
                    for n, (what, m) in enumerate(USES[:4 + TPB]):
                        b, k = n % 2, n // 2
                        act.wait_ge(p_done[b], i * PER_BANK + k + 1)
                        if what == "qk":
                            ins = act.activation(qk[:, m // 2, m % 2, :], p_ps[b][:, :], ACT.Silu)
                            if m // 2 == Q:
                                ins = act.activation(qk_r[:, Q, HI, m % 2, :], p_ps[b][:, :], ACT.Silu)
                            ins.then_inc(p_read[b], 1)
                        else:
                            act.activation(v[:, m, :], p_ps[b][:, 0:D], ACT.Copy).then_inc(p_read[b], 1)
                    for c in range(TPB):
                        for g in range(NG):
                            p, n = g % 2, 2 * c + g // 2
                            act.wait_ge(d_done[p], i * GB + n + 1)
                            act.activation(absd[p][:, :, :], d_ps[p][:, :, :], ACT.Abs)\
                               .then_inc(d_read[p], 1)
                            act.wait_ge(d_read[p], i * GB + n + 1)
                            act.wait_ge(a_read[p], i * GB + n)
                            act.activation(decay[p][:, :, :], absd[p][:, :, :], ACT.Exp, scale=-1.0)\
                               .then_inc(e_done[p], 1)

            @block.vector
            def _(dve):
                def low(i, m):
                    b, k = pass_at("qk", m)
                    dve.wait_ge(p_read[b], i * PER_BANK + k + 1)
                    if m // 2 == K:
                        dve.tensor_copy(qk_r[:, K, HI, m % 2, :], qk[:, K, m % 2, :]).then_inc(k_hi, 1)
                        dve.wait_ge(k_hi, i * KD + m % 2 + 1)
                    dve.tensor_tensor(qk_r[:, m // 2, LO, m % 2, :], qk[:, m // 2, m % 2, :],
                                      f32(qk_r[:, m // 2, HI, m % 2, :]), ALU.subtract)\
                       .then_inc(lo_done, 1)

                def batch(i, more):
                    def top_step(r, step):
                        at = (i * ROUNDS_PER_BATCH + r) * TOPK_ROUND
                        dve.wait_ge(topk, (i * ROUNDS_PER_BATCH + r) * TOP_STEPS + step)
                        dve.sem_inc(v_turn, 1)
                        if step == 0:
                            dve.max(m8[:, r, :], aff_t[:, :]).then_inc(topk, 1)
                        elif step == 1:
                            dve.max_index(i8[:, r, :], m8[:, r, :], aff_t[:, :]).then_inc(topk, 1)
                        else:
                            dve.match_replace(aff_t[:, :], m8[:, r, :], aff_t[:, :], -1.0).then_inc(topk, 1)
                            dve.tensor_copy(top_val[:, bass.ds(at, TOPK_ROUND)], m8[:, r, :])
                            dve.tensor_copy(top_idx[:, bass.ds(at, TOPK_ROUND)], i8[:, r, :])\
                               .then_inc(topk, 1)

                    dve.memset(state[:, :, :], 0.0).then_inc(s_done, 1)
                    for m in range(2, 4):
                        low(i, m)
                    for c in range(TPB):
                        b, k = pass_at("kt", c)
                        dve.wait_ge(p_done[b], i * PER_BANK + k + 1)
                        dve.tensor_tensor(kd[:, c, :].rearrange("p (h d) -> p h d", h=H),
                                          p_ps[b][:, 0:D].rearrange("p (h d) -> p h d", h=H),
                                          spread(exp_rest[:, bass.ds(i * TPB + c, 1), :]
                                                 .rearrange("p a h -> p (a h)"), HD),
                                          ALU.mult).then_inc(p_read[b], 1)

                    def output(c):
                        s = c % 2
                        dve.wait_ge(av_done[1], i * GB + 2 * c + 2)
                        dve.wait_ge(o_stored[s], (i * CH + c // 2) * 16)
                        dve.wait_ge(stats_done, i * TPB + c)
                        dve.tensor_tensor(o_sb[s][:, :, :],
                                          o_ps[s][:, 1, :].rearrange("p (h d) -> p h d", h=H),
                                          spread(exp_lb[:, bass.ds(i * TPB + c, 1), :]
                                                 .rearrange("p a h -> p (a h)"), HD),
                                          ALU.mult).then_inc(o_scaled, 1)
                        dve.wait_ge(o_scaled, i * TPB + c + 1)
                        dve.tensor_tensor(o_sb[s][:, :, :], o_sb[s][:, :, :],
                                          o_ps[s][:, 0, :].rearrange("p (h d) -> p h d", h=H), ALU.add)\
                           .then_inc(o_read, 1)
                        dve.wait_ge(o_read, i * TPB + c + 1)
                        dve.bn_stats(o_stats[:, bass.ds(i * TPB + c, 1), :].rearrange("p a n -> p (a n)"),
                                     o_sb[s][:, :, :].rearrange("p h d -> p (h d)")).then_inc(stats_done, 1)

                    def advance(c):
                        n = i * (TPB - 1) + c
                        dve.wait_ge(u_done, n + 1)
                        dve.tensor_tensor(upd[:, :, :], u_ps[:, :, :],
                                          block_mask[:, :, :].rearrange("p h d -> p (h d)").unsqueeze(1)
                                          .broadcast_to([P, KD, P]), ALU.mult).then_inc(u_read, 1)
                        dve.wait_ge(u_read, n + 1)
                        dve.wait_ge(s_done, i * TPB + c + 1)
                        dve.wait_ge(inter_done, i * TPB + c + 1)
                        for k in range(KD):
                            ins = dve.scalar_tensor_tensor(
                                out=state[:, k, :], in0=state[:, k, :],
                                scalar=exp_tot[:, k, bass.ds(i * TPB + c, 1)], in1=upd[:, k, :],
                                op0=ALU.mult, op1=ALU.add)
                        ins.then_inc(s_done, 1)

                    for t in range(TPB * NG):
                        c, g, p, n = t // NG, t % NG, t % 2, t // 2
                        dve.wait_ge(a_done[p], i * GB + n + 1)
                        dve.wait_ge(e_masked[p], i * GB + n + 1)
                        dve.wait_ge(av_done[p], i * GB + n)
                        dve.tensor_tensor(score[p][:, :, :], a_ps[p][:, :, :], decay[p][:, :, :],
                                          ALU.mult).then_inc(a_read[p], 1)
                        if g == 0 and c >= 1:
                            output(c - 1)
                        elif g == 2 and c < TPB - 1:
                            advance(c)
                        elif p == 1 and n < 3 * ROUNDS_PER_BATCH:
                            top_step(n // 3, n % 3)
                    if more:
                        for m in range(AHEAD):
                            low(i + 1, m)
                    output(TPB - 1)

                for m in range(AHEAD):
                    low(0, m)
                with dve.Fori(0, B - 1) as i:
                    batch(i, True)
                batch(B - 1, False)

            @block.tensor
            def _(pe):

                def project(i, n):
                    what, m = USES[n]
                    b, k = n % 2, n // 2
                    if n == 0:
                        pe.wait_ge(xt_in, i * 16 + 16)
                        pe.wait_ge(u_read, i * (TPB - 1))
                    pe.wait_ge(p_read[b], i * PER_BANK + k)
                    if what == "qk":
                        for j, (wp, xp) in enumerate(PASSES):
                            for kk in range(KD):
                                mm = pe.matmul(p_ps[b][:, :],
                                               attn_w[:, wp, m // 2, kk, (m % 2) * P:(m % 2 + 1) * P],
                                               xt[:, xp, kk, :], start=(j == 0 and kk == 0),
                                               stop=(j == len(PASSES) - 1 and kk == KD - 1))
                    elif what == "v":
                        for j, (xp, wp) in enumerate(PASSES):
                            for kk in range(KD):
                                mm = pe.matmul(p_ps[b][:, 0:D], xt[:, xp, kk, m * P:(m + 1) * P],
                                               attn_w[:, wp, 2, kk, :], start=(j == 0 and kk == 0),
                                               stop=(j == len(PASSES) - 1 and kk == KD - 1))
                    else:
                        for kk in range(KD):
                            mm = pe.transpose(p_ps[b][:, kk * P:(kk + 1) * P],
                                              qk[:, K, kk, m * P:(m + 1) * P], ident[:, :])
                    mm.then_inc(p_done[b], 1)

                def decays(i, t):
                    c, g, p, n = t // NG, t % NG, t % 2, t // 2
                    s = c % 2
                    if g == 0:
                        pe.wait_ge(lb_in[s], (i * CH + c // 2 + 1) * 48)
                    pe.wait_ge(d_read[p], i * GB + n)
                    pe.matmul(d_ps[p][:, :, :], lb_cols[s][:, :], pick[s][:, g * G4:(g + 1) * G4, :],
                              start=True, stop=True).then_inc(d_done[p], 1)

                def scores(i, t):
                    c, g, p, n = t // NG, t % NG, t % 2, t // 2
                    kk, first = g * G4 // HH, g * G4 % HH
                    if t == 0:
                        pe.wait_ge(q_in, (i + 1) * HH * 16)
                        pe.wait_ge(lo_done, i * 4 + 4)
                    pe.wait_ge(a_read[p], i * GB + n)
                    for j, (kp, qp) in enumerate(PASSES):
                        mm = pe.matmul(a_ps[p][:, :, :], qk_r[:, K, kp, kk, c * P:(c + 1) * P],
                                       q_sep[:, first:first + G4, qp, kk, c * P:(c + 1) * P],
                                       start=(j == 0), stop=(j == len(PASSES) - 1))
                    mm.then_inc(a_done[p], 1)

                def values(i, t):
                    c, g, p, n = t // NG, t % NG, t % 2, t // 2
                    pe.wait_ge(a_read[p], i * GB + n + 1)
                    for j in range(G4):
                        h = g * G4 + j
                        mm = pe.matmul(o_ps[c % 2][:, 0, h * HD:(h + 1) * HD], score[p][:, j, :],
                                       v[:, c, h * HD:(h + 1) * HD], start=True, stop=True)
                    mm.then_inc(av_done[p], 1)

                def from_state(i, c):
                    pe.wait_ge(s_done, i * TPB + c + 1)
                    if c >= 1:
                        pe.wait_ge(o_read, i * TPB + c - 1)
                    else:
                        pe.wait_ge(o_read, i * TPB)
                    for kk in range(KD):
                        mm = pe.matmul(o_ps[c % 2][:, 1, kk * P:(kk + 1) * P], qk[:, Q, kk, c * P:(c + 1) * P],
                                       state[:, kk, :], start=True, stop=True)
                    mm.then_inc(inter_done, 1)
                    if c == TPB - 1:
                        return
                    pe.wait_ge(u_read, i * (TPB - 1) + c)
                    for kk in range(KD):
                        mm = pe.matmul(u_ps[:, kk, :], kd[:, c, kk * P:(kk + 1) * P],
                                       v[:, c, kk * P:(kk + 1) * P], start=True, stop=True)
                    mm.then_inc(u_done, 1)

                def groups(i, more):
                    for t in range(TPB * NG):
                        scores(i, t)
                        if t + 2 < TPB * NG:
                            decays(i, t + 2)
                        if t == 1:
                            for n in range(2):
                                b, k = pass_at("kt", TPB - 2 + n)
                                pe.wait_ge(p_read[b], i * PER_BANK + k + 1)
                        if t % NG == 1:
                            from_state(i, t // NG)
                        if more and t >= TPB * NG - AHEAD:
                            project(i + 1, t - (TPB * NG - AHEAD))
                        if t >= 1:
                            values(i, t - 1)
                    values(i, TPB * NG - 1)

                def project_rest(i, first):
                    for n in range(first, len(USES)):
                        if USES[n] == ("kt", 0):
                            decays(i, 0)
                            decays(i, 1)
                        project(i, n)

                project_rest(0, 0)
                with pe.Fori(0, B - 1) as i:
                    groups(i, True)
                    project_rest(i + 1, AHEAD)
                groups(B - 1, False)


def out_proj(nc, stage, o_dram, s_dram, s_stored, ident, wo_r, o_stats, beside):
    stack, sb, ps, sem, pair = stage
    PER = beside["pieces"] // (B // 2 - 1)
    with stack:
        o_in_sb = [sb(f"o_in_sb{s}", [P, TPB, D]) for s in range(2)]
        s_sb = sb("s_sb", [P, NT, D])
        mv = sb("o_mv", [P, NT, 2])
        ms = sb("ms", [P, NT])
        ln_ms = sb("ln_ms", [P, NT])
        r0 = sb("r0", [P, NT])
        r1 = sb("r1", [P, NT])
        ot = [sb(f"ot{s}", [P, 2, KD, N], F32R) for s in range(2)]
        t_ps = [ps(f"ot_ps{s}", [P, KD, N]) for s in range(2)]
        y_ps = ps("s_ps", [P, TPB, D])
        o_in, r_step = pair("po_in"), sem("r_step")
        t_done, hi_done, lo_done = pair("ot_done"), pair("ohi_done"), pair("olo_done")
        y_done, y_read = pair("s_made"), sem("s_read")

        with nc.Block() as block:
            @block.sync
            def _(sp):
                def load_batches(i):
                    for s in range(2):
                        sp.wait_ge(t_done[s], i)
                        sp.dma_start(o_in_sb[s][:, :, :], o_dram[bass.ds((i * 2 + s) * TPB, TPB), :, :]
                                     .rearrange("t p d -> p t d")).then_inc(o_in[s], 16)

                for i in range(2):
                    load_batches(i)
                beside["load"](sp)
                with sp.Fori(2, B // 2) as i:
                    load_batches(i)
                beside["sp"](sp)

            @block.gpsimd
            def _(pool):
                beside["pool"](pool)

            @block.scalar
            def _(act):
                act.wait_ge(r_step, NT + 3)
                act.activation(ln_ms[:, :], ms[:, :], ACT.Ln).then_inc(r_step, 1)
                act.wait_ge(r_step, NT + 4)
                act.activation(r0[:, :], ln_ms[:, :], ACT.Exp, scale=-0.5).then_inc(r_step, 1)

                def turned(i, s):
                    act.wait_ge(t_done[s], i + 1)
                    act.wait_ge(y_done[s], i)
                    act.activation(ot[s][:, HI, :, :], t_ps[s][:, :, :], ACT.Copy)\
                       .then_inc(hi_done[s], 1)

                for s in range(2):
                    turned(0, s)

                def store(b):
                    act.wait_ge(y_read, (b + 2) * 2)
                    act.dma_start(s_dram[bass.ds(b, 1), :, :].rearrange("a p n -> (a p) n"),
                                  s_sb[:, bass.ds(b * TPB, TPB), :].rearrange("p t d -> p (t d)"))\
                       .then_inc(s_stored, 16)

                with act.Fori(1, B // 2) as i:
                    for s in range(2):
                        turned(i, s)
                        store(i * 2 + s - 2)
                        for n in range(PER // 2):
                            beside["piece"](act, (i - 1) * PER + s * (PER // 2) + n)
                beside["act_end"](act)
                for b in range(B - 2, B):
                    store(b)

            @block.vector
            def _(dve):
                beside["dve_start"](dve)
                for t in range(NT):
                    dve.bn_aggr(mv[:, t, :], o_stats[:, t, :]).then_inc(r_step, 1)
                dve.wait_ge(r_step, NT)
                dve.tensor_tensor(ms[:, :], mv[:, :, 0], mv[:, :, 0], ALU.mult).then_inc(r_step, 1)
                dve.wait_ge(r_step, NT + 1)
                dve.tensor_tensor(ms[:, :], ms[:, :], mv[:, :, 1], ALU.add).then_inc(r_step, 1)
                dve.wait_ge(r_step, NT + 2)
                dve.tensor_scalar(ms[:, :], ms[:, :], RMS_EPS, None, ALU.add).then_inc(r_step, 1)
                dve.wait_ge(r_step, NT + 5)
                dve.tensor_tensor(r1[:, :], r0[:, :], r0[:, :], ALU.mult).then_inc(r_step, 1)
                dve.wait_ge(r_step, NT + 6)
                dve.tensor_tensor(r1[:, :], r1[:, :], ms[:, :], ALU.mult).then_inc(r_step, 1)
                dve.wait_ge(r_step, NT + 7)
                dve.tensor_scalar(r1[:, :], r1[:, :], -0.5, 1.5, ALU.mult, ALU.add).then_inc(r_step, 1)
                dve.wait_ge(r_step, NT + 8)
                dve.tensor_tensor(r1[:, :], r1[:, :], r0[:, :], ALU.mult).then_inc(r_step, 1)
                dve.wait_ge(r_step, NT + 9)

                def low(i, s):
                    dve.wait_ge(hi_done[s], i + 1)
                    dve.tensor_tensor(ot[s][:, LO, :, :], t_ps[s][:, :, :], f32(ot[s][:, HI, :, :]),
                                      ALU.subtract).then_inc(lo_done[s], 1)

                def unit(b, i, s, more):
                    if more or s == 0:
                        low(i + s, 1 - s)
                    dve.wait_ge(y_done[s], i + 1)
                    for t in range(TPB):
                        ins = dve.tensor_scalar(
                            s_sb[:, bass.ds(b * TPB + t, 1), :].rearrange("p a d -> p (a d)"), y_ps[:, t, :],
                            r1[:, bass.ds(b * TPB + t, 1)], None, ALU.mult)
                        if t % 2 == 1:
                            ins.then_inc(y_read, 1)
                dve.sem_inc(y_read, 2)
                low(0, 0)
                each_batch(dve, unit)
                beside["dve"](dve)

            @block.tensor
            def _(pe):
                beside["pe_start"](pe)

                def turn(i, s):
                    pe.wait_ge(o_in[s], i * 16 + 16)
                    pe.wait_ge(lo_done[s], i)
                    for k in range(KD):
                        for t in range(TPB):
                            mm = pe.transpose(t_ps[s][:, k, t * P:(t + 1) * P],
                                              o_in_sb[s][:, t, k * P:(k + 1) * P], ident[:, :])
                    mm.then_inc(t_done[s], 1)

                def unit(b, i, s, more):
                    pe.wait_ge(lo_done[s], i + 1)
                    for t in range(TPB):
                        if t % 2 == 0:
                            pe.wait_ge(y_read, b * 2 + t // 2 + 1)
                        for j, (wp, xp) in enumerate(PASSES):
                            for k in range(KD):
                                mm = pe.matmul(y_ps[:, t, :], ot[s][:, wp, k, t * P:(t + 1) * P],
                                               wo_r[:, xp, k, :], start=(j == 0 and k == 0),
                                               stop=(j == len(PASSES) - 1 and k == KD - 1))
                    mm.then_inc(y_done[s], 1)
                    if more:
                        turn(i + 1, s)

                for s in range(2):
                    turn(0, s)
                each_batch(pe, unit)
                beside["pe"](pe)


def experts(nc, stage, makers, x_tiles, xn_dram, o_dram, s_dram, ffn_dram, ffn_tiles, out_tiles,
            w_experts, ident, top_val, top_idx, wo_r, o_stats):
    stack, sb, ps, sem, pair = stage
    SEC = WE // 3
    GATE, UP, DOWN = range(3)
    PIECES = 12
    PW = WE // PIECES
    FIRST = 2 * PIECES // 3
    HALVES = B // TPB
    STEPS = HALVES * MI
    SB2 = STEPS // 2
    FILLS = HALVES * KD
    SPLIT = 3
    TURN = STEPS - FILLS - 1
    COMBINE = STEPS - 4
    with stack:
        w_raw = sb("we_raw", [P, WE])
        w_r = [sb("we_r0", [P, 2, WE], F32R)]
        xg = sb("xg", [P, B, D])
        xgt = [sb("xgt0", [P, 2, KD, B * CAP], F32R)]
        gate_all = sb("gate_all", [P, E, B])
        idx_all = sb("idx_all", [P, E, B], I32)
        batch_base = sb("batch_base", [P, B, E])
        gate_e = [sb(f"gate_e{s}", [P, B]) for s in range(2)]
        idx_e = [sb(f"idx_e{s}", [P, B], I32) for s in range(2)]
        zeros = sb("zeros", [P, 2 * D])
        x_ps = [ps(f"x_ps{s}", [P, 512]) for s in range(2)]

        zero_set, zeroed, base_set = sem("zero_set"), sem("zeroed"), sem("base_set")
        top_t, top_read = sem("top_t"), sem("top_read")
        w_in, w_hi, w_lo = sem("we_in"), sem("we_hi"), sem("we_lo")
        staged, gathered, x_read = sem("staged"), sem("gathered"), pair("x_read")
        x_done, x_hi = pair("x_done"), pair("x_hi")
        gu_done, sg_done, h_done = pair("gu_done"), pair("sg_done"), pair("h_done")
        hh_done, hl_done, dn_done = pair("hh_done"), pair("hl_done"), pair("dn_done")
        y_read, scattered = sem("ye_read"), pair("scattered")
        turn, sp_turn = sem("e_turn"), sem("sp_turn")
        s_stored = sem("s_stored")

        def each_expert(eng, unit):
            with eng.Fori(0, E // 2 - 1) as i:
                for s in range(2):
                    unit(i * 2 + s, i, s, True)
            unit(E - 2, E // 2 - 1, 0, True)
            unit(E - 1, E // 2 - 1, 1, False)

        ZEROED = 16 * (B * N * D // P // (2 * D))

        def load(sp, e):
            sp.wait_ge(w_lo, e * PIECES)
            sp.sem_inc(sp_turn, 1)
            sp.dma_start(w_raw[:, :], w_experts[e, :, :] if isinstance(e, int) else
                         w_experts[bass.ds(e, 1), :, :].rearrange("a p n -> (a p) n")).then_inc(w_in, 16)

        def low(pool, e, s, n):
            at = slice(n * PW, (n + 1) * PW)
            pool.wait_ge(w_hi, e * PIECES + n + 1)
            pool.tensor_tensor(w_r[s][:, LO, at], w_raw[:, at], f32(w_r[s][:, HI, at]),
                               ALU.subtract).then_inc(w_lo, 1)

        def gather(pool, e, i, s):
            pool.wait_ge(scattered[s], i * 128)
            pool.sem_inc(turn, 1)
            pool.tensor_copy(idx_e[s][:, :], pick_expert(idx_all, e)).then_inc(staged, 1)
            pool.tensor_copy(gate_e[s][:, :], pick_expert(gate_all, e)).then_inc(staged, 1)
            pool.wait_ge(staged, e * 2 + 2)
            pool.sem_inc(turn, 1)
            for b in range(2):
                pool.wait_ge(x_read[b], e * (FILLS // 2))
                pool.sem_inc(turn, 1)
            for b in range(B):
                pool.indirect_dma_start(
                    out=xg[:, b, :], out_offset=None, in_=xn_dram[:, :],
                    in_offset=bass.IndirectOffsetOnAxis(ap=idx_e[s][:, b:b + 1], axis=0))\
                    .then_inc(gathered, 16)

        def high(act, e, s, n):
            at = slice(n * PW, (n + 1) * PW) if isinstance(n, int) else bass.ds(n * PW, PW)
            if isinstance(n, int) and n == 0:
                act.wait_ge(w_in, e * 16 + 16)
                act.wait_ge(dn_done[1], (e - 1) * SB2)
            act.activation(w_r[s][:, HI, at], w_raw[:, at], ACT.Copy).then_inc(w_hi, 1)

        def x_high(act, e, s, f):
            b = f % 2
            act.wait_ge(x_done[b], e * (FILLS // 2) + f // 2 + 1)
            act.activation(xgt[s][:, HI, f % KD, (f // KD) * 512:(f // KD + 1) * 512], x_ps[b][:, :],
                           ACT.Copy).then_inc(x_hi[b], 1)

        def x_low(dve, e, s, f):
            b = f % 2
            dst = slice((f // KD) * 512, (f // KD + 1) * 512)
            dve.wait_ge(x_hi[b], e * (FILLS // 2) + f // 2 + 1)
            dve.tensor_tensor(xgt[s][:, LO, f % KD, dst], x_ps[b][:, :],
                              f32(xgt[s][:, HI, f % KD, dst]), ALU.subtract).then_inc(x_read[b], 1)

        def turn_tokens(pe, e, f):
            b = f % 2
            if f == 0:
                pe.wait_ge(gathered, e * 128 + 128)
            pe.wait_ge(x_read[b], e * (FILLS // 2) + f // 2)
            for t in range(TPB):
                mm = pe.transpose(x_ps[b][:, t * P:(t + 1) * P],
                                  xg[:, (f // KD) * TPB + t, (f % KD) * P:(f % KD + 1) * P],
                                  ident[:, :])
            mm.then_inc(x_done[b], 1)

        def first_sp(sp):
            sp.wait_ge(zero_set, 1)
            rows = ffn_dram.rearrange("(p n) d -> p (n d)", p=P)
            for n in range(B * N * D // P // (2 * D)):
                sp.dma_start(rows[:, n * 2 * D:(n + 1) * 2 * D], zeros[:, :]).then_inc(zeroed, 16)

        def first_pool(pool):
            pool.memset(zeros[:, :], 0.0).then_inc(zero_set, 1)
            pool.iota(batch_base[:, :, :], pattern=[[N, B], [0, E]], base=0, channel_multiplier=0,
                      allow_small_or_imprecise_dtypes=True).then_inc(base_set, 1)
            pool.wait_ge(top_read, 2)
            gather(pool, 0, 0, 0)
            for n in range(FIRST):
                low(pool, 0, 0, n)

        def first_piece(act, n):
            act.wait_ge(w_in, 16)
            high(act, 0, 0, n)

        def first_act_end(act):
            for f in range(FILLS):
                x_high(act, 0, 0, f)

        def first_dve_start(dve):
            dve.wait_ge(top_t, 1)
            dve.wait_ge(base_set, 1)
            dve.tensor_copy(gate_all[:, :, :].rearrange("p e b -> p b e"),
                            x_ps[0][:, 0:B * E].rearrange("p (b e) -> p b e", b=B)).then_inc(top_read, 1)
            dve.tensor_tensor(idx_all[:, :, :].rearrange("p e b -> p b e"),
                              x_ps[0][:, B * E:2 * B * E].rearrange("p (b e) -> p b e", b=B),
                              batch_base[:, :, :], ALU.add).then_inc(top_read, 1)

        def first_dve(dve):
            dve.sem_inc(y_read, 2)
            for f in range(FILLS):
                x_low(dve, 0, 0, f)

        def first_pe_start(pe):
            pe.transpose(x_ps[0][:, 0:B * E], top_val[:, :], ident[0:B * E, 0:B * E])
            pe.transpose(x_ps[0][:, B * E:2 * B * E], top_idx[:, :], ident[0:B * E, 0:B * E])\
              .then_inc(top_t, 1)

        def first_pe(pe):
            pe.wait_ge(top_read, 2)
            for f in range(FILLS):
                turn_tokens(pe, 0, f)

        out_proj(nc, stage_of(makers), o_dram, s_dram, s_stored, ident, wo_r, o_stats,
                 dict(load=lambda sp: load(sp, 0), sp=first_sp, pool=first_pool, pieces=PIECES,
                      piece=first_piece, act_end=first_act_end, dve_start=first_dve_start, dve=first_dve, pe_start=first_pe_start, pe=first_pe))

        w_r.append(sb("we_r1", [P, 2, WE], F32R))
        xgt.append(sb("xgt1", [P, 2, KD, B * CAP], F32R))
        sg = [sb(f"sg{s}", [P, 512]) for s in range(2)]
        hid = [sb(f"hid{s}", [P, 512]) for s in range(2)]
        hid_r = [sb(f"hid_r{s}", [P, 2, 512], F32R) for s in range(2)]
        y_sb = [sb(f"y_sb{s}", [P, TPB, D]) for s in range(HALVES)]
        g_ps = [ps(f"g_ps{s}", [P, 512]) for s in range(2)]
        up_ps = [ps(f"up_ps{s}", [P, 512]) for s in range(2)]
        y_ps = ps("ye_ps", [P, TPB, D])
        TD = TPB * D
        last_w = [f32(w_r[s][:, :, :]).rearrange("p l n -> p (l n)") for s in range(2)]
        places = [last_w[0][:, n * TD:(n + 1) * TD] for n in range(2 * WE // TD)] \
            + [last_w[1][:, n * TD:(n + 1) * TD] for n in range(2 * B - 2 * WE // TD)]
        s_at, f_at = places[:B], places[B:]
        xg_flat = xg[:, :, :].rearrange("p b d -> p (b d)")
        x_at = [w_raw[:, b * TD:(b + 1) * TD] for b in range(WE // TD)] \
            + [xg_flat[:, b * TD:(b + 1) * TD] for b in range(B - WE // TD)]
        o_new = [sb(f"o_at{s}", [P, TD])[:, :] for s in range(2)]
        o_y = [y_sb[h][:, :, :].rearrange("p t d -> p (t d)") for h in range(HALVES)]
        o_at = [*o_new, *o_new, *o_y, *o_new]
        last_user = {2: 0, 3: 1, 6: 2, 7: 3}
        EARLY = 3
        x_in, s_in = sem("cx_in"), sem("cs_in")
        last_scattered = pair("last_scattered")
        g_done, m_done, o_done = sem("cg_done"), sem("cm_done"), sem("co_done")
        f_in, o_out = [sem(f"cf_in{b}") for b in range(B)], [sem(f"co_out{b}") for b in range(B)]

        def load_sum(sp, b):
            sp.dma_start(f_at[b].rearrange("p (t d) -> p t d", t=TPB),
                         ffn_tiles[:, b * TPB:(b + 1) * TPB, :]).then_inc(f_in[b], 16)

        def store_out(sp, b):
            sp.wait_ge(o_done, b + 1)
            sp.dma_start(out_tiles[:, b * TPB:(b + 1) * TPB, :], o_at[b].rearrange("p (t d) -> p t d", t=TPB))\
              .then_inc(o_out[b], 16)

        def silu_sum(act, b):
            act.wait_ge(f_in[b], 16)
            if b in last_user:
                act.wait_ge(o_out[last_user[b]], 16)
            act.activation(o_at[b], f_at[b], ACT.Silu).then_inc(g_done, 1)

        def finish(dve, b):
            if b == 0:
                dve.wait_ge(s_in, 16 * B)
                dve.wait_ge(x_in, 16 * B)
            dve.wait_ge(g_done, b + 1)
            dve.tensor_tensor(o_at[b], o_at[b], s_at[b], ALU.mult).then_inc(m_done, 1)
            dve.wait_ge(m_done, b + 1)
            dve.tensor_tensor(o_at[b], o_at[b], x_at[b], ALU.add).then_inc(o_done, 1)

        with nc.Block() as block:
            @block.sync
            def _(sp):
                def unit(e, i, s, more):
                    if more:
                        load(sp, e + 1)
                each_expert(sp, unit)
                sp.wait_ge(dn_done[1], (E - 1) * SB2)
                sp.wait_ge(s_stored, 16 * B)
                for b in range(B):
                    sp.dma_start(s_at[b], s_dram[b, :, :]).then_inc(s_in, 16)
                sp.wait_ge(w_lo, E * PIECES)
                for b in range(2):
                    sp.wait_ge(x_done[b], E * (FILLS // 2))
                for b in range(B):
                    sp.dma_start(x_at[b].rearrange("p (t d) -> p t d", t=TPB),
                                 x_tiles[:, b * TPB:(b + 1) * TPB, :]).then_inc(x_in, 16)
                sp.wait_ge(last_scattered[0], 16 * TPB)
                for b in range(TPB):
                    load_sum(sp, b)
                for b in range(EARLY):
                    store_out(sp, b)

            @block.gpsimd
            def _(pool):
                for n in range(FIRST, PIECES):
                    low(pool, 0, 0, n)
                pool.wait_ge(zeroed, ZEROED)

                def scatter(e, i, s, half):
                    pool.wait_ge(y_read, (e * HALVES + half + 2) * 2)
                    pool.sem_inc(turn, 1)
                    if half == 0:
                        pool.wait_ge(scattered[1 - s], (i + s) * 128)
                        pool.sem_inc(turn, 1)
                    for t in range(TPB):
                        b = half * TPB + t
                        pool.indirect_dma_start(
                            out=ffn_dram[:, :],
                            out_offset=bass.IndirectOffsetOnAxis(ap=idx_e[s][:, b:b + 1], axis=0),
                            in_=y_sb[half][:, t, :], in_offset=None, compute_op=ALU.add)\
                            .then_inc(last_scattered[half] if isinstance(e, int) and e == E - 1
                                      else scattered[s], 16)

                def unit(e, i, s, more):
                    if more:
                        gather(pool, e + 1, i + s, 1 - s)
                        for n in range(PIECES // 2):
                            low(pool, e + 1, 1 - s, n)
                    scatter(e, i, s, 0)
                    if more:
                        for n in range(PIECES // 2, PIECES):
                            low(pool, e + 1, 1 - s, n)
                    scatter(e, i, s, 1)
                each_expert(pool, unit)
                for s in range(2):
                    pool.wait_ge(scattered[s], (E // 2 - s) * 128)
                    pool.wait_ge(last_scattered[s], 16 * TPB)

            @block.scalar
            def _(act):
                act.wait_ge(s_stored, 16 * B)
                def unit(e, i, s, more):
                    for t in range(STEPS):
                        p, n = t % 2, t // 2
                        act.wait_ge(gu_done[p], e * SB2 + n + 1)
                        act.activation(sg[p][:, :], g_ps[p][:, :], ACT.Silu).then_inc(sg_done[p], 1)
                        if more and TURN <= t < TURN + FILLS:
                            x_high(act, e + 1, 1 - s, t - TURN)
                        act.wait_ge(h_done[p], e * SB2 + n + 1)
                        act.wait_ge(dn_done[p], e * SB2 + n)
                        act.activation(hid_r[p][:, HI, :], hid[p][:, :], ACT.Copy).then_inc(hh_done[p], 1)
                        if more and SPLIT <= t < SPLIT + PIECES:
                            high(act, e + 1, 1 - s, t - SPLIT)
                        if not more and 0 <= t - COMBINE < EARLY:
                            silu_sum(act, t - COMBINE)
                each_expert(act, unit)

            @block.vector
            def _(dve):
                def gated(e, i, s, half):
                    dve.wait_ge(dn_done[1], e * SB2 + (half + 1) * MI // 2)
                    dve.wait_ge(scattered[1 - s], (i + s) * 128)
                    dve.wait_ge(staged, e * 2 + 2)
                    for t in range(TPB):
                        b = half * TPB + t
                        ins = dve.tensor_scalar(y_sb[half][:, t, :], y_ps[:, t, :], gate_e[s][:, b:b + 1],
                                                None, ALU.mult)
                        if t % 2 == 1:
                            ins.then_inc(y_read, 1)

                def step(e, s, t, more):
                    p, n = t % 2, t // 2
                    dve.wait_ge(sg_done[p], e * SB2 + n + 1)
                    dve.tensor_tensor(hid[p][:, :], sg[p][:, :], up_ps[p][:, :], ALU.mult)\
                       .then_inc(h_done[p], 1)
                    if more and TURN <= t < TURN + FILLS:
                        x_low(dve, e + 1, 1 - s, t - TURN)
                    dve.wait_ge(hh_done[p], e * SB2 + n + 1)
                    dve.tensor_tensor(hid_r[p][:, LO, :], hid[p][:, :], f32(hid_r[p][:, HI, :]),
                                      ALU.subtract).then_inc(hl_done[p], 1)

                def unit(e, i, s, more):
                    for t in range(1, STEPS):
                        step(e, s, t, more)
                        if t == MI:
                            gated(e, i, s, 0)
                        if not more and 0 <= t - COMBINE < EARLY:
                            finish(dve, t - COMBINE)
                    if more:
                        step(e + 1, 1 - s, 0, False)
                    gated(e, i, s, 1)

                step(0, 0, 0, False)
                each_expert(dve, unit)

            @block.tensor
            def _(pe):
                def gate_up(e, s, t):
                    p, n, half, m = t % 2, t // 2, t // MI, t % MI
                    pe.wait_ge(h_done[p], e * SB2 + n)
                    for sec, bank in ((GATE, g_ps[p]), (UP, up_ps[p])):
                        for j, (a, b) in enumerate(PASSES):
                            for k in range(KD):
                                at = sec * SEC + k * I + m * P
                                mm = pe.matmul(bank[:, :], w_r[s][:, a, at:at + P],
                                               xgt[s][:, b, k, half * 512:(half + 1) * 512],
                                               start=(j == 0 and k == 0),
                                               stop=(j == len(PASSES) - 1 and k == KD - 1))
                    mm.then_inc(gu_done[p], 1)

                def down(e, s, t):
                    p, n, half, m = t % 2, t // 2, t // MI, t % MI
                    pe.wait_ge(hl_done[p], e * SB2 + n + 1)
                    at = DOWN * SEC + m * D
                    for j in range(TPB):
                        if m == 0 and j % 2 == 0:
                            pe.wait_ge(y_read, (e * HALVES + half) * 2 + j // 2 + 1)
                        for q, (a, b) in enumerate(PASSES):
                            mm = pe.matmul(y_ps[:, j, :], hid_r[p][:, a, j * P:(j + 1) * P],
                                           w_r[s][:, b, at:at + D],
                                           start=(m == 0 and q == 0 and j % 2 == 0),
                                           stop=(m == MI - 1 and q == len(PASSES) - 1),
                                           skip_group_check=True)
                    mm.then_inc(dn_done[p], 1)

                def start(e, s):
                    pe.wait_ge(w_lo, e * PIECES + FIRST)
                    for b in range(2):
                        pe.wait_ge(x_read[b], (e + 1) * (FILLS // 2))
                    gate_up(e, s, 0)

                def unit(e, i, s, more):
                    for t in range(1, STEPS):
                        gate_up(e, s, t)
                        if t == 1:
                            pe.wait_ge(w_lo, (e + 1) * PIECES)
                        down(e, s, t - 1)
                        if more and TURN <= t < TURN + FILLS:
                            turn_tokens(pe, e + 1, t - TURN)
                    if more:
                        start(e + 1, 1 - s)
                    down(e, s, STEPS - 1)

                start(0, 0)
                each_expert(pe, unit)

        with nc.Block() as block:
            @block.sync
            def _(sp):
                for b in range(TPB, B):
                    load_sum(sp, b)
                for b in range(EARLY, B):
                    store_out(sp, b)
                for b in range(B):
                    sp.wait_ge(o_out[b], 16)

            @block.scalar
            def _(act):
                for b in range(EARLY, B):
                    silu_sum(act, b)

            @block.vector
            def _(dve):
                for b in range(EARLY, B):
                    finish(dve, b)


def pick_expert(table, e):
    if isinstance(e, int):
        return table[:, e, :]
    return table[:, bass.ds(e, 1), :].rearrange("p a b -> p (a b)")


def kernel(L0_attn_x, L0_attn_Wq, L0_attn_Wk, L0_attn_Wv, L0_attn_Wo, L0_attn_Wf, L0_attn_delta,
           L0_attn_norm_weight, L0_ffn_gate_w, L0_ffn_w_gate, L0_ffn_w_up, L0_ffn_w_down):
    import concourse.bacc as bacc
    from concourse.bass_utils import run_bass_kernel_spmd

    def rows_in_halves(w):
        w = np.asarray(w).T
        return w.reshape(-1, P, w.shape[1]).transpose(1, 0, 2)

    w_attn = np.stack([rows_in_halves(w) for w in (L0_attn_Wq, L0_attn_Wk, L0_attn_Wv, L0_attn_Wo)], 1)
    w_logit = rows_in_halves(np.concatenate([np.asarray(L0_ffn_gate_w), np.asarray(L0_attn_Wf)], 0))
    w_experts = np.stack([
        np.concatenate([rows_in_halves(w[e]).reshape(P, -1)
                        for w in (L0_ffn_w_gate, L0_ffn_w_up, L0_ffn_w_down)], 1) for e in range(E)], 0)
    arrays = {
        "x": np.asarray(L0_attn_x).reshape(B * N, D),
        "w_attn": w_attn,
        "w_logit": w_logit,
        "delta": np.asarray(L0_attn_delta),
        "norm_w": np.asarray(L0_attn_norm_weight).reshape(KD, P).T,
        "w_experts": w_experts,
    }
    arrays = {n: np.ascontiguousarray(a) for n, a in arrays.items()}
    nc = bacc.Bacc("TRN2", target_bir_lowering=False, num_devices=1)
    aps = {n: nc.dram_tensor(n, a.shape, mybir.dt.from_np(a.dtype), kind="ExternalInput").ap()
           for n, a in arrays.items()}
    out = nc.dram_tensor("out", (B * N, D), F32, kind="ExternalOutput").ap()
    build(nc, out=out, **aps)
    result = run_bass_kernel_spmd(nc, [arrays], core_ids=[0])
    return result.results[0]["out"].reshape(B, N, D)
```
